# Optimizing a Trainium2 kernel written in Bass

```python
import numpy as np
import jax
import jax.numpy as jnp

def _softmax(x, axis=-1):
    return jax.nn.softmax(x, axis=axis)

def _gelu(x):
    return jax.nn.gelu(x, approximate=True)

def _silu(x):
    return jax.nn.silu(x)

def _sigmoid(x):
    return jax.nn.sigmoid(x)

def _layernorm(x, axis=-1, eps=1e-05):
    m = jnp.mean(x, axis=axis, keepdims=True)
    v = jnp.var(x, axis=axis, keepdims=True)
    return (x - m) / jnp.sqrt(v + eps)

def _scatter_add(tgt, idx, src, axis=0):
    return tgt.at[idx].add(src)

def _segment_sum(src, seg, n):
    return jax.ops.segment_sum(src, seg, n)
kernel_name = 'mk_decoder_preln_d2_seqx_r8_cee527'

def setup_inputs(seed: int=0):
    np.random.seed(seed)
    _w = jnp.asarray

    def _rec_inputs():
        import jax
        import jax.numpy as jnp
        _rk = jax.random.key(seed)
        x = -0.0005207 + 1.001 * jax.random.normal(jax.random.fold_in(_rk, 1), (64, 64, 128), jnp.float32)
        _lenS = 64 - jax.random.randint(jax.random.fold_in(_rk, 7), (64,), 0, max(1, 64 // 4) + 1, jnp.int32)
        _lenS2 = 64 - jax.random.randint(jax.random.fold_in(_rk, 8), (64,), 0, max(1, 64 // 4) + 1, jnp.int32)
        _ctx_1024P = jax.random.normal(jax.random.fold_in(_rk, 11), (64, 16, 128), jnp.float32)
        _ctx_1024c = jax.random.dirichlet(jax.random.fold_in(_rk, 511), 0.3 * jnp.ones((16,), jnp.float32), (64, 64))
        _ctx_1024t = jnp.einsum('bsk,bkd->bsd', _ctx_1024c, _ctx_1024P)
        _ctx_1024t = _ctx_1024t * jax.lax.rsqrt(jnp.mean(jnp.square(_ctx_1024t)) + 1e-12) * 0.953939
        ctx_1024 = -1.39393e-06 + 0.999914 * (_ctx_1024t + 0.3 * jax.random.normal(jax.random.fold_in(_rk, 611), (64, 64, 128), jnp.float32))
        _validS = jnp.arange(64)[None, :] < _lenS[:, None]
        _validS2 = jnp.arange(64)[None, :] < _lenS2[:, None]
        _causal = jnp.tril(jnp.ones((64, 64), dtype=bool))
        mask_BxS2_ik1 = jnp.where(jnp.broadcast_to(_validS2[:, :], (64, 64)), 1, 0).astype(jnp.int32)
        return (x, ctx_1024, mask_BxS2_ik1)
    x, ctx_1024, mask_BxS2_ik1 = _rec_inputs()

    def _L0_attn_setup():
        import jax, jax.numpy as jnp
        import numpy as np
        EMBED_DIM = 128
        NUM_HEADS = 16
        HEAD_DIM = EMBED_DIM // NUM_HEADS
        key = jax.random.key(seed)
        k1, k2, k3 = jax.random.split(key, 3)
        x = jax.random.normal(k1, (4, 256, EMBED_DIM), dtype=jnp.float32)
        W_qkv = jax.random.normal(k2, (3 * EMBED_DIM, EMBED_DIM), dtype=jnp.float32) * EMBED_DIM ** (-0.5)
        W_proj = jax.random.normal(k3, (EMBED_DIM, EMBED_DIM), dtype=jnp.float32) * EMBED_DIM ** (-0.5)
        return {'x': x, 'W_qkv': W_qkv, 'W_proj': W_proj}
    _L0_attn_all = _L0_attn_setup()
    _L0_attn_in = {k: v for k, v in _L0_attn_all.items() if k in ('W_qkv', 'W_proj')}
    del _L0_attn_all

    def _L0_xattn_setup():
        import jax, jax.numpy as jnp
        import numpy as np
        EMBED_DIM = 128
        NUM_HEADS = 16
        HEAD_DIM = EMBED_DIM // NUM_HEADS
        SCALE = HEAD_DIM ** (-0.5)
        key = jax.random.key(seed)
        ks = jax.random.split(key, 8)
        B, Nq, Nkv, C = (2, 128, 256, EMBED_DIM)
        xavier = (6.0 / (C + C)) ** 0.5

        def w(k):
            return jax.random.uniform(k, (C, C), jnp.float32, -xavier, xavier)
        return {'query': jax.random.normal(ks[0], (B, Nq, C), jnp.float32), 'key': jax.random.normal(ks[1], (B, Nkv, C), jnp.float32), 'value': jax.random.normal(ks[2], (B, Nkv, C), jnp.float32), 'Wq': w(ks[3]), 'bq': jnp.zeros((C,), jnp.float32), 'Wk': w(ks[4]), 'bk': jnp.zeros((C,), jnp.float32), 'Wv': w(ks[5]), 'bv': jnp.zeros((C,), jnp.float32), 'Wo': w(ks[6]), 'bo': jnp.zeros((C,), jnp.float32), 'temperature': jnp.ones((NUM_HEADS, 1, 1), jnp.float32)}
    _L0_xattn_all = _L0_xattn_setup()
    _L0_xattn_in = {k: v for k, v in _L0_xattn_all.items() if k in ('Wq', 'bq', 'Wk', 'bk', 'Wv', 'bv', 'Wo', 'bo', 'temperature')}
    del _L0_xattn_all

    def _L0_ffn_setup():
        import jax, jax.numpy as jnp
        import numpy as np
        TOP_K = 2
        NUM_EXPERTS = 8
        B, T, H, F = (4, 256, 128, 512)
        key = jax.random.key(seed)
        ks = jax.random.split(key, 6)
        s_in = 1.0 / np.sqrt(H)
        s_ff = 1.0 / np.sqrt(F)
        return {'x': jax.random.normal(ks[0], (B, T, H), dtype=jnp.float32), 'router_w': jax.random.normal(ks[1], (NUM_EXPERTS, H), dtype=jnp.float32) * s_in, 'router_b': jax.random.normal(ks[2], (NUM_EXPERTS,), dtype=jnp.float32) * 0.01, 'gate_w': jax.random.normal(ks[3], (NUM_EXPERTS, F, H), dtype=jnp.float32) * s_in, 'up_w': jax.random.normal(ks[4], (NUM_EXPERTS, F, H), dtype=jnp.float32) * s_in, 'down_w': jax.random.normal(ks[5], (NUM_EXPERTS, H, F), dtype=jnp.float32) * s_ff}
    _L0_ffn_all = _L0_ffn_setup()
    _L0_ffn_in = {k: v for k, v in _L0_ffn_all.items() if k in ('router_w', 'router_b', 'gate_w', 'up_w', 'down_w')}
    del _L0_ffn_all

    def _L1_attn_setup():
        import jax, jax.numpy as jnp
        import numpy as np
        HEADS = 16
        DIM_HEAD = 64
        B, T, C = (4, 256, 128)

        def apply_rope(x):
            d = x.shape[-1]
            seq_len = x.shape[1]
            inv_freq = 1.0 / 10000.0 ** (jnp.arange(0, d, 2, dtype=jnp.float32) / d)
            pos = jnp.arange(seq_len, dtype=jnp.float32)
            ang = pos[:, None] * inv_freq[None, :]
            sin = jnp.sin(ang)[None]
            cos = jnp.cos(ang)[None]
            x1, x2 = (x[..., 0::2], x[..., 1::2])
            rot = jnp.stack([x1 * cos - x2 * sin, x1 * sin + x2 * cos], axis=-1)
            return rot.reshape(x.shape)
        key = jax.random.key(seed)
        ks = jax.random.split(key, 6)
        inner = HEADS * DIM_HEAD
        w = 0.02
        return {'x': jax.random.normal(ks[0], (B, T, C), dtype=jnp.float32), 'Wq': jax.random.normal(ks[1], (C, inner), dtype=jnp.float32) * w, 'Wk': jax.random.normal(ks[2], (C, inner), dtype=jnp.float32) * w, 'Wv': jax.random.normal(ks[3], (C, inner), dtype=jnp.float32) * w, 'Wo': jax.random.normal(ks[4], (inner, C), dtype=jnp.float32) * w, 'bo': jnp.zeros((C,), dtype=jnp.float32)}
    _L1_attn_all = _L1_attn_setup()
    _L1_attn_in = {k: v for k, v in _L1_attn_all.items() if k in ('Wq', 'Wk', 'Wv', 'Wo', 'bo')}
    del _L1_attn_all

    def _L1_xattn_setup():
        import jax, jax.numpy as jnp
        import numpy as np
        import math
        B, T, EMB = (4, 256, 128)
        PAD_TAIL = 32
        key = jax.random.key(seed)
        kq, kk, kv = jax.random.split(key, 3)
        query = jax.random.normal(kq, (B, T, EMB), dtype=jnp.float32)
        k = jax.random.normal(kk, (B, T, EMB), dtype=jnp.float32)
        value = jax.random.normal(kv, (B, T, EMB), dtype=jnp.float32)
        attention_mask = jnp.concatenate([jnp.ones((B, T - PAD_TAIL), dtype=jnp.int32), jnp.zeros((B, PAD_TAIL), dtype=jnp.int32)], axis=1)
        return {'query': query, 'key': k, 'value': value, 'attention_mask': attention_mask}
    _L1_xattn_all = _L1_xattn_setup()
    _L1_xattn_in = {k: v for k, v in _L1_xattn_all.items() if k in ()}
    del _L1_xattn_all

    def _L1_ffn_setup():
        import jax, jax.numpy as jnp
        import numpy as np
        QMAX = 127.0

        def _ste_round(v):
            return v + jax.lax.stop_gradient(jnp.round(v) - v)

        def _act_fake_quant(x, clip_factor):
            scale = jax.nn.sigmoid(clip_factor) * jnp.max(jnp.abs(x)) / QMAX
            return jnp.clip(_ste_round(x / scale), -QMAX - 1.0, QMAX) * scale

        def _weight_fake_quant(w):
            scale = jnp.max(jnp.abs(w), axis=1, keepdims=True) / QMAX
            return jnp.clip(_ste_round(w / scale), -QMAX - 1.0, QMAX) * scale
        key = jax.random.key(seed)
        k1, k2, k3, k4 = jax.random.split(key, 4)
        B, S, H, I = (8, 1024, 128, 352)
        return {'x': jax.random.normal(k1, (B, S, H), dtype=jnp.float32), 'clip_x': jnp.full((1,), 4.0, dtype=jnp.float32), 'clip_down': jnp.full((1,), 4.0, dtype=jnp.float32), 'w_gate': jax.random.normal(k2, (I, H), dtype=jnp.float32) * 0.02, 'w_up': jax.random.normal(k3, (I, H), dtype=jnp.float32) * 0.02, 'w_down': jax.random.normal(k4, (H, I), dtype=jnp.float32) * 0.02}
    _L1_ffn_all = _L1_ffn_setup()
    _L1_ffn_in = {k: v for k, v in _L1_ffn_all.items() if k in ('clip_x', 'clip_down', 'w_gate', 'w_up', 'w_down')}
    del _L1_ffn_all
    return {'x': x, 'ctx_1024': ctx_1024, 'mask_BxS2_ik1': mask_BxS2_ik1, 'L0_attn_W_qkv': _L0_attn_in['W_qkv'], 'L0_attn_W_proj': _L0_attn_in['W_proj'], 'L0_xattn_Wq': _L0_xattn_in['Wq'], 'L0_xattn_bq': _L0_xattn_in['bq'], 'L0_xattn_Wk': _L0_xattn_in['Wk'], 'L0_xattn_bk': _L0_xattn_in['bk'], 'L0_xattn_Wv': _L0_xattn_in['Wv'], 'L0_xattn_bv': _L0_xattn_in['bv'], 'L0_xattn_Wo': _L0_xattn_in['Wo'], 'L0_xattn_bo': _L0_xattn_in['bo'], 'L0_xattn_temperature': _L0_xattn_in['temperature'], 'L0_ffn_router_w': _L0_ffn_in['router_w'], 'L0_ffn_router_b': _L0_ffn_in['router_b'], 'L0_ffn_gate_w': _L0_ffn_in['gate_w'], 'L0_ffn_up_w': _L0_ffn_in['up_w'], 'L0_ffn_down_w': _L0_ffn_in['down_w'], 'L1_attn_Wq': _L1_attn_in['Wq'], 'L1_attn_Wk': _L1_attn_in['Wk'], 'L1_attn_Wv': _L1_attn_in['Wv'], 'L1_attn_Wo': _L1_attn_in['Wo'], 'L1_attn_bo': _L1_attn_in['bo'], 'L1_ffn_clip_x': _L1_ffn_in['clip_x'], 'L1_ffn_clip_down': _L1_ffn_in['clip_down'], 'L1_ffn_w_gate': _L1_ffn_in['w_gate'], 'L1_ffn_w_up': _L1_ffn_in['w_up'], 'L1_ffn_w_down': _L1_ffn_in['w_down']}

def reference(x, ctx_1024, mask_BxS2_ik1, L0_attn_W_qkv, L0_attn_W_proj, L0_xattn_Wq, L0_xattn_bq, L0_xattn_Wk, L0_xattn_bk, L0_xattn_Wv, L0_xattn_bv, L0_xattn_Wo, L0_xattn_bo, L0_xattn_temperature, L0_ffn_router_w, L0_ffn_router_b, L0_ffn_gate_w, L0_ffn_up_w, L0_ffn_down_w, L1_attn_Wq, L1_attn_Wk, L1_attn_Wv, L1_attn_Wo, L1_attn_bo, L1_ffn_clip_x, L1_ffn_clip_down, L1_ffn_w_gate, L1_ffn_w_up, L1_ffn_w_down):
    import jax
    import jax.numpy as jnp

    def _L0_attn_ref(x, W_qkv, W_proj):
        import jax, jax.numpy as jnp
        import numpy as np
        EMBED_DIM = 128
        NUM_HEADS = 16
        HEAD_DIM = EMBED_DIM // NUM_HEADS
        B, T, C = x.shape
        H, D = (NUM_HEADS, HEAD_DIM)
        qkv = x @ W_qkv.T
        q, k, v = jnp.split(qkv, 3, axis=-1)
        q = q.reshape(B, T, H, D).transpose(0, 2, 1, 3)
        k = k.reshape(B, T, H, D).transpose(0, 2, 1, 3)
        v = v.reshape(B, T, H, D).transpose(0, 2, 1, 3)
        scores = jnp.einsum('bhqd,bhkd->bhqk', q, k) / jnp.sqrt(jnp.asarray(D, x.dtype))
        causal = jnp.tril(jnp.ones((T, T), dtype=bool))
        scores = jnp.where(causal, scores, -jnp.inf)
        weights = jax.nn.softmax(scores, axis=-1)
        out = jnp.einsum('bhqk,bhkd->bhqd', weights, v)
        out = out.transpose(0, 2, 1, 3).reshape(B, T, C)
        return out @ W_proj.T

    def _L0_xattn_ref(query, key, value, Wq, bq, Wk, bk, Wv, bv, Wo, bo, temperature):
        import jax, jax.numpy as jnp
        import numpy as np
        EMBED_DIM = 128
        NUM_HEADS = 16
        HEAD_DIM = EMBED_DIM // NUM_HEADS
        SCALE = HEAD_DIM ** (-0.5)
        B, Nq, C = query.shape
        Nkv = key.shape[1]
        H, D = (NUM_HEADS, HEAD_DIM)
        Q = (query @ Wq.T + bq).reshape(B, Nq, H, D).transpose(0, 2, 1, 3)
        K = (key @ Wk.T + bk).reshape(B, Nkv, H, D).transpose(0, 2, 1, 3)
        V = (value @ Wv.T + bv).reshape(B, Nkv, H, D).transpose(0, 2, 1, 3)
        scores = jnp.einsum('bhqd,bhkd->bhqk', Q, K) * SCALE
        scores = scores / temperature
        attn = jax.nn.softmax(scores, axis=-1)
        out = jnp.einsum('bhqk,bhkd->bhqd', attn, V)
        out = out.transpose(0, 2, 1, 3).reshape(B, Nq, C)
        return out @ Wo.T + bo

    def _L0_ffn_ref(x, router_w, router_b, gate_w, up_w, down_w):
        import jax, jax.numpy as jnp
        import numpy as np
        TOP_K = 2
        NUM_EXPERTS = 8
        B, T, H, F = (4, 256, 128, 512)
        logits = jnp.einsum('bth,eh->bte', x, router_w) + router_b
        topv, topi = jax.lax.top_k(logits, TOP_K)
        gates = jax.nn.softmax(topv, axis=-1)

        def body(acc, inputs):
            e, gw, uw, dw = inputs
            w = jnp.sum(gates * (topi == e), axis=-1)
            h = jax.nn.silu(jnp.einsum('bth,fh->btf', x, gw)) * jnp.einsum('bth,fh->btf', x, uw)
            y = jnp.einsum('btf,hf->bth', h, dw)
            return (acc + y * w[..., None], None)
        init = jnp.zeros_like(x)
        xs = (jnp.arange(NUM_EXPERTS), gate_w, up_w, down_w)
        out, _ = jax.lax.scan(body, init, xs)
        return out

    def _L1_attn_ref(x, Wq, Wk, Wv, Wo, bo):
        import jax, jax.numpy as jnp
        import numpy as np
        HEADS = 16
        DIM_HEAD = 64
        B, T, C = (4, 256, 128)

        def apply_rope(x):
            d = x.shape[-1]
            seq_len = x.shape[1]
            inv_freq = 1.0 / 10000.0 ** (jnp.arange(0, d, 2, dtype=jnp.float32) / d)
            pos = jnp.arange(seq_len, dtype=jnp.float32)
            ang = pos[:, None] * inv_freq[None, :]
            sin = jnp.sin(ang)[None]
            cos = jnp.cos(ang)[None]
            x1, x2 = (x[..., 0::2], x[..., 1::2])
            rot = jnp.stack([x1 * cos - x2 * sin, x1 * sin + x2 * cos], axis=-1)
            return rot.reshape(x.shape)
        b, t, c = x.shape
        h, d = (HEADS, DIM_HEAD)
        scale = d ** (-0.5)

        def split_heads(z):
            return z.reshape(b, t, h, d).transpose(0, 2, 1, 3).reshape(b * h, t, d)
        q = split_heads(x @ Wq)
        k = split_heads(x @ Wk)
        v = split_heads(x @ Wv)
        q = apply_rope(q)
        k = apply_rope(k)
        sim = jnp.einsum('bid,bjd->bij', q, k) * scale
        causal = jnp.tril(jnp.ones((t, t), dtype=bool))
        sim = jnp.where(causal[None], sim, -jnp.inf)
        attn = jax.nn.softmax(sim, axis=-1)
        out = jnp.einsum('bij,bjd->bid', attn, v)
        out = out.reshape(b, h, t, d).transpose(0, 2, 1, 3).reshape(b, t, h * d)
        return out @ Wo + bo

    def _L1_xattn_ref(query, key, value, attention_mask):
        import jax, jax.numpy as jnp
        import numpy as np
        import math
        B, T, EMB = (4, 256, 128)
        PAD_TAIL = 32
        Bq, Tq, emb = query.shape
        Tk = key.shape[1]
        scale = 1.0 / math.sqrt(emb)
        scores = jnp.einsum('bqd,bkd->bqk', query, key) * scale
        neg_inf = jnp.float32(-jnp.inf)
        if Tq == Tk:
            causal = jnp.triu(jnp.ones((Tq, Tk), dtype=bool), k=1)
            scores = jnp.where(causal[None, :, :], neg_inf, scores)
        key_pad = (attention_mask == 0)[:, None, :]
        scores = jnp.where(key_pad, neg_inf, scores)
        attn = jax.nn.softmax(scores, axis=-1)
        out = jnp.einsum('bqk,bkd->bqd', attn, value)
        return out

    def _L1_ffn_ref(x, clip_x, clip_down, w_gate, w_up, w_down):
        import jax, jax.numpy as jnp
        import numpy as np
        QMAX = 127.0

        def _ste_round(v):
            return v + jax.lax.stop_gradient(jnp.round(v) - v)

        def _act_fake_quant(x, clip_factor):
            scale = jax.nn.sigmoid(clip_factor) * jnp.max(jnp.abs(x)) / QMAX
            return jnp.clip(_ste_round(x / scale), -QMAX - 1.0, QMAX) * scale

        def _weight_fake_quant(w):
            scale = jnp.max(jnp.abs(w), axis=1, keepdims=True) / QMAX
            return jnp.clip(_ste_round(w / scale), -QMAX - 1.0, QMAX) * scale
        xq = _act_fake_quant(x, clip_x[0])
        gate = jnp.einsum('bsh,ih->bsi', xq, _weight_fake_quant(w_gate))
        up = jnp.einsum('bsh,ih->bsi', xq, _weight_fake_quant(w_up))
        h = _act_fake_quant(jax.nn.silu(gate) * up, clip_down[0])
        return jnp.einsum('bsi,hi->bsh', h, _weight_fake_quant(w_down))
    x = x + _L0_attn_ref(_layernorm(x, axis=-1), L0_attn_W_qkv, L0_attn_W_proj)
    x = x + _L0_xattn_ref(_layernorm(x, axis=-1), ctx_1024, ctx_1024, L0_xattn_Wq, L0_xattn_bq, L0_xattn_Wk, L0_xattn_bk, L0_xattn_Wv, L0_xattn_bv, L0_xattn_Wo, L0_xattn_bo, L0_xattn_temperature)
    x = x + _L0_ffn_ref(_layernorm(x, axis=-1), L0_ffn_router_w, L0_ffn_router_b, L0_ffn_gate_w, L0_ffn_up_w, L0_ffn_down_w)
    x = x + _L1_attn_ref(_layernorm(x, axis=-1), L1_attn_Wq, L1_attn_Wk, L1_attn_Wv, L1_attn_Wo, L1_attn_bo)
    x = x + _L1_xattn_ref(_layernorm(x, axis=-1), ctx_1024, ctx_1024, mask_BxS2_ik1)
    x = x + _L1_ffn_ref(_layernorm(x, axis=-1), L1_ffn_clip_x, L1_ffn_clip_down, L1_ffn_w_gate, L1_ffn_w_up, L1_ffn_w_down)
    return x

_drawn_inputs = setup_inputs


def setup_inputs(seed=0):
    import zlib

    import numpy as np

    out = dict(_drawn_inputs(seed))
    spreads = {'L0_xattn_bq': (0.0, 0.1),
     'L0_xattn_bk': (0.0, 0.8),
     'L0_xattn_bv': (0.0, 0.1),
     'L0_xattn_bo': (0.0, 0.1),
     'L0_xattn_temperature': (1.0, 0.2),
     'L1_attn_bo': (0.0, 0.1)}
    factors = {'L1_attn_Wq': 8.0,
     'L1_attn_Wk': 8.0,
     'L1_ffn_w_gate': 8.0,
     'L1_ffn_w_up': 8.0,
     'L1_ffn_w_down': 8.0}
    for name, (base, spread) in spreads.items():
        noise = np.random.default_rng([zlib.crc32(name.encode()), seed]).standard_normal(out[name].shape)
        drawn = base * np.exp(spread * noise) if base else spread * noise
        out[name] = jnp.asarray(drawn.astype(out[name].dtype))
    for name, factor in factors.items():
        out[name] = (out[name] * factor).astype(out[name].dtype)
    return out
```

```python
from contextlib import ExitStack

import numpy as np

import concourse.bass as bass
from concourse import mybir

P = 128
B, T, C = 64, 64, 128
NU = B * T // P
H = 16
D0 = C // H
EPS = 1e-5
NEG = -1e30

F32 = mybir.dt.float32
BF16 = mybir.dt.bfloat16
I32 = mybir.dt.int32
ALU = mybir.AluOpType
ACT = mybir.ActivationFunctionType
AX = mybir.AxisListType


class Core:
    pass


def run_blocks(eng, n_blocks, prologue, step, epilogue):
    prologue()
    step(0, 0, prev=False, nxt=True)
    with eng.Fori(0, n_blocks // 2 - 1) as i:
        step(i * 2 + 1, 1, prev=True, nxt=True)
        step(i * 2 + 2, 0, prev=True, nxt=True)
    step(n_blocks - 1, (n_blocks - 1) % 2, prev=True, nxt=False)
    epilogue()


def wait_here(eng, sem, value, passed):
    eng.wait_ge(sem, value)
    eng.sem_inc(passed, 1)


def run_phase(nc, phase, *args, **named):
    with nc.cleanup_on_exit():
        phase(nc, *args, **named)


def load_phase(nc, k, zeros):
    with ExitStack() as ctx:
        loaded = nc.alloc_semaphore("shared_loaded")
        staged_in = nc.alloc_semaphore("staged_in")
        zeros_made = nc.alloc_semaphore("zeros_made")
        narrowed = [(dst, ctx.enter_context(nc.sbuf_tensor(f"staged_{name}", list(dst.shape), F32)), name)
                    for dst, name in ((k.causal_keys, "c_causal_keys"), (k.causal_queries, "c_causal_queries"),
                                      (k.identb, "c_ident"), (k.of_batch, "c_of_batch"))]
        block = ctx.enter_context(nc.Block())

        @block.sync
        def _(sp):
            sp.dma_start(k.X[:], k.d["x"].rearrange("(u r) t d -> (r t) u d", r=2)).then_inc(loaded, 16)
            sp.dma_start(k.ident[:], k.d["c_ident"]).then_inc(loaded, 16)
            sp.dma_start(k.ones_row[:], k.d["c_ones_row"]).then_inc(loaded, 16)
            for _, staged, name in narrowed:
                sp.dma_start(staged[:], k.d[name]).then_inc(staged_in, 16)
            sp.wait_ge(zeros_made, 1)
            filled = k.slot_rows.rearrange("(n p r) c -> n p (r c)", p=P, r=4)
            for i in range(k.n_zeroed):
                sp.dma_start(filled[i], zeros[:]).then_inc(k.zeroed, 16)
            sp.wait_ge(loaded, 3 * 16)

        @block.vector
        def _(dve):
            dve.wait_ge(staged_in, 16 * len(narrowed))
            for dst, staged, _ in narrowed:
                nc.vector.tensor_copy(dst[:], staged[:])

        @block.gpsimd
        def _(pool):
            nc.gpsimd.memset(zeros[:], 0.0).then_inc(zeros_made, 1)


def narrow_attention_phase(nc, k, cross):
    UB = 4
    NB = NU // UB
    BB = 2 * UB
    TOK = UB * P
    PAIRS = H // 2
    LAG = 3
    VW = 2 * 2 * D0 + 2
    n = "x0" if cross else "a0"
    d = k.d
    with ExitStack() as ctx:
        def sb(name, shape, dt=F32):
            return ctx.enter_context(nc.sbuf_tensor(f"{n}_{name}", shape, dt))

        def sem(name):
            return nc.alloc_semaphore(f"{n}_{name}")

        wq = sb("wq", [P, C])
        wk = sb("wk", [P, C])
        wv = sb("wv", [P, C])
        wo = sb("wo", [64, 2, C])
        bq = sb("bq", [P, 1])
        bk = sb("bk", [P, 1])
        bv = sb("bv", [1, C])
        bo = sb("bo", [1, C])
        temp = sb("temp", [P, 1])
        qscale = sb("qscale", [P, 1])
        ctxT = sb("ctxT", [P, 2, TOK])
        stats = sb("stats", [P, UB, 6])
        mv = sb("mv", [P, UB, 2])
        var_eps = sb("var_eps", [P, UB])
        minus_half = sb("minus_half", [P, UB])
        rstd = sb("rstd", [P, UB])
        xn = sb("xn", [P, UB, C])
        xnT = sb("xnT", [P, TOK])
        QT = sb("QT", [P, TOK])
        QX = sb("QX", [P, 2, BB, H * T])
        KT = sb("KT", [P, 2, TOK])
        V = sb("V", [P, 2, BB, PAIRS // 2, VW])
        row_max = sb("row_max", [P, 2, PAIRS])
        E = sb("E", [P, 4, PAIRS * T])
        ET = sb("ET", [P, 2, PAIRS * T])
        rden = sb("rden", [P, 2, PAIRS])
        O = sb("O", [P, BB, 64])
        OT = sb("OT", [64, 2, TOK])
        S_ps = [ctx.enter_context(nc.psum_tensor(f"{n}_S{i}", [P, 512], F32)) for i in range(2)]
        ET_ps = [ctx.enter_context(nc.psum_tensor(f"{n}_ET{i}", [P, 512], F32)) for i in range(2)]
        PV_ps = [ctx.enter_context(nc.psum_tensor(f"{n}_PV{i}", [P, 512], F32)) for i in range(2)]
        G_ps = [ctx.enter_context(nc.psum_tensor(f"{n}_G{i}", [P, 512], F32)) for i in range(2)]

        weights = sem("weights")
        ctx_in = [sem("ctx_in0"), sem("ctx_in1")]
        setup = sem("setup")
        stats_done = sem("stats_done")
        max_done = sem("max_done")
        rden_done = sem("rden_done")
        qscale_done = sem("qscale_done")
        var_ready = sem("var_ready")
        rstd_ready = sem("rstd_ready")
        xn_ready = sem("xn_ready")
        xnT_ps = sem("xnT_ps")
        xnT_ready = sem("xnT_ready")
        q_ps = sem("q_ps")
        k_ps = sem("k_ps")
        v_ps = sem("v_ps")
        qT_ready = sem("qT_ready")
        qx_ready = [sem("qx_ready0"), sem("qx_ready1")]
        kT_ready = sem("kT_ready")
        v_ready = sem("v_ready")
        s_ps = sem("s_ps")
        d_ready = sem("d_ready")
        e_ready = sem("e_ready")
        et_ps = sem("et_ps")
        et_ready = sem("et_ready")
        pv_ps = sem("pv_ps")
        o_ready = sem("o_ready")
        ot_ps = sem("ot_ps")
        ot_ready = sem("ot_ready")
        y_ps = sem("y_ps")
        x_done = sem("x_done")

        N_WEIGHTS = 9 if cross else 4

        passed = sem("passed")
        block = ctx.enter_context(nc.Block())

        @block.sync
        def _(sp):
            w = "L0_xattn_" if cross else "L0_attn_"
            names = [(wq, "wqT"), (wk, "wkT"), (wv, "wvT"), (wo, "woT")]
            if cross:
                names += [(bq, "bq"), (bk, "bk"), (bv, "bv"), (bo, "bo"), (temp, "temp")]
            for dst, name in names:
                sp.dma_start(dst[:], d[w + name]).then_inc(weights, 16)

            def load_ctx(nb, p):
                if cross:
                    sp.dma_start(ctxT[:, p, :], d["ctxT"][:, bass.ds(nb * TOK, TOK)]).then_inc(ctx_in[p], 16)

            def spread(nb, p):
                if not isinstance(nb, int) or nb >= 2:
                    wait_here(sp, s_ps, (nb - 1) * BB, passed)
                sp.wait_ge(qT_ready, nb + 1)
                for h in range(H):
                    r = slice(h * D0, (h + 1) * D0)
                    sp.dma_start(QX[r, p, :, h * T:(h + 1) * T], QT[r, :].rearrange("c (b t) -> c b t", t=T)).then_inc(qx_ready[p], 16)

            def prologue():
                load_ctx(0, 0)
                sp.wait_ge(setup, 2)
                spread(0, 0)

            def step(blk, p, prev, nxt):
                if nxt:
                    if prev:
                        wait_here(sp, v_ps, blk, passed)
                    load_ctx(blk + 1, 1 - p)
                    spread(blk + 1, 1 - p)

            run_blocks(sp, NB, prologue, step, lambda: None)

        @block.gpsimd
        def _(pool):
            nc.gpsimd.memset(minus_half[:], -0.5).then_inc(setup, 1)
            nc.gpsimd.memset(QX[:], 0.0).then_inc(setup, 1)
            nc.gpsimd.memset(V[:], 0.0).then_inc(setup, 1)
            pool.wait_ge(setup, 3)
            for j in range(2):
                half = V[64 * j:64 * j + 64, :, :, :, 4 * D0 + j:4 * D0 + j + 1]
                nc.gpsimd.memset(half.rearrange("p a b c e -> p (a b c) e"), 1.0).then_inc(setup, 1)

            def power(nb):
                pool.wait_ge(var_ready, nb + 1)
                nc.gpsimd.tensor_tensor(rstd[:], var_eps[:], minus_half[:], ALU.pow).then_inc(rstd_ready, 1)

            def step(blk, p, prev, nxt):
                if nxt:
                    power(blk + 1)

            run_blocks(pool, NB, lambda: power(0), step, lambda: None)

        @block.tensor
        def _(pe):
            def transpose_x(nb):
                pe.wait_ge(xn_ready, nb + 1)
                if not isinstance(nb, int) or nb >= 2:
                    pe.wait_ge(ot_ready, (nb - 1) * 2)
                for u in range(UB):
                    mm = nc.tensor.transpose(G_ps[1][:, u * P:(u + 1) * P], xn[:, u, :], k.ident[:])
                mm.then_inc(xnT_ps, 1)

            def project_q(nb):
                pe.wait_ge(xnT_ready, nb + 1)
                if not isinstance(nb, int) or nb >= 2:
                    pe.wait_ge(x_done, nb - 1)
                nc.tensor.matmul(G_ps[0][:], wq[:], xnT[:], start=True, stop=True).then_inc(q_ps, 1)

            def project_k(nb, p):
                if cross:
                    pe.wait_ge(ctx_in[p], (nb // 2 + 1) * 16)
                src = ctxT[:, p, :] if cross else xnT[:]
                nc.tensor.matmul(G_ps[1][:], wk[:], src, start=True, stop=True).then_inc(k_ps, 1)

            def project_v(nb, p):
                pe.wait_ge(qT_ready, nb + 1)
                for u in range(UB):
                    src = ctxT[:, p, u * P:(u + 1) * P] if cross else xnT[:, u * P:(u + 1) * P]
                    out = G_ps[0][:, u * P:(u + 1) * P]
                    mm = nc.tensor.matmul(out, src, wv[:], start=True, stop=not cross)
                    if cross:
                        mm = nc.tensor.matmul(out, k.ones_row[0:1, 0:P], bv[:], start=False, stop=True)
                mm.then_inc(v_ps, 1)

            def scores(blk, b, p):
                n_ = blk * BB + b
                if b == 0:
                    pe.wait_ge(qx_ready[p], (blk // 2 + 1) * 16 * H)
                    pe.wait_ge(kT_ready, blk + 1)
                if not (isinstance(blk, int) and blk == 0 and b < 2):
                    pe.wait_ge(d_ready, n_ - 1)
                bank = S_ps[b % 2]
                if not cross:
                    nc.tensor.matmul(bank[:], k.causal_queries[0:T, :], k.causal_keys[0:T, 0:PAIRS * T], start=True, stop=False)
                for j in range(PAIRS):
                    mm = nc.tensor.matmul(bank[:, j * T:(j + 1) * T], QX[:, p, b, 2 * j * T:2 * (j + 1) * T],
                                          KT[:, p, b * T:(b + 1) * T], start=cross, stop=cross or j == PAIRS - 1)
                mm.then_inc(s_ps, 1)

            def transpose_e(blk, b):
                n_ = blk * BB + b
                pe.wait_ge(e_ready, n_ + 1)
                if not (isinstance(blk, int) and blk == 0 and b < 2):
                    pe.wait_ge(et_ready, n_ - 1)
                for j in range(PAIRS // 2):
                    mm = nc.tensor.transpose(ET_ps[b % 2][:, j * P:(j + 1) * P], E[:, b % 4, j * P:(j + 1) * P], k.ident[:])
                mm.then_inc(et_ps, 1)

            def weigh_values(blk, b, p):
                n_ = blk * BB + b
                if b == 0:
                    pe.wait_ge(v_ready, blk + 1)
                pe.wait_ge(et_ready, n_ + 1)
                if not (isinstance(blk, int) and blk == 0 and b < 2):
                    pe.wait_ge(o_ready, n_ - 1)
                for j in range(PAIRS // 2):
                    mm = nc.tensor.matmul(PV_ps[b % 2][:, j * VW:(j + 1) * VW], ET[:, b % 2, j * P:(j + 1) * P],
                                          V[:, p, b, j, :], start=True, stop=True)
                mm.then_inc(pv_ps, 1)

            def transpose_o(blk, half, p):
                pe.wait_ge(o_ready, blk * BB + 4 * half + 4)
                wait_here(pe, xnT_ready, blk + 1, passed)
                for q in range(4):
                    mm = nc.tensor.transpose(G_ps[1][0:64, q * P:(q + 1) * P], O[:, 4 * half + q, :], k.ident[:])
                mm.then_inc(ot_ps, 1)

            def project_o(blk, p):
                pe.wait_ge(ot_ready, blk * 2 + 2)
                for u in range(UB):
                    out = G_ps[0][:, u * P:(u + 1) * P]
                    for r in range(2):
                        mm = nc.tensor.matmul(out, OT[:, r, u * P:(u + 1) * P], wo[:, r, :], start=(r == 0),
                                              stop=(r == 1 and not cross))
                    if cross:
                        mm = nc.tensor.matmul(out, k.ones_row[0:1, 0:P], bo[:], start=False, stop=True)
                mm.then_inc(y_ps, 1)

            def prologue():
                pe.wait_ge(weights, 16 * N_WEIGHTS)
                pe.wait_ge(setup, 5)
                transpose_x(0)
                project_q(0)
                pe.wait_ge(xnT_ready, 1)
                project_k(0, 0)
                project_v(0, 0)
                for b in range(LAG):
                    scores(0, b, 0)
                transpose_e(0, 0)

            def step(blk, p, prev, nxt):
                for b in range(BB):
                    if prev and b == 0:
                        pe.wait_ge(ot_ready, blk * 2 - 1)
                        transpose_o(blk - 1, 1, 1 - p)
                    if prev and b == 1:
                        pe.wait_ge(v_ready, blk + 1)
                        project_o(blk - 1, 1 - p)
                    if nxt and b == 2:
                        transpose_x(blk + 1)
                    if nxt and b == 3:
                        if prev:
                            pe.wait_ge(x_done, blk)
                        project_q(blk + 1)
                        project_k(blk + 1, 1 - p)
                    if nxt and b == 4:
                        project_v(blk + 1, 1 - p)
                    if b == 6:
                        if nxt:
                            pe.wait_ge(kT_ready, blk + 2)
                        transpose_o(blk, 0, p)
                    if b + LAG < BB:
                        scores(blk, b + LAG, p)
                    elif nxt:
                        scores(blk + 1, b + LAG - BB, 1 - p)
                    if b + 1 < BB:
                        transpose_e(blk, b + 1)
                    elif nxt:
                        transpose_e(blk + 1, 0)
                    weigh_values(blk, b, p)

            def epilogue():
                p = (NB - 1) % 2
                pe.wait_ge(ot_ready, NB * 2 - 1)
                transpose_o(NB - 1, 1, p)
                pe.wait_ge(v_ready, NB)
                project_o(NB - 1, p)

            run_blocks(pe, NB, prologue, step, epilogue)

        @block.scalar
        def _(act):
            def evacuate_xT(nb):
                act.wait_ge(xnT_ps, nb + 1)
                if not isinstance(nb, int) or nb >= 1:
                    act.wait_ge(v_ps, nb)
                nc.scalar.activation(xnT[:], G_ps[1][:], ACT.Copy).then_inc(xnT_ready, 1)

            def evacuate_k(nb, p):
                act.wait_ge(k_ps, nb + 1)
                if not isinstance(nb, int) or nb >= 2:
                    act.wait_ge(s_ps, (nb - 1) * BB)
                if cross:
                    nc.scalar.activation(KT[:, p, :], G_ps[1][:], ACT.Identity, bias=bk[:, 0:1]).then_inc(kT_ready, 1)
                else:
                    nc.scalar.activation(KT[:, p, :], G_ps[1][:], ACT.Copy).then_inc(kT_ready, 1)

            def evacuate_v(nb, p):
                act.wait_ge(v_ps, nb + 1)
                if not isinstance(nb, int) or nb >= 2:
                    act.wait_ge(pv_ps, (nb - 1) * BB)
                src = G_ps[0][:].rearrange("p (u j r e) -> p u j r e", u=UB, j=PAIRS // 2, r=2)
                dst = V[:, p].rearrange("p (u r) j e -> p u r j e", r=2)
                for r in range(2):
                    for j in range(2):
                        last = nc.scalar.activation(dst[64 * j:64 * j + 64, :, r, :, 2 * D0 * j:2 * D0 * (j + 1)],
                                                    src[64 * r:64 * r + 64, :, :, j, :], ACT.Copy)
                last.then_inc(v_ready, 1)

            def exponentials(blk, b):
                n_ = blk * BB + b
                act.wait_ge(d_ready, n_ + 1)
                nc.scalar.activation(E[:, b % 4, :], E[:, b % 4, :], ACT.Exp,
                                     scale=1.0 if cross else float(D0) ** -0.5).then_inc(e_ready, 1)

            def evacuate_e(blk, b):
                n_ = blk * BB + b
                act.wait_ge(et_ps, n_ + 1)
                if not (isinstance(blk, int) and blk == 0 and b < 2):
                    act.wait_ge(pv_ps, n_ - 1)
                nc.scalar.activation(ET[:, b % 2, :], ET_ps[b % 2][:], ACT.Copy).then_inc(et_ready, 1)

            def evacuate_o(blk, half, p):
                act.wait_ge(ot_ps, blk * 2 + half + 1)
                if half == 0 and (not isinstance(blk, int) or blk >= 1):
                    act.wait_ge(y_ps, blk)
                dst = OT[:, :, half * 256:(half + 1) * 256].rearrange("e r (b t) -> e r b t", b=4)
                src = G_ps[1][0:64, :].rearrange("e (b r t) -> e r b t", b=4, r=2)
                nc.scalar.activation(dst, src, ACT.Copy).then_inc(ot_ready, 1)

            def prologue():
                act.wait_ge(weights, 16 * N_WEIGHTS)
                act.wait_ge(setup, 5)
                evacuate_xT(0)
                evacuate_k(0, 0)
                evacuate_v(0, 0)
                for b in range(LAG):
                    exponentials(0, b)
                evacuate_e(0, 0)

            def step(blk, p, prev, nxt):
                for b in range(BB):
                    if prev and b == 0:
                        evacuate_o(blk - 1, 1, 1 - p)
                    if nxt and b == 2:
                        evacuate_xT(blk + 1)
                    if nxt and b == 3:
                        evacuate_k(blk + 1, 1 - p)
                    if nxt and b == 4:
                        evacuate_v(blk + 1, 1 - p)
                    if b == 6:
                        evacuate_o(blk, 0, p)
                    if b + LAG < BB:
                        exponentials(blk, b + LAG)
                    elif nxt:
                        exponentials(blk + 1, b + LAG - BB)
                    if b + 1 < BB:
                        evacuate_e(blk, b + 1)
                    elif nxt:
                        evacuate_e(blk + 1, 0)

            run_blocks(act, NB, prologue, step, lambda: evacuate_o(NB - 1, 1, (NB - 1) % 2))

        @block.vector
        def _(dve):
            def statistics(nb):
                for u in range(UB):
                    last = nc.vector.bn_stats(stats[:, u, :], k.X[:, nb * UB + u, :])
                last.then_inc(stats_done, 1)
                wait_here(dve, stats_done, nb * 2 + 1, passed)
                for u in range(UB):
                    last = nc.vector.bn_aggr(mv[:, u, :], stats[:, u, :])
                last.then_inc(stats_done, 1)
                dve.wait_ge(stats_done, nb * 2 + 2)
                nc.vector.tensor_scalar(var_eps[:], mv[:, :, 1], EPS, None, ALU.add).then_inc(var_ready, 1)

            def normalise(nb):
                dve.wait_ge(rstd_ready, nb + 1)
                if not isinstance(nb, int) or nb >= 1:
                    dve.wait_ge(xnT_ps, nb)
                for u in range(UB):
                    last = nc.vector.tensor_scalar(xn[:, u, :], k.X[:, nb * UB + u, :], mv[:, u, 0:1], rstd[:, u:u + 1],
                                                   ALU.subtract, ALU.mult)
                last.then_inc(xn_ready, 1)

            def evacuate_q(nb, p):
                dve.wait_ge(q_ps, nb + 1)
                if not isinstance(nb, int) or nb >= 1:
                    dve.wait_ge(qx_ready[1 - p], ((nb + 1) // 2) * 16 * H)
                if cross:
                    nc.vector.tensor_scalar(QT[:], G_ps[0][:], bq[:, 0:1], qscale[:, 0:1], ALU.add, ALU.mult)\
                        .then_inc(qT_ready, 1)
                else:
                    nc.vector.tensor_copy(QT[:], G_ps[0][:]).then_inc(qT_ready, 1)

            def subtract_max(blk, b):
                n_ = blk * BB + b
                dve.wait_ge(s_ps, n_ + 1)
                bank = S_ps[b % 2][:].rearrange("p (j t) -> p j t", t=T)
                nc.vector.tensor_reduce(row_max[:, b % 2, :], bank, AX.X, ALU.max).then_inc(max_done, 1)
                dve.wait_ge(max_done, n_ + 1)
                if not (isinstance(blk, int) and blk == 0 and b < 4):
                    dve.wait_ge(et_ps, n_ - 3)
                nc.vector.tensor_tensor(E[:, b % 4, :].rearrange("p (j t) -> p j t", t=T), bank,
                                        row_max[:, b % 2, :].unsqueeze(2).broadcast_to([P, PAIRS, T]),
                                        ALU.subtract).then_inc(d_ready, 1)

            def normalise_output(blk, b, p):
                n_ = blk * BB + b
                dve.wait_ge(pv_ps, n_ + 1)
                if b == 0 and (not isinstance(blk, int) or blk >= 1):
                    dve.wait_ge(ot_ps, blk * 2)
                bank = PV_ps[b % 2][:, 0:VW * PAIRS // 2].rearrange("p (j e) -> p j e", e=VW)
                r = rden[:, b % 2, :].rearrange("p (j i) -> p j i", i=2)
                nc.vector.reciprocal(r, bank[:, :, 4 * D0:4 * D0 + 2]).then_inc(rden_done, 1)
                dve.wait_ge(rden_done, n_ + 1)
                for h in range(2):
                    s = slice(64 * h, 64 * h + 64)
                    src = bank[s, :, 0:4 * D0].rearrange("p j (i h e) -> p j i h e", i=2, h=2)[:, :, :, h, :]
                    dst = O[s, b, :].rearrange("p (j i e) -> p j i e", j=PAIRS // 2, i=2)
                    last = nc.vector.tensor_tensor(dst, src, r[s].unsqueeze(3).broadcast_to([64, PAIRS // 2, 2, D0]),
                                                   ALU.mult)
                last.then_inc(o_ready, 1)

            def add_residual(blk):
                dve.wait_ge(y_ps, blk + 1)
                x = k.X[:, bass.ds(blk * UB, UB), :]
                nc.vector.tensor_tensor(x, G_ps[0][:].rearrange("p (u c) -> p u c", u=UB), x, ALU.add).then_inc(x_done, 1)

            def prologue():
                dve.wait_ge(setup, 5)
                dve.wait_ge(weights, 16 * N_WEIGHTS)
                if cross:
                    nc.vector.reciprocal(temp[:], temp[:]).then_inc(qscale_done, 1)
                    dve.wait_ge(qscale_done, 1)
                    nc.vector.tensor_scalar(qscale[:], temp[:], float(D0) ** -0.5, None, ALU.mult).then_inc(qscale_done, 1)
                    dve.wait_ge(qscale_done, 2)
                statistics(0)
                normalise(0)
                evacuate_q(0, 0)
                for b in range(LAG):
                    subtract_max(0, b)

            def step(blk, p, prev, nxt):
                for b in range(BB):
                    if nxt and b == 0:
                        statistics(blk + 1)
                    if nxt and b == 1:
                        normalise(blk + 1)
                    if prev and b == 2:
                        add_residual(blk - 1)
                    if nxt and b == 3:
                        evacuate_q(blk + 1, 1 - p)
                    if b + LAG < BB:
                        subtract_max(blk, b + LAG)
                    elif nxt:
                        subtract_max(blk + 1, b + LAG - BB)
                    normalise_output(blk, b, p)

            run_blocks(dve, NB, prologue, step, lambda: add_residual(NB - 1))


def mixture_phases(nc, k):
    UB = 4
    NB = NU // UB
    TOK = UB * P
    NE = 8
    F = 512
    FC = F // P
    NT = 2 * NU + NE
    d = k.d
    with ExitStack() as ctx:
        def sb(name, shape, dt=F32):
            return ctx.enter_context(nc.sbuf_tensor(f"m0_{name}", shape, dt))

        XN = sb("XN", [P, NU, C])
        LG = sb("LG", [P, NU, NE])
        gates = sb("gates", [P, 2, NU])
        slots = sb("slots", [P, 2, NU], I32)
        experts = sb("experts", [1, NT], I32)
        gate_w = sb("gate_w", [P, NE * F])
        up_w = sb("up_w", [P, NE * F])
        down_w = sb("down_w", [P, NE * F])
        w_loaded = nc.alloc_semaphore("m0_w_loaded")
        run_phase(nc, router_phase, k, XN, LG, gate_w, up_w, down_w, w_loaded)
        run_phase(nc, plan_phase, k, LG, gates, slots, experts)
        run_phase(nc, scatter_phase, k, XN, slots)
        run_phase(nc, expert_phase, k, experts, gate_w, up_w, down_w, w_loaded, NT)
        run_phase(nc, combine_phase, k, gates, slots)


def router_phase(nc, k, XN, LG, gate_w, up_w, down_w, w_loaded):
    UB = 4
    NB = NU // UB
    NE = 8
    d = k.d
    with ExitStack() as ctx:
        def sb(name, shape, dt=F32):
            return ctx.enter_context(nc.sbuf_tensor(f"r_{name}", shape, dt))

        def sem(name):
            return nc.alloc_semaphore(f"r_{name}")

        rw = sb("rw", [P, NE])
        rb = sb("rb", [1, NE])
        stats = sb("stats", [P, UB, 6])
        mv = sb("mv", [P, UB, 2])
        var_eps = sb("var_eps", [P, UB])
        minus_half = sb("minus_half", [P, UB])
        rstd = sb("rstd", [P, UB])
        xn = sb("xn", [P, 2, UB, C])
        xnT = sb("xnT", [P, 2, UB * P])
        T_ps = [ctx.enter_context(nc.psum_tensor(f"r_T{i}", [P, 512], F32)) for i in range(2)]
        L_ps = [ctx.enter_context(nc.psum_tensor(f"r_L{i}", [P, 512], F32)) for i in range(2)]

        loaded = sem("loaded")
        setup = sem("setup")
        stats_done = sem("stats_done")
        var_ready = sem("var_ready")
        rstd_ready = sem("rstd_ready")
        xn_ready = sem("xn_ready")
        kept = sem("kept")
        xnT_ps = sem("xnT_ps")
        xnT_ready = sem("xnT_ready")
        l_ps = sem("l_ps")
        l_ready = sem("l_ready")
        passed = sem("passed")
        block = ctx.enter_context(nc.Block())

        def later(blk, least):
            return not isinstance(blk, int) or blk >= least

        def pairs(eng, body):
            body(0, 0)
            body(1, 1)
            with eng.Fori(1, NB // 2) as i:
                body(i * 2, 0)
                body(i * 2 + 1, 1)

        @block.sync
        def _(sp):
            sp.dma_start(rw[:], d["L0_ffn_router_w"]).then_inc(loaded, 16)
            sp.dma_start(rb[:], d["L0_ffn_router_b"]).then_inc(loaded, 16)
            for w, name in ((gate_w, "gate_w"), (up_w, "up_w"), (down_w, "down_w")):
                sp.dma_start(w[:], d[f"L0_ffn_{name}"]).then_inc(w_loaded, 16)

        @block.gpsimd
        def _(pool):
            nc.gpsimd.memset(minus_half[:], -0.5).then_inc(setup, 1)
            pool.wait_ge(setup, 1)

            def body(blk, p):
                pool.wait_ge(var_ready, blk + 1)
                nc.gpsimd.tensor_tensor(rstd[:], var_eps[:], minus_half[:], ALU.pow).then_inc(rstd_ready, 1)
                pool.wait_ge(xn_ready, blk + 1)
                nc.gpsimd.tensor_copy(XN[:, bass.ds(blk * UB, UB), :], xn[:, p]).then_inc(kept, 1)

            pairs(pool, body)

        @block.tensor
        def _(pe):
            pe.wait_ge(loaded, 32)

            def logits(blk, p):
                pe.wait_ge(xnT_ready, blk + 1)
                if later(blk, 2):
                    pe.wait_ge(l_ready, blk - 1)
                for u in range(UB):
                    out = L_ps[p][:, u * NE:(u + 1) * NE]
                    nc.tensor.matmul(out, xnT[:, p, u * P:(u + 1) * P], rw[:], start=True, stop=False)
                    mm = nc.tensor.matmul(out, k.ones_row[0:1, 0:P], rb[:], start=False, stop=True)
                mm.then_inc(l_ps, 1)

            def body(blk, p):
                pe.wait_ge(xn_ready, blk + 1)
                if later(blk, 2):
                    pe.wait_ge(xnT_ready, blk - 1)
                for u in range(UB):
                    mm = nc.tensor.transpose(T_ps[p][:, u * P:(u + 1) * P], xn[:, p, u, :], k.ident[:])
                mm.then_inc(xnT_ps, 1)
                logits(blk, p)

            pairs(pe, body)

        @block.scalar
        def _(act):
            def body(blk, p):
                act.wait_ge(xnT_ps, blk + 1)
                if later(blk, 2):
                    act.wait_ge(l_ps, blk - 1)
                nc.scalar.activation(xnT[:, p, :], T_ps[p][:], ACT.Copy).then_inc(xnT_ready, 1)
                act.wait_ge(l_ps, blk + 1)
                nc.scalar.activation(LG[:, bass.ds(blk * UB, UB), :], L_ps[p][:, 0:UB * NE].rearrange("p (u e) -> p u e", e=NE),
                                     ACT.Copy).then_inc(l_ready, 1)

            pairs(act, body)

        @block.vector
        def _(dve):
            def body(blk, p):
                for u in range(UB):
                    last = nc.vector.bn_stats(stats[:, u, :], k.X[:, blk * UB + u, :])
                last.then_inc(stats_done, 1)
                wait_here(dve, stats_done, blk * 2 + 1, passed)
                for u in range(UB):
                    last = nc.vector.bn_aggr(mv[:, u, :], stats[:, u, :])
                last.then_inc(stats_done, 1)
                dve.wait_ge(stats_done, blk * 2 + 2)
                nc.vector.tensor_scalar(var_eps[:], mv[:, :, 1], EPS, None, ALU.add).then_inc(var_ready, 1)
                dve.wait_ge(rstd_ready, blk + 1)
                if later(blk, 2):
                    dve.wait_ge(xnT_ps, blk - 1)
                    dve.wait_ge(kept, blk - 1)
                for u in range(UB):
                    last = nc.vector.tensor_scalar(xn[:, p, u, :], k.X[:, blk * UB + u, :], mv[:, u, 0:1], rstd[:, u:u + 1],
                                                   ALU.subtract, ALU.mult)
                last.then_inc(xn_ready, 1)

            pairs(dve, body)


def plan_phase(nc, k, LG, gates, slots, experts):
    NE = 8
    N = NU * NE
    NT = experts.shape[1]
    d = k.d
    with ExitStack() as ctx:
        def sb(name, shape, dt=F32):
            return ctx.enter_context(nc.sbuf_tensor(f"p_{name}", shape, dt))

        def sem(name):
            return nc.alloc_semaphore(f"p_{name}")

        upper = sb("upper", [P, P])
        ones = sb("ones", [P, P])
        rank = sb("rank", [P, NE])
        tile_no = sb("tile_no", [1, NT])
        best = sb("best", [P, 2, NU])
        eq = sb("eq", [P, NU, NE])
        who = sb("who", [P, 2, NU])
        hot = sb("hot", [P, 2, NU, NE])
        rest = sb("rest", [P, NU, NE])
        chosen = sb("chosen", [P, N])
        delta = sb("delta", [P, NU])
        ratio = sb("ratio", [P, NU])
        total = sb("total", [P, 1 + N // NE, NE])
        run = sb("run", [P, 2, N])
        place = sb("place", [P, N])
        count = sb("count", [P, NE])
        tiles_i = sb("tiles_i", [P, NE], I32)
        base = sb("base", [P, 2, NE])
        picked = sb("picked", [P, NU, NE])
        slot_f = sb("slot_f", [P, 2, NU])
        past = sb("past", [1, NT, NE - 1])
        expert_f = sb("expert_f", [1, NT])
        before_ps = ctx.enter_context(nc.psum_tensor("p_before_ps", [P, 512], F32))
        total_ps = ctx.enter_context(nc.psum_tensor("p_total_ps", [P, 512], F32))

        loaded = sem("loaded")
        chain = sem("chain")
        chosen_ready = sem("chosen_ready")
        delta_ready = sem("delta_ready")
        ratio_ready = sem("ratio_ready")
        counted = sem("counted")
        block = ctx.enter_context(nc.Block())

        @block.sync
        def _(sp):
            for dst, name in ((upper, "c_upper"), (ones, "c_ones"), (rank, "c_rank"), (tile_no, "c_tile_no")):
                sp.dma_start(dst[:], d[name]).then_inc(loaded, 16)

        @block.tensor
        def _(pe):
            pe.wait_ge(loaded, 64)
            pe.wait_ge(chosen_ready, 1)
            nc.tensor.matmul(before_ps[:, 0:N], upper[:], chosen[:], start=True, stop=True).then_inc(counted, 1)
            nc.tensor.matmul(total_ps[:, 0:N], ones[:], chosen[:], start=True, stop=True).then_inc(counted, 1)

        @block.scalar
        def _(act):
            act.wait_ge(delta_ready, 1)
            nc.scalar.activation(ratio[:], delta[:], ACT.Exp).then_inc(ratio_ready, 1)

        @block.vector
        def _(dve):
            steps = [0]

            def chained(ins):
                steps[0] += 1
                ins.then_inc(chain, 1)
                dve.wait_ge(chain, steps[0])

            tt, ts = nc.vector.tensor_tensor, nc.vector.tensor_scalar
            by_unit = lambda ap: ap.unsqueeze(2).broadcast_to([P, NU, NE])
            dve.wait_ge(loaded, 64)
            for i, logits in enumerate((LG, rest)):
                chained(nc.vector.tensor_reduce(best[:, i], logits[:], AX.X, ALU.max))
                chained(tt(eq[:], logits[:], by_unit(best[:, i]), ALU.is_equal))
                chained(tt(eq[:], eq[:], rank[:].unsqueeze(1).broadcast_to([P, NU, NE]), ALU.mult))
                chained(nc.vector.tensor_reduce(who[:, i], eq[:], AX.X, ALU.max))
                chained(tt(hot[:, i], rank[:].unsqueeze(1).broadcast_to([P, NU, NE]), by_unit(who[:, i]), ALU.is_equal))
                if i == 0:
                    chained(nc.vector.scalar_tensor_tensor(out=rest[:], in0=hot[:, 0], scalar=NEG, in1=LG[:],
                                                           op0=ALU.mult, op1=ALU.add))
            tt(delta[:], best[:, 1], best[:, 0], ALU.subtract).then_inc(delta_ready, 1)
            tt(chosen[:].rearrange("p (u e) -> p u e", e=NE), hot[:, 0], hot[:, 1], ALU.add).then_inc(chosen_ready, 1)
            dve.wait_ge(ratio_ready, 1)
            chained(ts(gates[:, 0], ratio[:], 1.0, None, ALU.add))
            chained(nc.vector.reciprocal(gates[:, 0], gates[:, 0]))
            chained(tt(gates[:, 1], ratio[:], gates[:, 0], ALU.mult))
            dve.wait_ge(counted, 2)
            chained(nc.vector.tensor_copy(run[:, 0], total_ps[:, 0:N]))
            src = 0
            reach = 1
            while reach < NU:
                w = reach * NE
                nc.vector.tensor_copy(run[:, 1 - src, 0:w], run[:, src, 0:w])
                chained(tt(run[:, 1 - src, w:N], run[:, src, w:N], run[:, src, 0:N - w], ALU.add))
                src, reach = 1 - src, reach * 2
            nc.vector.tensor_copy(count[:], run[:, src, N - NE:N])
            chained(tt(place[:], before_ps[:, 0:N], run[:, src], ALU.add))
            chained(tt(place[:], total_ps[:, 0:N], place[:], ALU.subtract))
            chained(ts(place[:], place[:], -1.0, None, ALU.mult))
            chained(ts(count[:], count[:], float(P - 1), None, ALU.add))
            chained(nc.vector.tensor_copy(tiles_i[:], count[:]))
            chained(ts(tiles_i[:], tiles_i[:], 7, None, ALU.arith_shift_right))
            chained(nc.vector.tensor_copy(base[:, 0], tiles_i[:]))
            chained(nc.vector.tensor_copy(count[:], base[:, 0]))
            b = 0
            for reach in (1, 2, 4):
                nc.vector.tensor_copy(base[:, 1 - b, 0:reach], base[:, b, 0:reach])
                chained(tt(base[:, 1 - b, reach:NE], base[:, b, reach:NE], base[:, b, 0:NE - reach], ALU.add))
                b = 1 - b
            chained(tt(base[:, b], base[:, b], count[:], ALU.subtract))
            chained(tt(past[:], tile_no[:].unsqueeze(2).broadcast_to([1, NT, NE - 1]),
                       base[0:1, b, 1:NE].unsqueeze(1).broadcast_to([1, NT, NE - 1]), ALU.is_ge))
            chained(nc.vector.tensor_reduce(expert_f[:], past[:], AX.X, ALU.add))
            nc.vector.tensor_copy(experts[:], expert_f[:])
            chained(ts(base[:, 1 - b], base[:, b], float(P), None, ALU.mult))
            chained(tt(place[:].rearrange("p (u e) -> p u e", e=NE), place[:].rearrange("p (u e) -> p u e", e=NE),
                       base[:, 1 - b].unsqueeze(1).broadcast_to([P, NU, NE]), ALU.add))
            for i in range(2):
                chained(tt(picked[:], hot[:, i], place[:].rearrange("p (u e) -> p u e", e=NE), ALU.mult))
                chained(nc.vector.tensor_reduce(slot_f[:, i], picked[:], AX.X, ALU.add))
            chained(nc.vector.tensor_copy(slots[:], slot_f[:]))


def scatter_phase(nc, k, XN, slots):
    UB = 4
    NB = NU // UB
    with ExitStack() as ctx:
        def sem(name):
            return nc.alloc_semaphore(f"s_{name}")

        rows = ctx.enter_context(nc.sbuf_tensor("s_rows", [P, 2, UB, C], F32))
        where = ctx.enter_context(nc.sbuf_tensor("s_where", [P, 2, 2, UB], I32))
        rows_ready = sem("rows_ready")
        where_ready = sem("where_ready")
        sent = [sem("sent0"), sem("sent1")]
        passed = sem("passed")
        block = ctx.enter_context(nc.Block())

        def pairs(eng, body):
            body(0, 0)
            body(1, 1)
            with eng.Fori(1, NB // 2) as i:
                body(i * 2, 0)
                body(i * 2 + 1, 1)

        def free(eng, blk, p):
            if not isinstance(blk, int):
                eng.wait_ge(sent[p], (blk // 2) * (16 * 2 * UB))

        @block.vector
        def _(dve):
            def body(blk, p):
                free(dve, blk, p)
                nc.vector.tensor_copy(where[:, p], slots[:, :, bass.ds(blk * UB, UB)]).then_inc(where_ready, 1)

            pairs(dve, body)

        @block.scalar
        def _(act):
            def body(blk, p):
                free(act, blk, p)
                nc.scalar.activation(rows[:, p], XN[:, bass.ds(blk * UB, UB), :], ACT.Copy).then_inc(rows_ready, 1)

            pairs(act, body)

        @block.gpsimd
        def _(pool):
            pool.wait_ge(k.zeroed, 16 * k.n_zeroed)

            def body(blk, p):
                pool.wait_ge(where_ready, blk + 1)
                wait_here(pool, rows_ready, blk + 1, passed)
                for u in range(UB):
                    for i in range(2):
                        nc.gpsimd.indirect_dma_start(
                            out=k.slot_rows, out_offset=bass.IndirectOffsetOnAxis(ap=where[:, p, i, u:u + 1], axis=0),
                            in_=rows[:, p, u, :], in_offset=None).then_inc(sent[p], 16)

            pairs(pool, body)
            for q in sent:
                pool.wait_ge(q, (NB // 2) * 16 * 2 * UB)


def expert_phase(nc, k, experts, gate_w, up_w, down_w, w_loaded, NT):
    F = 512
    FC = F // P
    with ExitStack() as ctx:
        def sb(name, shape, dt=F32):
            return ctx.enter_context(nc.sbuf_tensor(f"e_{name}", shape, dt))

        def ps(name):
            return ctx.enter_context(nc.psum_tensor(f"e_{name}_ps", [P, 512], F32))

        def sem(name):
            return nc.alloc_semaphore(f"e_{name}")

        x = sb("x", [P, 4, C])
        xT = sb("xT", [P, 2, P])
        silu = sb("silu", [P, 2, F])
        h = sb("h", [P, 2, F])
        hT = sb("hT", [P, 2, F])
        y = sb("y", [P, 2, C])
        xT_ps = ps("xT")
        G_ps = [ps(f"G{i}") for i in range(2)]
        U_ps = [ps(f"U{i}") for i in range(2)]
        hT_ps = [ps(f"hT{i}") for i in range(2)]
        Y_ps = ps("Y")

        x_in = [sem(f"x_in{i}") for i in range(4)]
        xT_done = sem("xT_done")
        xT_ready = sem("xT_ready")
        gate_done = sem("gate_done")
        up_done = sem("up_done")
        silu_ready = sem("silu_ready")
        h_ready = sem("h_ready")
        hT_done = sem("hT_done")
        hT_ready = sem("hT_ready")
        y_done = sem("y_done")
        y_ready = sem("y_ready")
        stored = [sem("stored0"), sem("stored1")]
        passed = sem("passed")
        block = ctx.enter_context(nc.Block())
        Q = 4

        def later(t, least):
            return not isinstance(t, int) or t >= least

        def tiles(eng, body):
            for j in range(Q):
                body(j, j, NT)
            with eng.Fori(1, NT // Q - 1) as i:
                for j in range(Q):
                    body(i * Q + j, j, NT)
            for j in range(Q):
                body(NT - Q + j, j, Q - j)

        @block.sync
        def _(sp):
            def body(t, j, left):
                if later(t, 4):
                    wait_here(sp, xT_done, t - 3, passed)
                sp.dma_start(x[:, j, :], k.slot_rows[bass.ds(t * P, P), :]).then_inc(x_in[j], 16)

            tiles(sp, body)

        @block.scalar
        def _(act):
            def body(t, j, left):
                p = j % 2
                act.wait_ge(gate_done, t + 1)
                if later(t, 2):
                    act.wait_ge(h_ready, t - 1)
                nc.scalar.activation(silu[:, p, :], G_ps[p][:], ACT.Silu).then_inc(silu_ready, 1)
                if later(t, 1):
                    hidden_turned(t - 1, 1 - p)

            def hidden_turned(t, p):
                act.wait_ge(hT_done, t + 1)
                if later(t, 2):
                    act.wait_ge(y_done, t - 1)
                nc.scalar.activation(hT[:, p, :], hT_ps[p][:], ACT.Copy).then_inc(hT_ready, 1)

            tiles(act, body)
            hidden_turned(NT - 1, 1)

        @block.tensor
        def _(pe):
            def turn_x(t, j):
                pe.wait_ge(x_in[j], (t // Q + 1) * 16)
                if later(t, 1):
                    pe.wait_ge(xT_ready, t)
                nc.tensor.transpose(xT_ps[:, 0:P], x[:, j, :], k.ident[:]).then_inc(xT_done, 1)

            def gate_up(t, j):
                p = j % 2
                e = nc.tensor.value_load(experts[0:1, bass.ds(t, 1)], min_val=0, max_val=7)
                pe.wait_ge(xT_ready, t + 1)
                if later(t, 2):
                    pe.wait_ge(h_ready, t - 1)
                nc.tensor.matmul(G_ps[p][:], xT[:, p, :], gate_w[:, bass.ds(e * F, F)], start=True, stop=True)\
                    .then_inc(gate_done, 1)
                nc.tensor.matmul(U_ps[p][:], xT[:, p, :], up_w[:, bass.ds(e * F, F)], start=True, stop=True)\
                    .then_inc(up_done, 1)

            def turn_h(t, j):
                p = j % 2
                pe.wait_ge(h_ready, t + 1)
                if later(t, 2):
                    pe.wait_ge(hT_ready, t - 1)
                for c in range(FC):
                    mm = nc.tensor.transpose(hT_ps[p][:, c * P:(c + 1) * P], h[:, p, c * P:(c + 1) * P], k.ident[:])
                mm.then_inc(hT_done, 1)

            def down(t, j):
                p = j % 2
                e = nc.tensor.value_load(experts[0:1, bass.ds(t, 1)], min_val=0, max_val=7)
                pe.wait_ge(hT_ready, t + 1)
                if later(t, 1):
                    pe.wait_ge(y_ready, t)
                for c in range(FC):
                    mm = nc.tensor.matmul(Y_ps[:, 0:C], hT[:, p, c * P:(c + 1) * P], down_w[:, bass.ds(e * F + c * C, C)],
                                          start=(c == 0), stop=(c == FC - 1))
                mm.then_inc(y_done, 1)

            pe.wait_ge(w_loaded, 48)
            turn_x(0, 0)
            turn_x(1, 1)
            gate_up(0, 0)

            def body(t, j, left):
                if left > 2:
                    turn_x(t + 2, (j + 2) % Q)
                if left > 1:
                    gate_up(t + 1, (j + 1) % Q)
                turn_h(t, j)
                if later(t, 1):
                    down(t - 1, (j - 1) % Q)

            tiles(pe, body)
            down(NT - 1, Q - 1)

        @block.vector
        def _(dve):
            def x_turned(t, p):
                dve.wait_ge(xT_done, t + 1)
                if later(t, 2):
                    dve.wait_ge(up_done, t - 1)
                nc.vector.tensor_copy(xT[:, p, :], xT_ps[:, 0:P]).then_inc(xT_ready, 1)

            def output(t, p):
                dve.wait_ge(y_done, t + 1)
                if later(t, 2):
                    dve.wait_ge(stored[p], (t // 2) * 16)
                nc.vector.tensor_copy(y[:, p, :], Y_ps[:, 0:C]).then_inc(y_ready, 1)

            x_turned(0, 0)
            x_turned(1, 1)

            def body(t, j, left):
                p = j % 2
                if left > 2:
                    x_turned(t + 2, p)
                dve.wait_ge(silu_ready, t + 1)
                dve.wait_ge(up_done, t + 1)
                if later(t, 2):
                    dve.wait_ge(hT_done, t - 1)
                nc.vector.tensor_tensor(h[:, p, :], U_ps[p][:], silu[:, p, :], ALU.mult).then_inc(h_ready, 1)
                if later(t, 1):
                    output(t - 1, 1 - p)

            tiles(dve, body)
            output(NT - 1, 1)

        @block.gpsimd
        def _(pool):
            def body(t, j, left):
                p = j % 2
                pool.wait_ge(y_ready, t + 1)
                pool.dma_start(k.slot_out[bass.ds(t * P, P), :], y[:, p, :]).then_inc(stored[p], 16)

            tiles(pool, body)
            for q in stored:
                pool.wait_ge(q, NT // 2 * 16)


def combine_phase(nc, k, gates, slots):
    UB = 4
    NB = NU // UB
    with ExitStack() as ctx:
        def sem(name):
            return nc.alloc_semaphore(f"c_{name}")

        rows = ctx.enter_context(nc.sbuf_tensor("c_rows", [P, 2, 2, UB, C], F32))
        where = ctx.enter_context(nc.sbuf_tensor("c_where", [P, 2, 2, UB], I32))
        where_ready = sem("where_ready")
        got = [sem("got0"), sem("got1")]
        passed = sem("passed")
        added = sem("added")
        summed = sem("summed")
        block = ctx.enter_context(nc.Block())

        def pairs(eng, body):
            body(0, 0)
            body(1, 1)
            with eng.Fori(1, NB // 2) as i:
                body(i * 2, 0)
                body(i * 2 + 1, 1)

        @block.scalar
        def _(act):
            def body(blk, p):
                if not isinstance(blk, int):
                    act.wait_ge(got[p], (blk // 2) * (16 * 2 * UB))
                nc.scalar.activation(where[:, p].rearrange("p i u -> p i u"), slots[:, :, bass.ds(blk * UB, UB)], ACT.Copy)\
                    .then_inc(where_ready, 1)

            pairs(act, body)

        @block.gpsimd
        def _(pool):
            def body(blk, p):
                if not isinstance(blk, int):
                    pool.wait_ge(summed, blk - 1)
                wait_here(pool, where_ready, blk + 1, passed)
                for u in range(UB):
                    for i in range(2):
                        nc.gpsimd.indirect_dma_start(
                            out=rows[:, p, i, u, :], out_offset=None, in_=k.slot_out,
                            in_offset=bass.IndirectOffsetOnAxis(ap=where[:, p, i, u:u + 1], axis=0)).then_inc(got[p], 16)

            pairs(pool, body)

        @block.vector
        def _(dve):
            def body(blk, p):
                dve.wait_ge(got[p], (blk // 2 + 1) * (16 * 2 * UB))
                for i in range(2):
                    for u in range(UB):
                        x = k.X[:, blk * UB + u, :]
                        last = nc.vector.scalar_tensor_tensor(out=x, in0=rows[:, p, i, u, :],
                                                              scalar=gates[:, i, bass.ds(blk * UB + u, 1)], in1=x,
                                                              op0=ALU.mult, op1=ALU.add)
                    if i == 0:
                        last.then_inc(added, 1)
                        dve.wait_ge(added, blk + 1)
                last.then_inc(summed, 1)

            pairs(dve, body)


def wide_attention_phase(nc, k):
    UB = 2
    NB = NU // UB
    BB = 2 * UB
    TOK = UB * P
    D1 = 64
    G = H // 4
    SCALE = float(D1) ** -0.5
    n = "a1"
    d = k.d
    with ExitStack() as ctx:
        def sb(name, shape, dt=F32):
            return ctx.enter_context(nc.sbuf_tensor(f"{n}_{name}", shape, dt))

        def ps(name, shape):
            return ctx.enter_context(nc.psum_tensor(f"{n}_{name}_ps", shape, F32))

        def sem(name):
            return nc.alloc_semaphore(f"{n}_{name}")

        wq = sb("wq", [P, G, 2, P])
        wk = sb("wk", [P, G, 2, P])
        wv = sb("wv", [P, G, 4 * D1])
        wo = sb("wo", [P, G, 2, C])
        bo = sb("bo", [1, C])
        cos = sb("cos", [P, T])
        sin = sb("sin", [P, T])
        parity = sb("parity", [P, 2])
        stats = sb("stats", [P, UB, 6])
        mv = sb("mv", [P, UB, 2])
        var_eps = sb("var_eps", [P, UB])
        minus_half = sb("minus_half", [P, UB])
        rstd = sb("rstd", [P, UB])
        xn = sb("xn", [P, UB, C])
        xnT = sb("xnT", [P, 2, TOK])
        PQ = sb("PQ", [P, 2, 2, TOK])
        PK = sb("PK", [P, 2, 2, TOK])
        RQ = sb("RQ", [P, 2, TOK])
        QD = sb("QD", [P, 2, 2, BB, P])
        KT = sb("KT", [P, 2, 2, TOK])
        V = sb("V", [P, 2, BB, 2, P])
        row_max = sb("row_max", [P, 2, BB])
        row_sum = sb("row_sum", [P, 2 * BB])
        rsum = sb("rsum", [P, 2, 2 * BB])
        E = sb("E", [P, 2, 512])
        ET = sb("ET", [P, 2, 512])
        OT = sb("OT", [P, 2, 2, TOK])
        Q_ps = ps("Q", [P, 512])
        K_ps = ps("K", [P, 512])
        V_ps = ps("V", [P, 512])
        S_ps = ps("S", [P, 2, 512])
        ET_ps = ps("ET", [P, 512])
        PV_ps = ps("PV", [P, 512])
        Y_ps = ps("Y", [P, 512])

        weights = sem("weights")
        setup = sem("setup")
        stats_done = sem("stats_done")
        var_ready = sem("var_ready")
        rstd_ready = sem("rstd_ready")
        xn_ready = sem("xn_ready")
        xnT_ps = sem("xnT_ps")
        xnT_ready = sem("xnT_ready")
        q_ps = sem("q_ps")
        k_ps = sem("k_ps")
        v_ps = sem("v_ps")
        pq_ready = sem("pq_ready")
        pk_ready = sem("pk_ready")
        rq_ready = sem("rq_ready")
        kt_ready = sem("kt_ready")
        qd_ready = sem("qd_ready")
        v_ready = sem("v_ready")
        s_ps = sem("s_ps")
        max_done = sem("max_done")
        d_ready = sem("d_ready")
        e_ready = sem("e_ready")
        sum_done = sem("sum_done")
        rsum_ready = sem("rsum_ready")
        en_ready = sem("en_ready")
        et_ps = sem("et_ps")
        et_ready = sem("et_ready")
        pv_ps = sem("pv_ps")
        ot_ready = sem("ot_ready")
        y_ps = sem("y_ps")
        x_done = sem("x_done")
        passed = sem("passed")
        N_WEIGHTS = 8

        block = ctx.enter_context(nc.Block())

        def item_at(blk, g):
            return blk + g // G, g % G

        def later(blk, least):
            return not isinstance(blk, int) or blk >= least

        @block.sync
        def _(sp):
            for dst, name in [(wq, "L1_attn_wq"), (wk, "L1_attn_wk"), (wv, "L1_attn_wv"), (wo, "L1_attn_wo"),
                              (bo, "L1_attn_bo"), (cos, "c_cos"), (sin, "c_sin"), (parity, "c_parity")]:
                sp.dma_start(dst[:], d[name]).then_inc(weights, 16)

        @block.gpsimd
        def _(pool):
            def power(nb):
                pool.wait_ge(var_ready, nb + 1)
                nc.gpsimd.tensor_tensor(rstd[:], var_eps[:], minus_half[:], ALU.pow).then_inc(rstd_ready, 1)

            def rotate(dst, src):
                nc.gpsimd.tensor_tensor(dst[:, 0, :], src[:, 0, 0, :], src[:, 1, 1, :], ALU.subtract)
                return nc.gpsimd.tensor_tensor(dst[:, 1, :], src[:, 1, 0, :], src[:, 0, 1, :], ALU.add)

            def rotate_k(blk, g):
                n_ = blk * G + g
                pool.wait_ge(pk_ready, n_ + 1)
                if later(n_, 2):
                    pool.wait_ge(s_ps, n_ - 1)
                rotate(KT[:, g % 2], PK).then_inc(kt_ready, 1)

            def rotate_q(blk, g):
                n_ = blk * G + g
                pool.wait_ge(pq_ready, n_ + 1)
                if later(n_, 1):
                    pool.wait_ge(qd_ready, n_)
                rotate(RQ, PQ).then_inc(rq_ready, 1)

            def normalise_e(blk, g):
                n_ = blk * G + g
                pool.wait_ge(rsum_ready, n_ + 1)
                e = E[:, g % 2, :].rearrange("p (r t) -> p r t", t=T)
                nc.gpsimd.tensor_tensor(e, e, rsum[:, g % 2, :].unsqueeze(2).broadcast_to([P, 2 * BB, T]), ALU.mult)\
                    .then_inc(en_ready, 1)

            def prologue():
                nc.gpsimd.memset(minus_half[:], -0.5).then_inc(setup, 1)
                nc.gpsimd.memset(V[:], 0.0).then_inc(setup, 1)
                pool.wait_ge(setup, 2)
                power(0)
                for g in range(3):
                    rotate_q(0, g)
                    rotate_k(0, g)
                    if g == 1:
                        normalise_e(0, 0)

            def step(blk, p, prev, nxt):
                for g in range(G):
                    if nxt and g == 0:
                        power(blk + 1)
                    if g + 1 < G or nxt:
                        normalise_e(*item_at(blk, g + 1))
                    if g + 3 < G or nxt:
                        rotate_q(*item_at(blk, g + 3))
                        rotate_k(*item_at(blk, g + 3))

            run_blocks(pool, NB, prologue, step, lambda: None)

        @block.tensor
        def _(pe):
            def transpose_x(nb, p):
                pe.wait_ge(xn_ready, nb + 1)
                if later(nb, 1):
                    pe.wait_ge(pq_ready, nb * G)
                for u in range(UB):
                    mm = nc.tensor.transpose(Q_ps[:, u * P:(u + 1) * P], xn[:, u, :], k.ident[:])
                mm.then_inc(xnT_ps, 1)

            def project_qk(blk, g, p):
                n_ = blk * G + g
                pe.wait_ge(xnT_ready, blk + 1)
                if later(n_, 1):
                    pe.wait_ge(pq_ready, n_)
                for a in range(2):
                    mm = nc.tensor.matmul(Q_ps[:, a * TOK:(a + 1) * TOK], wq[:, g, a, :], xnT[:, p, :], start=True, stop=True)
                mm.then_inc(q_ps, 1)
                if later(n_, 1):
                    pe.wait_ge(pk_ready, n_)
                for a in range(2):
                    mm = nc.tensor.matmul(K_ps[:, a * TOK:(a + 1) * TOK], wk[:, g, a, :], xnT[:, p, :], start=True, stop=True)
                mm.then_inc(k_ps, 1)

            def project_v(blk, g, p):
                n_ = blk * G + g
                if later(n_, 1):
                    pe.wait_ge(v_ready, n_)
                for u in range(UB):
                    mm = nc.tensor.matmul(V_ps[:, u * 256:(u + 1) * 256], xnT[:, p, u * P:(u + 1) * P], wv[:, g, :],
                                          start=True, stop=True)
                mm.then_inc(v_ps, 1)

            def scores(blk, g):
                n_ = blk * G + g
                pe.wait_ge(qd_ready, n_ + 1)
                pe.wait_ge(kt_ready, n_ + 1)
                if later(n_, 1):
                    pe.wait_ge(d_ready, n_)
                for pair in range(2):
                    rows = slice(64 * pair, 64 * pair + 64)
                    bank = S_ps[:, pair, 0:BB * T]
                    nc.tensor.matmul(bank, k.causal_queries[rows, :], k.causal_keys[rows, 0:BB * T], start=True, stop=False)
                    for b in range(BB):
                        for a in range(2):
                            mm = nc.tensor.matmul(bank[:, b * T:(b + 1) * T], QD[rows, g % 2, a, b, :],
                                                  KT[rows, g % 2, a, b * T:(b + 1) * T], start=False,
                                                  stop=(b == BB - 1 and a == 1))
                mm.then_inc(s_ps, 1)

            def transpose_e(blk, g):
                n_ = blk * G + g
                pe.wait_ge(en_ready, n_ + 1)
                if later(n_, 1):
                    pe.wait_ge(et_ready, n_)
                for b in range(BB):
                    mm = nc.tensor.transpose(ET_ps[:, b * P:(b + 1) * P], E[:, g % 2, b * P:(b + 1) * P], k.ident[:])
                mm.then_inc(et_ps, 1)

            def weigh_values(blk, g):
                n_ = blk * G + g
                pe.wait_ge(et_ready, n_ + 1)
                pe.wait_ge(v_ready, n_ + 1)
                if later(n_, 1):
                    pe.wait_ge(ot_ready, n_)
                for h in range(2):
                    for b in range(BB):
                        at = h * TOK + b * T
                        mm = nc.tensor.matmul(PV_ps[:, at:at + T], V[:, g % 2, b, h, :],
                                              ET[:, g % 2, b * P + h * T:b * P + (h + 1) * T], start=True, stop=True)
                mm.then_inc(pv_ps, 1)

            def project_o(blk, g):
                n_ = blk * G + g
                pe.wait_ge(ot_ready, n_ + 1)
                if g == 0 and later(blk, 1):
                    pe.wait_ge(x_done, blk)
                for u in range(UB):
                    out = Y_ps[:, u * P:(u + 1) * P]
                    for h in range(2):
                        mm = nc.tensor.matmul(out, OT[:, g % 2, h, u * P:(u + 1) * P], wo[:, g, h, :],
                                              start=(g == 0 and u == 0 and h == 0), stop=False, skip_group_check=True)
                    if g == G - 1:
                        mm = nc.tensor.matmul(out, k.ones_row[0:1, 0:P], bo[:], start=False, stop=(u == UB - 1),
                                              skip_group_check=True)
                mm.then_inc(y_ps, 1)

            def prologue():
                pe.wait_ge(weights, 16 * N_WEIGHTS)
                transpose_x(0, 0)
                for g in range(3):
                    project_qk(0, g, 0)
                    if g >= 1:
                        scores(0, g - 1)
                        project_v(0, g - 1, 0)
                transpose_e(0, 0)

            def step(blk, p, prev, nxt):
                for g in range(G):
                    if g + 3 < G or nxt:
                        nb, gg = item_at(blk, g + 3)
                        project_qk(nb, gg, p if g + 3 < G else 1 - p)
                    if g + 2 < G or nxt:
                        scores(*item_at(blk, g + 2))
                    if g + 1 < G or nxt:
                        transpose_e(*item_at(blk, g + 1))
                    if g + 2 < G or nxt:
                        nb, gg = item_at(blk, g + 2)
                        project_v(nb, gg, p if g + 2 < G else 1 - p)
                    weigh_values(blk, g)
                    if nxt and g == 0:
                        transpose_x(blk + 1, 1 - p)
                    if g > 0:
                        project_o(blk, g - 1)
                    elif prev:
                        project_o(blk - 1, G - 1)

            run_blocks(pe, NB, prologue, step, lambda: project_o(NB - 1, G - 1))

        @block.scalar
        def _(act):
            def evacuate_xT(nb, p):
                act.wait_ge(xnT_ps, nb + 1)
                if later(nb, 2):
                    act.wait_ge(v_ps, (nb - 1) * G)
                nc.scalar.activation(xnT[:, p, :], Q_ps[:, 0:TOK], ACT.Copy).then_inc(xnT_ready, 1)

            def spread_q(blk, g):
                n_ = blk * G + g
                act.wait_ge(rq_ready, n_ + 1)
                if later(n_, 2):
                    act.wait_ge(s_ps, n_ - 1)
                for h in range(2):
                    last = nc.scalar.activation(QD[:, g % 2, :, :, h * T:(h + 1) * T],
                                                RQ[:].rearrange("p a (b t) -> p a b t", t=T), ACT.Copy,
                                                scale=parity[:, h:h + 1])
                last.then_inc(qd_ready, 1)

            def evacuate_v(blk, g):
                n_ = blk * G + g
                act.wait_ge(v_ps, n_ + 1)
                if later(n_, 2):
                    act.wait_ge(pv_ps, n_ - 1)
                src = V_ps[:].rearrange("p (u q h e) -> p u q h e", u=UB, q=2, h=2)
                dst = V[:, g % 2].rearrange("p (u r) h (q e) -> p u r h q e", r=2, q=2)
                for r in range(2):
                    for q in range(2):
                        last = nc.scalar.activation(dst[64 * q:64 * q + 64, :, r, :, q, :],
                                                    src[64 * r:64 * r + 64, :, q, :, :], ACT.Copy)
                last.then_inc(v_ready, 1)

            def exponentials(blk, g):
                n_ = blk * G + g
                act.wait_ge(d_ready, n_ + 1)
                nc.scalar.activation(E[:, g % 2, :], E[:, g % 2, :], ACT.Exp, scale=SCALE).then_inc(e_ready, 1)

            def evacuate_e(blk, g):
                n_ = blk * G + g
                act.wait_ge(et_ps, n_ + 1)
                if later(n_, 2):
                    act.wait_ge(pv_ps, n_ - 1)
                nc.scalar.activation(ET[:, g % 2, :], ET_ps[:], ACT.Copy).then_inc(et_ready, 1)

            def evacuate_o(blk, g):
                n_ = blk * G + g
                act.wait_ge(pv_ps, n_ + 1)
                if later(n_, 2):
                    act.wait_ge(y_ps, n_ - 1)
                nc.scalar.activation(OT[:, g % 2].rearrange("p h t -> p (h t)"), PV_ps[:], ACT.Copy).then_inc(ot_ready, 1)

            def prologue():
                act.wait_ge(weights, 16 * N_WEIGHTS)
                act.wait_ge(setup, 2)
                evacuate_xT(0, 0)
                spread_q(0, 0)
                for g in range(1, 3):
                    exponentials(0, g - 1)
                    evacuate_v(0, g - 1)
                    spread_q(0, g)
                evacuate_e(0, 0)

            def step(blk, p, prev, nxt):
                for g in range(G):
                    if g + 1 < G or nxt:
                        evacuate_e(*item_at(blk, g + 1))
                    if g + 2 < G or nxt:
                        evacuate_v(*item_at(blk, g + 2))
                    evacuate_o(blk, g)
                    if nxt and g == 0:
                        evacuate_xT(blk + 1, 1 - p)
                    if g + 2 < G or nxt:
                        exponentials(*item_at(blk, g + 2))
                    if g + 3 < G or nxt:
                        spread_q(*item_at(blk, g + 3))

            run_blocks(act, NB, prologue, step, lambda: None)

        @block.vector
        def _(dve):
            def statistics(nb):
                for u in range(UB):
                    last = nc.vector.bn_stats(stats[:, u, :], k.X[:, nb * UB + u, :])
                last.then_inc(stats_done, 1)
                wait_here(dve, stats_done, nb * 2 + 1, passed)
                for u in range(UB):
                    last = nc.vector.bn_aggr(mv[:, u, :], stats[:, u, :])
                last.then_inc(stats_done, 1)
                dve.wait_ge(stats_done, nb * 2 + 2)
                nc.vector.tensor_scalar(var_eps[:], mv[:, :, 1], EPS, None, ALU.add).then_inc(var_ready, 1)

            def normalise(nb):
                dve.wait_ge(rstd_ready, nb + 1)
                if later(nb, 1):
                    dve.wait_ge(xnT_ps, nb)
                for u in range(UB):
                    last = nc.vector.tensor_scalar(xn[:, u, :], k.X[:, nb * UB + u, :], mv[:, u, 0:1], rstd[:, u:u + 1],
                                                   ALU.subtract, ALU.mult)
                last.then_inc(xn_ready, 1)

            def products(bank, dst):
                src = bank[:].rearrange("p (r t) -> p r t", t=T)
                for i, table in enumerate((cos, sin)):
                    last = nc.vector.tensor_tensor(dst[:, i].rearrange("p a (b t) -> p (a b) t", t=T), src,
                                                   table[:].unsqueeze(1).broadcast_to([P, 2 * BB, T]), ALU.mult)
                return last

            def products_qk(blk, g):
                n_ = blk * G + g
                dve.wait_ge(q_ps, n_ + 1)
                if later(n_, 1):
                    dve.wait_ge(rq_ready, n_)
                products(Q_ps, PQ).then_inc(pq_ready, 1)
                dve.wait_ge(k_ps, n_ + 1)
                if later(n_, 1):
                    dve.wait_ge(kt_ready, n_)
                products(K_ps, PK).then_inc(pk_ready, 1)

            def subtract_max(blk, g):
                n_ = blk * G + g
                dve.wait_ge(s_ps, n_ + 1)
                src = S_ps[:, :, 0:BB * T].rearrange("p q (b t) -> p q b t", t=T)
                nc.vector.tensor_reduce(row_max[:], src, AX.X, ALU.max).then_inc(max_done, 1)
                dve.wait_ge(max_done, n_ + 1)
                if later(n_, 2):
                    dve.wait_ge(et_ps, n_ - 1)
                dst = E[:, g % 2, :].rearrange("p (b q t) -> p q b t", b=BB, q=2)
                nc.vector.tensor_tensor(dst, src, row_max[:].unsqueeze(3).broadcast_to([P, 2, BB, T]), ALU.subtract)\
                    .then_inc(d_ready, 1)

            def sums(blk, g):
                n_ = blk * G + g
                dve.wait_ge(e_ready, n_ + 1)
                nc.vector.tensor_reduce(row_sum[:], E[:, g % 2, :].rearrange("p (r t) -> p r t", t=T), AX.X, ALU.add)\
                    .then_inc(sum_done, 1)
                dve.wait_ge(sum_done, n_ + 1)
                if later(n_, 2):
                    dve.wait_ge(en_ready, n_ - 1)
                nc.vector.reciprocal(rsum[:, g % 2, :], row_sum[:]).then_inc(rsum_ready, 1)

            def add_residual(blk):
                dve.wait_ge(y_ps, (blk + 1) * G)
                x = k.X[:, bass.ds(blk * UB, UB), :]
                nc.vector.tensor_tensor(x, Y_ps[:, 0:TOK].rearrange("p (u c) -> p u c", u=UB), x, ALU.add)\
                    .then_inc(x_done, 1)

            def prologue():
                dve.wait_ge(weights, 16 * N_WEIGHTS)
                statistics(0)
                normalise(0)
                products_qk(0, 0)
                for g in range(1, 3):
                    products_qk(0, g)
                    subtract_max(0, g - 1)
                    if g == 1:
                        sums(0, 0)

            def step(blk, p, prev, nxt):
                for g in range(G):
                    if nxt and g == 0:
                        statistics(blk + 1)
                    if g + 1 < G or nxt:
                        sums(*item_at(blk, g + 1))
                    if nxt and g == 0:
                        normalise(blk + 1)
                    if g + 3 < G or nxt:
                        products_qk(*item_at(blk, g + 3))
                    if g + 2 < G or nxt:
                        subtract_max(*item_at(blk, g + 2))
                    if prev and g == 1:
                        add_residual(blk - 1)

            run_blocks(dve, NB, prologue, step, lambda: add_residual(NB - 1))


def masked_attention_phase(nc, k):
    UB = 4
    NB = NU // UB
    BB = 2 * UB
    TOK = UB * P
    n = "x1"
    d = k.d
    with ExitStack() as ctx:
        def sb(name, shape, dt=F32):
            return ctx.enter_context(nc.sbuf_tensor(f"{n}_{name}", shape, dt))

        def ps(name, shape):
            return ctx.enter_context(nc.psum_tensor(f"{n}_{name}_ps", shape, F32))

        def sem(name):
            return nc.alloc_semaphore(f"{n}_{name}")

        ctxT = sb("ctxT", [P, 2, TOK])
        ctxK = sb("ctxK", [T, 2, BB, C])
        mask = sb("mask", [2, NU * T], I32)
        pad = sb("pad", [2, NU * T], BF16)
        stats = sb("stats", [P, UB, 6])
        mv = sb("mv", [P, UB, 2])
        var_eps = sb("var_eps", [P, UB])
        minus_half = sb("minus_half", [P, UB])
        rstd = sb("rstd", [P, UB])
        xn = sb("xn", [P, UB, C])
        xnT = sb("xnT", [P, TOK])
        row_max = sb("row_max", [P, UB])
        row_sum = sb("row_sum", [P, UB])
        rsum = sb("rsum", [P, UB])
        E = sb("E", [P, UB, T])
        ET = sb("ET", [T, TOK])
        xT_ps = ps("xT", [P, 512])
        S_ps = [ps(f"S{i}", [P, 512]) for i in range(2)]
        ET_ps = ps("ET", [P, 512])
        PV_ps = ps("PV", [P, 512])

        loaded = sem("loaded")
        ctx_in = [sem("ctx_in0"), sem("ctx_in1")]
        setup = sem("setup")
        stats_done = sem("stats_done")
        var_ready = sem("var_ready")
        rstd_ready = sem("rstd_ready")
        xn_ready = sem("xn_ready")
        xnT_ps = sem("xnT_ps")
        xnT_ready = sem("xnT_ready")
        s_ps = sem("s_ps")
        softmax_done = sem("softmax_done")
        d_ready = sem("d_ready")
        e_ready = sem("e_ready")
        en_ready = sem("en_ready")
        et_ps = sem("et_ps")
        et_ready = sem("et_ready")
        pv_ps = sem("pv_ps")
        x_done = sem("x_done")
        passed = sem("passed")

        block = ctx.enter_context(nc.Block())

        def later(blk, least):
            return not isinstance(blk, int) or blk >= least

        @block.sync
        def _(sp):
            sp.dma_start(mask[:], d["mask"]).then_inc(loaded, 16)

            def load_ctx(nb, p):
                if later(nb, 2):
                    wait_here(sp, pv_ps, nb - 1, passed)
                sp.dma_start(ctxT[:, p, :], d["ctxT"][:, bass.ds(nb * TOK, TOK)]).then_inc(ctx_in[p], 16)
                sp.dma_start(ctxK[:, p, :, :], d["ctxK"][:, bass.ds(nb * BB, BB), :]).then_inc(ctx_in[p], 16)

            def step(blk, p, prev, nxt):
                if nxt:
                    load_ctx(blk + 1, 1 - p)

            run_blocks(sp, NB, lambda: load_ctx(0, 0), step, lambda: None)

        @block.gpsimd
        def _(pool):
            nc.gpsimd.memset(minus_half[:], -0.5).then_inc(setup, 1)
            pool.wait_ge(setup, 1)

            def power(nb):
                pool.wait_ge(var_ready, nb + 1)
                nc.gpsimd.tensor_tensor(rstd[:], var_eps[:], minus_half[:], ALU.pow).then_inc(rstd_ready, 1)

            def step(blk, p, prev, nxt):
                if nxt:
                    power(blk + 1)

            run_blocks(pool, NB, lambda: power(0), step, lambda: None)

        @block.tensor
        def _(pe):
            def front(nb, p):
                pe.wait_ge(xn_ready, nb + 1)
                if later(nb, 1):
                    pe.wait_ge(xnT_ready, nb)
                for u in range(UB):
                    mm = nc.tensor.transpose(xT_ps[:, u * P:(u + 1) * P], xn[:, u, :], k.ident[:])
                mm.then_inc(xnT_ps, 1)
                bank = S_ps[p]
                if later(nb, 2):
                    pe.wait_ge(d_ready, nb - 1)
                nc.tensor.matmul(bank[:, 0:UB * T], k.causal_queries[0:T, :], k.causal_keys[0:T, 0:UB * T],
                                 start=True, stop=False)
                nc.tensor.matmul(bank[:, 0:UB * T], k.of_batch[:], pad[:, bass.ds(nb * UB * T, UB * T)],
                                 start=False, stop=False)
                pe.wait_ge(ctx_in[p], (nb // 2 + 1) * 32)
                pe.wait_ge(xnT_ready, nb + 1)
                for b in range(BB):
                    half = slice(64 * (b % 2), 64 * (b % 2) + 64)
                    mm = nc.tensor.matmul(bank[half, (b // 2) * T:(b // 2 + 1) * T], xnT[:, b * T:(b + 1) * T],
                                          ctxT[:, p, b * T:(b + 1) * T], start=False, stop=(b >= BB - 2))
                mm.then_inc(s_ps, 1)

            def back(blk, p):
                if later(blk, 1):
                    pe.wait_ge(et_ready, blk)
                wait_here(pe, en_ready, blk + 1, passed)
                for u in range(UB):
                    mm = nc.tensor.transpose(ET_ps[0:T, u * P:(u + 1) * P], E[:, u, :], k.ident[:])
                mm.then_inc(et_ps, 1)
                if later(blk, 1):
                    pe.wait_ge(x_done, blk)
                wait_here(pe, et_ready, blk + 1, passed)
                for b in range(BB):
                    half = slice(64 * (b % 2), 64 * (b % 2) + 64)
                    mm = nc.tensor.matmul(PV_ps[half, (b // 2) * C:(b // 2 + 1) * C], ET[:, b * T:(b + 1) * T],
                                          ctxK[:, p, b, :], start=True, stop=True)
                mm.then_inc(pv_ps, 1)

            def prologue():
                pe.wait_ge(softmax_done, 1)
                front(0, 0)

            def step(blk, p, prev, nxt):
                if nxt:
                    front(blk + 1, 1 - p)
                back(blk, p)

            run_blocks(pe, NB, prologue, step, lambda: None)

        @block.scalar
        def _(act):
            def evacuate_xT(nb):
                act.wait_ge(xnT_ps, nb + 1)
                if later(nb, 1):
                    act.wait_ge(s_ps, nb)
                nc.scalar.activation(xnT[:], xT_ps[:], ACT.Copy).then_inc(xnT_ready, 1)

            def step(blk, p, prev, nxt):
                if nxt:
                    evacuate_xT(blk + 1)
                act.wait_ge(d_ready, blk + 1)
                nc.scalar.activation(E[:], E[:], ACT.Exp, scale=float(C) ** -0.5).then_inc(e_ready, 1)
                act.wait_ge(et_ps, blk + 1)
                if later(blk, 1):
                    act.wait_ge(pv_ps, blk)
                nc.scalar.activation(ET[:], ET_ps[0:T, :], ACT.Copy).then_inc(et_ready, 1)

            run_blocks(act, NB, lambda: evacuate_xT(0), step, lambda: None)

        @block.vector
        def _(dve):
            def front(nb):
                for u in range(UB):
                    last = nc.vector.bn_stats(stats[:, u, :], k.X[:, nb * UB + u, :])
                last.then_inc(stats_done, 1)
                wait_here(dve, stats_done, nb * 2 + 1, passed)
                for u in range(UB):
                    last = nc.vector.bn_aggr(mv[:, u, :], stats[:, u, :])
                last.then_inc(stats_done, 1)
                dve.wait_ge(stats_done, nb * 2 + 2)
                nc.vector.tensor_scalar(var_eps[:], mv[:, :, 1], EPS, None, ALU.add).then_inc(var_ready, 1)
                dve.wait_ge(rstd_ready, nb + 1)
                if later(nb, 1):
                    dve.wait_ge(xnT_ps, nb)
                for u in range(UB):
                    last = nc.vector.tensor_scalar(xn[:, u, :], k.X[:, nb * UB + u, :], mv[:, u, 0:1], rstd[:, u:u + 1],
                                                   ALU.subtract, ALU.mult)
                last.then_inc(xn_ready, 1)

            def back(blk, p):
                done = blk * 3 + 1
                dve.wait_ge(s_ps, blk + 1)
                src = S_ps[p][:, 0:UB * T].rearrange("p (u t) -> p u t", t=T)
                nc.vector.tensor_reduce(row_max[:], src, AX.X, ALU.max).then_inc(softmax_done, 1)
                dve.wait_ge(softmax_done, done + 1)
                if later(blk, 1):
                    dve.wait_ge(et_ps, blk)
                nc.vector.tensor_tensor(E[:], src, row_max[:].unsqueeze(2).broadcast_to([P, UB, T]), ALU.subtract)\
                    .then_inc(d_ready, 1)
                dve.wait_ge(e_ready, blk + 1)
                nc.vector.tensor_reduce(row_sum[:], E[:], AX.X, ALU.add).then_inc(softmax_done, 1)
                dve.wait_ge(softmax_done, done + 2)
                nc.vector.reciprocal(rsum[:], row_sum[:]).then_inc(softmax_done, 1)
                dve.wait_ge(softmax_done, done + 3)
                nc.vector.tensor_tensor(E[:], E[:], rsum[:].unsqueeze(2).broadcast_to([P, UB, T]), ALU.mult)\
                    .then_inc(en_ready, 1)
                dve.wait_ge(pv_ps, blk + 1)
                x = k.X[:, bass.ds(blk * UB, UB), :]
                nc.vector.tensor_tensor(x, PV_ps[:].rearrange("p (u c) -> p u c", u=UB), x, ALU.add).then_inc(x_done, 1)

            def prologue():
                dve.wait_ge(loaded, 16)
                nc.vector.tensor_scalar(pad[:], mask[:], 0.0, NEG, ALU.is_equal, ALU.mult).then_inc(softmax_done, 1)
                front(0)

            def step(blk, p, prev, nxt):
                if nxt:
                    front(blk + 1)
                back(blk, p)

            run_blocks(dve, NB, prologue, step, lambda: None)


MAGIC = 1.5 * 2.0 ** 23
QMAX = 127.0


def quantised_ffn_phase(nc, k):
    UB = 4
    NB = NU // UB
    TOK = UB * P
    I = k.d["L1_ffn_w_down"].shape[1]
    NC = (I + P - 1) // P
    ROWS = [min(P, I - c * P) for c in range(NC)]
    n = "q1"
    d = k.d
    with ExitStack() as ctx:
        def sb(name, shape, dt=F32):
            return ctx.enter_context(nc.sbuf_tensor(f"{n}_{name}", shape, dt))

        def ps(name, shape, dt=F32):
            return ctx.enter_context(nc.psum_tensor(f"{n}_{name}_ps", shape, dt))

        def sem(name):
            return nc.alloc_semaphore(f"{n}_{name}")

        w_rows = [sb("w_gate", [P, NC, C]), sb("w_up", [P, NC, C])]
        w_down = sb("w_down", [P, I])
        w_q = sb("w_q", [P, 2, NC, C], BF16)
        w_t = sb("w_t", [P, NC * C])
        wd_q = sb("wd_q", [P, I], BF16)
        wT = sb("wT", [P, 2, NC * P], BF16)
        wdT = sb("wdT", [P, NC, C], BF16)
        w_max = sb("w_max", [P, 2 * NC + 1])
        w_scale = sb("w_scale", [P, 2 * NC + 1])
        w_inv = sb("w_inv", [P, 2 * NC + 1])
        clip = sb("clip", [P, 2])
        sig = sb("sig", [P, 2])
        stats = sb("stats", [P, UB, 6])
        mv = sb("mv", [P, UB, 2])
        var_eps = sb("var_eps", [P, UB])
        minus_half = sb("minus_half", [P, UB])
        rstd = sb("rstd", [P, UB])
        XN = sb("XN", [P, NU, C])
        x_max = sb("x_max", [P, NB])
        h_max = sb("h_max", [P, NB * NC])
        all_max = sb("all_max", [P, 4])
        scale = sb("scale", [P, 2])
        inv = sb("inv", [P, 2])
        gu_scale = sb("gu_scale", [P, 2 * NC])
        out_scale = sb("out_scale", [P, 1])
        out_row = sb("out_row", [P, C])
        tq = sb("tq", [P, 2, NC * TOK])
        xq = sb("xq", [P, 2, TOK], BF16)
        xqT = sb("xqT", [P, 2, TOK], BF16)
        act_g = sb("act_g", [P, 2, TOK])
        HT = sb("HT", [P, NC, NB * TOK])
        hq = sb("hq", [P, 2, NC * TOK], BF16)
        y = sb("y", [P, 2, TOK])
        T_ps = ps("T", [P, 1024], BF16)
        G_ps = [ps(f"G{i}", [P, 512]) for i in range(2)]
        U_ps = [ps(f"U{i}", [P, 512]) for i in range(2)]
        D_ps = [ps(f"D{i}", [P, 512]) for i in range(2)]

        loaded = sem("loaded")
        setup = sem("setup")
        stats_done = sem("stats_done")
        var_ready = sem("var_ready")
        rstd_ready = sem("rstd_ready")
        xn_done = sem("xn_done")
        xmax_done = sem("xmax_done")
        wprep = sem("wprep")
        wq_ready = sem("wq_ready")
        wt_ps = sem("wt_ps")
        wt_ready = sem("wt_ready")
        local_max = sem("local_max")
        whole_max = sem("whole_max")
        sig_steps = sem("sig_steps")
        scale_steps = sem("scale_steps")
        gu_ready = sem("gu_ready")
        tq_done = sem("tq_done")
        xq_ready = sem("xq_ready")
        xqT_ps = sem("xqT_ps")
        xqT_ready = sem("xqT_ready")
        g_ps = sem("g_ps")
        u_ps = sem("u_ps")
        silu_ready = sem("silu_ready")
        h_done = sem("h_done")
        hmax_done = sem("hmax_done")
        row_ps = sem("row_ps")
        row_ready = sem("row_ready")
        tq2_done = sem("tq2_done")
        tq2_clipped = sem("tq2_clipped")
        hq_ready = sem("hq_ready")
        d_ps = sem("d_ps")
        y_scaled = sem("y_scaled")
        y_ready = sem("y_ready")
        stored = [sem("stored0"), sem("stored1")]
        passed = sem("passed")
        out_d = k.out.rearrange("(u r) t d -> (r t) u d", r=2)

        block = ctx.enter_context(nc.Block())

        def later(blk, least):
            return not isinstance(blk, int) or blk >= least

        def pairs(eng, body):
            body(0, 0)
            body(1, 1)
            with eng.Fori(1, NB // 2) as i:
                body(i * 2, 0)
                body(i * 2 + 1, 1)

        @block.sync
        def _(sp):
            sp.wait_ge(setup, 3)
            for w, name in zip(w_rows, ("L1_ffn_w_gate", "L1_ffn_w_up")):
                for c in range(NC):
                    sp.dma_start(w[0:ROWS[c], c, :], d[name][c * P:c * P + ROWS[c], :]).then_inc(loaded, 16)
            sp.dma_start(w_down[:], d["L1_ffn_w_down"]).then_inc(loaded, 16)
            sp.dma_start(clip[:], d["L1_ffn_clips"]).then_inc(loaded, 16)

            def store(blk, p):
                wait_here(sp, y_ready, blk + 1, passed)
                sp.dma_start(out_d[:, bass.ds(blk * UB, UB), :], y[:, p, :].rearrange("p (u c) -> p u c", c=C))\
                    .then_inc(stored[p], 16)

            pairs(sp, store)
            for q in stored:
                sp.wait_ge(q, 16 * NB // 2)

        @block.gpsimd
        def _(pool):
            for w in w_rows:
                nc.gpsimd.memset(w[:], 1.0).then_inc(setup, 1)
            nc.gpsimd.memset(h_max[:], 0.0).then_inc(setup, 1)
            nc.gpsimd.memset(minus_half[:], -0.5).then_inc(setup, 1)
            pool.wait_ge(setup, 4)
            nc.gpsimd.memset(HT[ROWS[-1]:P, NC - 1, :], 0.0).then_inc(setup, 1)
            pool.wait_ge(setup, 5)
            with pool.Fori(0, NB) as nb:
                pool.wait_ge(var_ready, nb + 1)
                nc.gpsimd.tensor_tensor(rstd[:], var_eps[:], minus_half[:], ALU.pow).then_inc(rstd_ready, 1)
            for i in range(2):
                pool.wait_ge(local_max, i + 1)
                nc.gpsimd.partition_all_reduce(all_max[:, 2 * i + 1:2 * i + 2], all_max[:, 2 * i:2 * i + 1], P,
                                               bass.bass_isa.ReduceOp.max).then_inc(whole_max, 1)

        @block.tensor
        def _(pe):
            pe.wait_ge(wq_ready, 1)
            for c in range(2 * NC):
                if c >= 4:
                    pe.wait_ge(wt_ready, 1)
                mm = nc.tensor.transpose(T_ps[:, (c % 4) * P:(c % 4 + 1) * P], w_q[:, c // NC, c % NC, :], k.identb[:])
                if c == 3:
                    mm.then_inc(wt_ps, 1)
            mm.then_inc(wt_ps, 1)
            pe.wait_ge(wt_ready, 2)
            for c in range(NC):
                mm = nc.tensor.transpose(T_ps[0:ROWS[c], c * P:(c + 1) * P], wd_q[:, c * P:c * P + ROWS[c]], k.identb[:])
            mm.then_inc(wt_ps, 1)
            pe.wait_ge(wt_ready, 3)

            def up(blk, p):
                pe.wait_ge(xq_ready, blk + 1)
                if later(blk, 1):
                    pe.wait_ge(xqT_ready, blk)
                for u in range(UB):
                    mm = nc.tensor.transpose(T_ps[:, u * P:(u + 1) * P], xq[:, p, u * P:(u + 1) * P], k.identb[:])
                mm.then_inc(xqT_ps, 1)
                pe.wait_ge(xqT_ready, blk + 1)
                for c in range(NC):
                    n_ = blk * NC + c
                    r = (p * NC + c) % 2
                    if later(n_, 2):
                        pe.wait_ge(h_done, n_ - 1)
                    nc.tensor.matmul(G_ps[r][0:ROWS[c], :], wT[:, 0, c * P:c * P + ROWS[c]], xqT[:, p, :],
                                     start=True, stop=True).then_inc(g_ps, 1)
                    nc.tensor.matmul(U_ps[r][0:ROWS[c], :], wT[:, 1, c * P:c * P + ROWS[c]], xqT[:, p, :],
                                     start=True, stop=True).then_inc(u_ps, 1)

            pairs(pe, up)
            pe.wait_ge(scale_steps, 5)
            nc.tensor.matmul(D_ps[0][:, 0:C], out_scale[:, 0:1].broadcast_to([P, P]), k.ident[:], start=True, stop=True)\
                .then_inc(row_ps, 1)
            pe.wait_ge(row_ready, 1)

            def down(blk, p):
                pe.wait_ge(hq_ready, blk + 1)
                if later(blk, 2):
                    pe.wait_ge(y_scaled, blk - 1)
                for u in range(UB):
                    for c in range(NC):
                        mm = nc.tensor.matmul(D_ps[p][:, u * C:(u + 1) * C],
                                              hq[0:ROWS[c], p, c * TOK + u * P:c * TOK + (u + 1) * P],
                                              wdT[0:ROWS[c], c, :], start=(c == 0), stop=(c == NC - 1))
                mm.then_inc(d_ps, 1)

            pairs(pe, down)

        @block.scalar
        def _(act):
            act.wait_ge(loaded, 16 * (2 * NC + 2))
            nc.scalar.activation(sig[:], clip[:], ACT.Exp, scale=-1.0).then_inc(sig_steps, 1)
            act.wait_ge(wt_ps, 1)
            nc.scalar.activation(wT[:].rearrange("p g n -> p (g n)")[:, 0:4 * P], T_ps[:, 0:4 * P], ACT.Copy).then_inc(wt_ready, 1)
            act.wait_ge(wt_ps, 2)
            nc.scalar.activation(wT[:].rearrange("p g n -> p (g n)")[:, 4 * P:6 * P], T_ps[:, 0:2 * P], ACT.Copy).then_inc(wt_ready, 1)
            act.wait_ge(wt_ps, 3)
            for c in range(NC):
                last = nc.scalar.activation(wdT[0:ROWS[c], c, :], T_ps[0:ROWS[c], c * P:(c + 1) * P], ACT.Copy)
            last.then_inc(wt_ready, 1)
            act.wait_ge(gu_ready, 1)

            def up(blk, p):
                act.wait_ge(tq_done, blk * 2 + 2)
                if later(blk, 2):
                    act.wait_ge(xqT_ps, blk - 1)
                nc.scalar.activation(xq[:, p, :], tq[:, p, 0:TOK], ACT.Copy, bias=-MAGIC).then_inc(xq_ready, 1)
                act.wait_ge(xqT_ps, blk + 1)
                if later(blk, 2):
                    act.wait_ge(u_ps, (blk - 1) * NC)
                nc.scalar.activation(xqT[:, p, :], T_ps[:, 0:TOK], ACT.Copy).then_inc(xqT_ready, 1)
                for c in range(NC):
                    n_ = blk * NC + c
                    r = (p * NC + c) % 2
                    act.wait_ge(g_ps, n_ + 1)
                    if later(n_, 2):
                        act.wait_ge(h_done, n_ - 1)
                    nc.scalar.activation(act_g[0:ROWS[c], r, :], G_ps[r][0:ROWS[c], :], ACT.Silu,
                                         scale=gu_scale[0:ROWS[c], c:c + 1]).then_inc(silu_ready, 1)

            pairs(act, up)

            def down(blk, p):
                act.wait_ge(tq2_clipped, blk + 1)
                if later(blk, 2):
                    act.wait_ge(d_ps, blk - 1)
                nc.scalar.activation(hq[:, p, :], tq[:, p, :], ACT.Copy, bias=-MAGIC).then_inc(hq_ready, 1)

            act.wait_ge(scale_steps, 5)
            pairs(act, down)

        @block.vector
        def _(dve):
            step_no = [0]

            def chained(ins):
                step_no[0] += 1
                ins.then_inc(wprep, 1)
                dve.wait_ge(wprep, step_no[0])

            dve.wait_ge(loaded, 16 * (2 * NC + 2))
            for g in range(2):
                nc.vector.tensor_reduce(w_max[:, g * NC:(g + 1) * NC], w_rows[g][:], AX.X, ALU.max, apply_absolute_value=True)
            chained(nc.vector.tensor_reduce(w_max[:, 2 * NC:2 * NC + 1], w_down[:], AX.X, ALU.max, apply_absolute_value=True))
            chained(nc.vector.tensor_scalar(w_scale[:], w_max[:], 1.0 / QMAX, None, ALU.mult))
            chained(nc.vector.reciprocal(w_inv[:], w_scale[:]))
            for g in range(2):
                t3 = w_t[:].rearrange("p (c n) -> p c n", n=C)
                chained(nc.vector.tensor_tensor(t3, w_rows[g][:], w_inv[:, g * NC:(g + 1) * NC].unsqueeze(2)
                                                .broadcast_to([P, NC, C]), ALU.mult))
                chained(nc.vector.tensor_scalar(w_t[:], w_t[:], MAGIC, MAGIC - QMAX - 1.0, ALU.add, ALU.max))
                chained(nc.vector.tensor_scalar(w_q[:, g].rearrange("p c n -> p (c n)"), w_t[:], MAGIC + QMAX, MAGIC,
                                                ALU.min, ALU.subtract))
            chained(nc.vector.tensor_scalar(w_t[:, 0:I], w_down[:], w_inv[:, 2 * NC:2 * NC + 1], MAGIC, ALU.mult, ALU.add))
            chained(nc.vector.tensor_scalar(w_t[:, 0:I], w_t[:, 0:I], MAGIC - QMAX - 1.0, MAGIC + QMAX, ALU.max, ALU.min))
            nc.vector.tensor_scalar(wd_q[:], w_t[:, 0:I], MAGIC, None, ALU.subtract).then_inc(wq_ready, 1)
            dve.wait_ge(sig_steps, 1)
            chained(nc.vector.tensor_scalar(sig[:], sig[:], 1.0, None, ALU.add))
            chained(nc.vector.reciprocal(sig[:], sig[:]))

            dve.wait_ge(setup, 5)
            with dve.Fori(0, NB) as nb:
                for u in range(UB):
                    last = nc.vector.bn_stats(stats[:, u, :], k.X[:, nb * UB + u, :])
                last.then_inc(stats_done, 1)
                wait_here(dve, stats_done, nb * 2 + 1, passed)
                for u in range(UB):
                    last = nc.vector.bn_aggr(mv[:, u, :], stats[:, u, :])
                last.then_inc(stats_done, 1)
                dve.wait_ge(stats_done, nb * 2 + 2)
                nc.vector.tensor_scalar(var_eps[:], mv[:, :, 1], EPS, None, ALU.add).then_inc(var_ready, 1)
                dve.wait_ge(rstd_ready, nb + 1)
                for u in range(UB):
                    last = nc.vector.tensor_scalar(XN[:, nb * UB + u, :], k.X[:, nb * UB + u, :], mv[:, u, 0:1],
                                                   rstd[:, u:u + 1], ALU.subtract, ALU.mult)
                last.then_inc(xn_done, 1)
                dve.wait_ge(xn_done, nb + 1)
                nc.vector.tensor_reduce(x_max[:, bass.ds(nb, 1)], XN[:, bass.ds(nb * UB, UB), :].rearrange("p u c -> p (u c)"),
                                        AX.X, ALU.max, apply_absolute_value=True).then_inc(xmax_done, 1)
            dve.wait_ge(xmax_done, NB)

            def find_scale(i, maxima):
                nc.vector.tensor_reduce(all_max[:, 2 * i:2 * i + 1], maxima[:], AX.X, ALU.max).then_inc(local_max, 1)
                dve.wait_ge(whole_max, i + 1)
                nc.vector.tensor_scalar(scale[:, i:i + 1], all_max[:, 2 * i + 1:2 * i + 2], sig[:, i:i + 1], 1.0 / QMAX,
                                        ALU.mult, ALU.mult).then_inc(scale_steps, 1)
                dve.wait_ge(scale_steps, 2 * i + 1)
                nc.vector.reciprocal(inv[:, i:i + 1], scale[:, i:i + 1]).then_inc(scale_steps, 1)
                dve.wait_ge(scale_steps, 2 * i + 2)

            find_scale(0, x_max)
            nc.vector.tensor_scalar(gu_scale[:], w_scale[:, 0:2 * NC], scale[:, 0:1], None, ALU.mult)\
                .then_inc(gu_ready, 1)
            dve.wait_ge(gu_ready, 1)

            def quantise_x(blk, p):
                if later(blk, 2):
                    dve.wait_ge(xq_ready, blk - 1)
                t = tq[:, p, 0:TOK]
                nc.vector.tensor_scalar(t, XN[:, bass.ds(blk * UB, UB), :].rearrange("p u c -> p (u c)"), inv[:, 0:1], MAGIC,
                                        ALU.mult, ALU.add).then_inc(tq_done, 1)
                dve.wait_ge(tq_done, blk * 2 + 1)
                nc.vector.tensor_scalar(t, t, MAGIC - QMAX - 1.0, MAGIC + QMAX, ALU.max, ALU.min).then_inc(tq_done, 1)

            def hidden(blk, p):
                for c in range(NC):
                    n_ = blk * NC + c
                    r = (p * NC + c) % 2
                    h = HT[0:ROWS[c], c, bass.ds(blk * TOK, TOK)]
                    dve.wait_ge(u_ps, n_ + 1)
                    dve.wait_ge(silu_ready, n_ + 1)
                    nc.vector.scalar_tensor_tensor(out=h, in0=U_ps[r][0:ROWS[c], :],
                                                   scalar=gu_scale[0:ROWS[c], NC + c:NC + c + 1],
                                                   in1=act_g[0:ROWS[c], r, :], op0=ALU.mult, op1=ALU.mult).then_inc(h_done, 1)
                    dve.wait_ge(h_done, n_ + 1)
                    nc.vector.tensor_reduce(h_max[0:ROWS[c], bass.ds(n_, 1)], h, AX.X, ALU.max, apply_absolute_value=True)\
                        .then_inc(hmax_done, 1)

            def up(blk, p):
                quantise_x(blk + 1, 1 - p)
                hidden(blk, p)

            quantise_x(0, 0)
            up(0, 0)
            up(1, 1)
            with dve.Fori(1, NB // 2 - 1) as i:
                up(i * 2, 0)
                up(i * 2 + 1, 1)
            up(NB - 2, 0)
            hidden(NB - 1, 1)
            dve.wait_ge(hmax_done, NB * NC)
            find_scale(1, h_max)
            nc.vector.tensor_scalar(out_scale[:], w_scale[:, 2 * NC:2 * NC + 1], scale[:, 1:2], None, ALU.mult)\
                .then_inc(scale_steps, 1)
            dve.wait_ge(scale_steps, 5)
            dve.wait_ge(row_ps, 1)
            nc.vector.tensor_copy(out_row[:], D_ps[0][:, 0:C]).then_inc(row_ready, 1)
            dve.wait_ge(row_ready, 1)

            def quantise_h(blk, p):
                t = tq[:, p, :]
                if later(blk, 2):
                    dve.wait_ge(hq_ready, blk - 1)
                for c in range(NC):
                    last = nc.vector.tensor_scalar(tq[:, p, c * TOK:(c + 1) * TOK], HT[:, c, bass.ds(blk * TOK, TOK)],
                                                   inv[:, 1:2], MAGIC, ALU.mult, ALU.add)
                last.then_inc(tq2_done, 1)
                dve.wait_ge(tq2_done, blk + 1)
                nc.vector.tensor_scalar(t, t, MAGIC - QMAX - 1.0, MAGIC + QMAX, ALU.max, ALU.min).then_inc(tq2_clipped, 1)

            def output(blk, p):
                dve.wait_ge(d_ps, blk + 1)
                if later(blk, 2):
                    dve.wait_ge(stored[p], (blk // 2) * 16)
                y3 = y[:, p, :].rearrange("p (u c) -> p u c", c=C)
                nc.vector.tensor_tensor(y3, D_ps[p][:].rearrange("p (u c) -> p u c", c=C),
                                        out_row[:].unsqueeze(1).broadcast_to([P, UB, C]), ALU.mult).then_inc(y_scaled, 1)
                dve.wait_ge(y_scaled, blk + 1)
                nc.vector.tensor_tensor(y3, y3, k.X[:, bass.ds(blk * UB, UB), :], ALU.add).then_inc(y_ready, 1)

            def down(blk, p):
                quantise_h(blk + 1, 1 - p)
                output(blk, p)

            quantise_h(0, 0)
            down(0, 0)
            down(1, 1)
            with dve.Fori(1, NB // 2 - 1) as i:
                down(i * 2, 0)
                down(i * 2 + 1, 1)
            down(NB - 2, 0)
            output(NB - 1, 1)


def store_phase(nc, k):
    with ExitStack() as ctx:
        stored = nc.alloc_semaphore("stored")
        block = ctx.enter_context(nc.Block())

        @block.sync
        def _(sp):
            sp.dma_start(k.out.rearrange("(u r) t d -> (r t) u d", r=2), k.X[:]).then_inc(stored, 16)
            sp.wait_ge(stored, 16)


TEST = ""


def decoder_kernel(nc, dram, out):
    k = Core()
    k.d = dram
    k.out = out
    with ExitStack() as ctx:
        def sb(name, shape, dt=F32):
            return ctx.enter_context(nc.sbuf_tensor(name, shape, dt))

        k.X = sb("X", [P, NU, C])
        k.ident = sb("ident", [P, P])
        k.ones_row = sb("ones_row", [1, 512])
        k.causal_queries = sb("causal_queries", [P, P], BF16)
        k.causal_keys = sb("causal_keys", [P, 512], BF16)
        k.identb = sb("identb", [P, P], BF16)
        k.of_batch = sb("of_batch", [2, P], BF16)
        zeros = sb("zeros", [P, 512])
        n_slots = (2 * NU + 8) * P
        k.slot_rows = nc.dram_tensor("slot_rows", (n_slots, C), F32, kind="Internal").ap()
        k.slot_out = nc.dram_tensor("slot_out", (n_slots, C), F32, kind="Internal").ap()
        k.zeroed = nc.alloc_semaphore("zeroed")
        k.n_zeroed = n_slots * C // (P * 512)
        run_phase(nc, load_phase, k, zeros)
        phases = TEST or "abcdef"
        if "a" in phases: run_phase(nc, narrow_attention_phase, k, cross=False)
        if "b" in phases: run_phase(nc, narrow_attention_phase, k, cross=True)
        if "c" in phases: mixture_phases(nc, k)
        if "d" in phases: run_phase(nc, wide_attention_phase, k)
        if "e" in phases: run_phase(nc, masked_attention_phase, k)
        if "f" in phases:
            run_phase(nc, quantised_ffn_phase, k)
        else:
            run_phase(nc, store_phase, k)


def constants():
    t = np.arange(T)
    inv_freq = np.float32(1.0) / np.float32(10000.0) ** (np.arange(0, 64, 2, dtype=np.float32) / np.float32(64))
    angle = inv_freq[:, None] * t.astype(np.float32)[None, :]
    return {
        "c_ident": np.eye(P, dtype=np.float32),
        "c_upper": np.triu(np.ones((P, P), np.float32), 1),
        "c_ones": np.ones((P, P), np.float32),
        "c_rank": np.tile(8.0 - np.arange(8, dtype=np.float32), (P, 1)),
        "c_tile_no": np.arange(2 * NU + 8, dtype=np.float32)[None, :],
        "c_of_batch": (np.arange(P)[None, :] // T == np.arange(2)[:, None]).astype(np.float32),
        "c_ones_row": np.ones((1, 512), np.float32),
        "c_causal_queries": np.tile(np.eye(T), (2, 2)).astype(np.float32),
        "c_causal_keys": np.tile(np.where(t[None, :] > t[:, None], NEG, 0.0), (2, 8)).astype(np.float32),
        "c_cos": np.tile(np.cos(angle), (4, 1)).astype(np.float32),
        "c_sin": np.tile(np.sin(angle), (4, 1)).astype(np.float32),
        "c_parity": (np.arange(P)[:, None] // 32 % 2 == np.arange(2)[None, :]).astype(np.float32),
    }


def laid_out(inputs):
    a = {name: np.asarray(v) for name, v in inputs.items()}
    f = {"x": a["x"], "ctxT": a["ctx_1024"].reshape(B * T, C).T,
         "ctxK": a["ctx_1024"].transpose(1, 0, 2), "mask": a["mask_BxS2_ik1"].reshape(NU, 2, T).transpose(1, 0, 2).reshape(2, NU * T)}
    for n in ("w_gate", "w_up", "w_down"):
        f[f"L1_ffn_{n}"] = a[f"L1_ffn_{n}"]
    f["L1_ffn_clips"] = np.broadcast_to(np.stack([a["L1_ffn_clip_x"], a["L1_ffn_clip_down"]], 1), (P, 2))
    def woT(w):
        return w.T.reshape(H // 2, 2, D0, C).transpose(0, 2, 1, 3).reshape(64, 2, C)
    qkv = a["L0_attn_W_qkv"]
    for i, n in enumerate("qkv"):
        f[f"L0_attn_w{n}T"] = qkv[i * C:(i + 1) * C].T
        f[f"L0_xattn_w{n}T"] = a[f"L0_xattn_W{n}"].T
    f["L0_attn_woT"] = woT(a["L0_attn_W_proj"])
    f["L0_xattn_woT"] = woT(a["L0_xattn_Wo"])
    for n in ("bq", "bk"):
        f[f"L0_xattn_{n}"] = a[f"L0_xattn_{n}"].reshape(C, 1)
    for n in ("bv", "bo"):
        f[f"L0_xattn_{n}"] = a[f"L0_xattn_{n}"].reshape(1, C)
    f["L0_xattn_temp"] = np.repeat(a["L0_xattn_temperature"].reshape(H), D0).reshape(C, 1)
    f["L0_ffn_router_w"] = a["L0_ffn_router_w"].T
    f["L0_ffn_router_b"] = a["L0_ffn_router_b"].reshape(1, 8)
    for n in ("gate_w", "up_w"):
        f[f"L0_ffn_{n}"] = a[f"L0_ffn_{n}"].transpose(2, 0, 1).reshape(C, -1)
    f["L0_ffn_down_w"] = a["L0_ffn_down_w"].reshape(8, C, 4, P).transpose(3, 0, 2, 1).reshape(P, -1)
    for n in "qk":
        f[f"L1_attn_w{n}"] = a[f"L1_attn_W{n}"].reshape(C, 4, 4, 32, 2).transpose(0, 1, 4, 2, 3).reshape(C, 4, 2, P)
    f["L1_attn_wv"] = a["L1_attn_Wv"].reshape(C, 4, 256)
    f["L1_attn_wo"] = a["L1_attn_Wo"].reshape(4, 2, 2, 64, C).transpose(1, 3, 0, 2, 4).reshape(P, 4, 2, C)
    f["L1_attn_bo"] = a["L1_attn_bo"].reshape(1, C)
    return f


def kernel(**inputs):
    import concourse.bacc as _bacc
    from concourse.bass_utils import run_bass_kernel_spmd as _run

    nc = _bacc.Bacc("TRN2", target_bir_lowering=False, num_devices=1)
    arrays, dram = {}, {}
    for name, a in {**laid_out(inputs), **constants()}.items():
        a = np.ascontiguousarray(a)
        arrays[f"in_{name}"] = a
        dram[name] = nc.dram_tensor(f"in_{name}", a.shape, mybir.dt.from_np(a.dtype), kind="ExternalInput").ap()
    out = nc.dram_tensor("out_x", (B, T, C), F32, kind="ExternalOutput").ap()
    decoder_kernel(nc, dram, out)
    r = _run(nc, [arrays], core_ids=[0])
    return r.results[0]["out_x"]
```

```python
from contextlib import ExitStack

import numpy as np

import concourse.bass as bass
from concourse import mybir

P = 128
B, T, C = 64, 64, 128
NU = B * T // P
H = 16
D0 = C // H
EPS = 1e-5
NEG = -1e30

F32 = mybir.dt.float32
BF16 = mybir.dt.bfloat16
I32 = mybir.dt.int32
ALU = mybir.AluOpType
ACT = mybir.ActivationFunctionType
AX = mybir.AxisListType


class Core:
    pass


def run_blocks(eng, n_blocks, prologue, step, epilogue):
    prologue()
    step(0, 0, prev=False, nxt=True)
    with eng.Fori(0, n_blocks // 2 - 1) as i:
        step(i * 2 + 1, 1, prev=True, nxt=True)
        step(i * 2 + 2, 0, prev=True, nxt=True)
    step(n_blocks - 1, (n_blocks - 1) % 2, prev=True, nxt=False)
    epilogue()


def wait_here(eng, sem, value, passed):
    eng.wait_ge(sem, value)
    eng.sem_inc(passed, 1)


def run_phase(nc, phase, *args, **named):
    with nc.cleanup_on_exit():
        phase(nc, *args, **named)


def load_phase(nc, k):
    with ExitStack() as ctx:
        loaded = nc.alloc_semaphore("shared_loaded")
        staged_in = nc.alloc_semaphore("staged_in")
        narrowed = [(dst, ctx.enter_context(nc.sbuf_tensor(f"staged_{name}", list(dst.shape), F32)), name)
                    for dst, name in ((k.causal_keys, "c_causal_keys"), (k.causal_queries, "c_causal_queries"),
                                      (k.identb, "c_ident"), (k.of_batch, "c_of_batch"))]
        block = ctx.enter_context(nc.Block())

        @block.sync
        def _(sp):
            sp.dma_start(k.X[:], k.d["x"].rearrange("(u r) t d -> (r t) u d", r=2)).then_inc(loaded, 16)
            sp.dma_start(k.ident[:], k.d["c_ident"]).then_inc(loaded, 16)
            sp.dma_start(k.ones_row[:], k.d["c_ones_row"]).then_inc(loaded, 16)
            for _, staged, name in narrowed:
                sp.dma_start(staged[:], k.d[name]).then_inc(staged_in, 16)
            sp.wait_ge(loaded, 3 * 16)

        @block.vector
        def _(dve):
            dve.wait_ge(staged_in, 16 * len(narrowed))
            for dst, staged, _ in narrowed:
                nc.vector.tensor_copy(dst[:], staged[:])


def narrow_attention_phase(nc, k, cross):
    UB = 4
    NB = NU // UB
    BB = 2 * UB
    TOK = UB * P
    HALF = H // 2
    PAIRS = HALF // 2
    QUADS = H // 4
    ROWS = 2 * H // 2
    LAG = 2
    QW = 2 * 2 * D0
    n = "x0" if cross else "a0"
    d = k.d
    with ExitStack() as ctx:
        def sb(name, shape, dt=F32):
            return ctx.enter_context(nc.sbuf_tensor(f"{n}_{name}", shape, dt))

        def ps(name, shape):
            return ctx.enter_context(nc.psum_tensor(f"{n}_{name}_ps", shape, F32))

        def sem(name):
            return nc.alloc_semaphore(f"{n}_{name}")

        wq = sb("wq", [P, C])
        wk = sb("wk", [P, C])
        wv = sb("wv", [P, C])
        wo = sb("wo", [P, C])
        wo_of = sb("wo_of", [P, 2, C])
        parity = sb("parity", [P, 2])
        bq = sb("bq", [P, 1])
        bk = sb("bk", [P, 1])
        bv = sb("bv", [1, C])
        bo = sb("bo", [1, C])
        temp = sb("temp", [P, 1])
        qscale = sb("qscale", [P, 1])
        of_head = sb("of_head", [P, HALF])
        q_factor = sb("q_factor", [P, HALF])
        q_offset = sb("q_offset", [P, HALF])
        ctxT = sb("ctxT", [P, 2, TOK])
        stats = sb("stats", [P, UB, 6])
        mv = sb("mv", [P, UB, 2])
        var_eps = sb("var_eps", [P, UB])
        minus_half = sb("minus_half", [P, UB])
        rstd = sb("rstd", [P, UB])
        xn = sb("xn", [P, UB, C])
        xnT = sb("xnT", [P, TOK])
        QX = sb("QX", [P, 2, BB, HALF * T])
        KT = sb("KT", [P, 2, TOK])
        V = sb("V", [P, 2, BB, QUADS * (P + QW)])
        row_max = sb("row_max", [P, 2, ROWS])
        E = sb("E", [P, 2, ROWS * T])
        ET = sb("ET", [P, 2, ROWS * T])
        row_sum = sb("row_sum", [P, ROWS])
        rsum = sb("rsum", [P, 2, ROWS])
        OT = sb("OT", [P, 2, 2, TOK])
        S_ps = [ps(f"S{i}", [P, 2, 512]) for i in range(2)]
        ET_ps = ps("ET", [P, 2 * 512])
        PV_ps = ps("PV", [P, 512])
        G_ps = ps("G", [P, 512])

        weights = sem("weights")
        ctx_in = [sem("ctx_in0"), sem("ctx_in1")]
        setup = sem("setup")
        wo_split = sem("wo_split")
        stats_done = sem("stats_done")
        max_done = sem("max_done")
        sum_done = sem("sum_done")
        q_tables = sem("q_tables")
        var_ready = sem("var_ready")
        rstd_ready = sem("rstd_ready")
        xn_ready = sem("xn_ready")
        xnT_ps = sem("xnT_ps")
        xnT_ready = sem("xnT_ready")
        q_ps = sem("q_ps")
        k_ps = sem("k_ps")
        v_ps = sem("v_ps")
        qx_ready = sem("qx_ready")
        kT_ready = sem("kT_ready")
        v_ready = sem("v_ready")
        s_ps = sem("s_ps")
        d_ready = sem("d_ready")
        e_ready = sem("e_ready")
        rsum_ready = sem("rsum_ready")
        en_ready = sem("en_ready")
        et_ps = sem("et_ps")
        et_ready = sem("et_ready")
        pv_ps = sem("pv_ps")
        ot_ready = sem("ot_ready")
        y_ps = sem("y_ps")
        x_done = sem("x_done")
        passed = sem("passed")
        N_WEIGHTS = 11 if cross else 6
        Q_TABLES = 4 if cross else 0

        block = ctx.enter_context(nc.Block())

        def later(number, least):
            return not isinstance(number, int) or number >= least

        def ahead(blk, u, p, by):
            return (blk, u + by, p) if u + by < UB else (blk + 1, u + by - UB, 1 - p)

        @block.sync
        def _(sp):
            w = "L0_xattn_" if cross else "L0_attn_"
            names = [(wq, w + "wqT"), (wk, w + "wkT"), (wv, w + "wvT"), (wo, w + "woT"), (of_head, "c_of_head"),
                     (parity, "c_narrow_parity")]
            if cross:
                names += [(t, w + name) for t, name in ((bq, "bq"), (bk, "bk"), (bv, "bv"), (bo, "bo"), (temp, "temp"))]
            for dst, name in names:
                sp.dma_start(dst[:], d[name]).then_inc(weights, 16)

            def load_ctx(nb, p):
                if cross:
                    sp.dma_start(ctxT[:, p, :], d["ctxT"][:, bass.ds(nb * TOK, TOK)]).then_inc(ctx_in[p], 16)

            def step(blk, p, prev, nxt):
                if nxt and cross:
                    if prev:
                        wait_here(sp, v_ps, blk, passed)
                    load_ctx(blk + 1, 1 - p)

            run_blocks(sp, NB, lambda: load_ctx(0, 0), step, lambda: None)

        @block.gpsimd
        def _(pool):
            def power(nb):
                pool.wait_ge(var_ready, nb + 1)
                nc.gpsimd.tensor_tensor(rstd[:], var_eps[:], minus_half[:], ALU.pow).then_inc(rstd_ready, 1)

            def normalise_e(blk, u):
                pool.wait_ge(rsum_ready, blk * UB + u + 1)
                e = E[:, u % 2, :].rearrange("p (r t) -> p r t", t=T)
                nc.gpsimd.tensor_tensor(e, e, rsum[:, u % 2, :].unsqueeze(2).broadcast_to([P, ROWS, T]), ALU.mult)\
                    .then_inc(en_ready, 1)

            def prologue():
                nc.gpsimd.memset(minus_half[:], -0.5).then_inc(setup, 1)
                pool.wait_ge(setup, 1)
                power(0)
                pool.wait_ge(rstd_ready, 1)
                nc.gpsimd.memset(V[:], 0.0).then_inc(setup, 1)
                pool.wait_ge(setup, 2)
                for u in range(LAG):
                    normalise_e(0, u)

            def step(blk, p, prev, nxt):
                for u in range(UB):
                    if u == 0 and nxt:
                        power(blk + 1)
                    if u + LAG < UB or nxt:
                        normalise_e(*ahead(blk, u, p, LAG)[:2])

            run_blocks(pool, NB, prologue, step, lambda: None)

        @block.tensor
        def _(pe):
            def transpose_x(nb):
                pe.wait_ge(xn_ready, nb + 1)
                if later(nb, 1):
                    pe.wait_ge(v_ready, nb)
                for u in range(UB):
                    mm = nc.tensor.transpose(G_ps[:, u * P:(u + 1) * P], xn[:, u, :], k.ident[:])
                mm.then_inc(xnT_ps, 1)

            def project_q(nb):
                pe.wait_ge(xnT_ready, nb + 1)
                nc.tensor.matmul(G_ps[:], wq[:], xnT[:], start=True, stop=True).then_inc(q_ps, 1)

            def project_k(nb, p):
                if cross:
                    pe.wait_ge(ctx_in[p], (nb // 2 + 1) * 16)
                pe.wait_ge(qx_ready, nb + 1)
                src = ctxT[:, p, :] if cross else xnT[:]
                nc.tensor.matmul(G_ps[:], wk[:], src, start=True, stop=True).then_inc(k_ps, 1)

            def project_v(nb, p):
                pe.wait_ge(kT_ready, nb + 1)
                for u in range(UB):
                    src = ctxT[:, p, u * P:(u + 1) * P] if cross else xnT[:, u * P:(u + 1) * P]
                    out = G_ps[:, u * P:(u + 1) * P]
                    mm = nc.tensor.matmul(out, src, wv[:], start=True, stop=not cross)
                    if cross:
                        mm = nc.tensor.matmul(out, k.ones_row[0:1, 0:P], bv[:], start=False, stop=True)
                mm.then_inc(v_ps, 1)

            def scores(blk, u, p):
                n_ = blk * UB + u
                if u == 0:
                    pe.wait_ge(qx_ready, blk + 1)
                    pe.wait_ge(kT_ready, blk + 1)
                if later(blk, 1) or u >= 2:
                    pe.wait_ge(d_ready, n_ - 1)
                rows = [slice(64 * r, 64 * r + 64) for r in range(2)]
                bank = [S_ps[u % 2][:, r, :] for r in range(2)]
                if not cross:
                    for r in range(2):
                        nc.tensor.matmul(bank[r], k.causal_queries[rows[r], :], k.causal_keys[rows[r], :],
                                         start=True, stop=False)
                for b in range(2):
                    for j in range(PAIRS):
                        for r in range(2):
                            at = (b * PAIRS + j) * T
                            token = (2 * u + b) * T
                            mm = nc.tensor.matmul(bank[r][:, at:at + T],
                                                  QX[rows[r], p, 2 * u + b, 2 * j * T:2 * (j + 1) * T],
                                                  KT[rows[r], p, token:token + T], start=cross,
                                                  stop=cross or (b == 1 and j == PAIRS - 1))
                mm.then_inc(s_ps, 1)

            def transpose_e(blk, u):
                n_ = blk * UB + u
                pe.wait_ge(en_ready, n_ + 1)
                if later(n_, 1):
                    pe.wait_ge(et_ready, n_)
                for b in range(2):
                    for j in range(QUADS):
                        at = (b * QUADS + j) * P
                        src = (j // 2 * 2 + b) * 256 + j % 2 * P
                        mm = nc.tensor.transpose(ET_ps[:, at:at + P], E[:, u % 2, src:src + P], k.ident[:])
                mm.then_inc(et_ps, 1)

            def weigh_values(blk, u, p):
                n_ = blk * UB + u
                if u == 0:
                    pe.wait_ge(v_ready, blk + 1)
                pe.wait_ge(et_ready, n_ + 1)
                if later(n_, 1):
                    pe.wait_ge(ot_ready, n_)
                for b in range(2):
                    for j in range(QUADS):
                        at = b * QUADS + j
                        mm = nc.tensor.matmul(PV_ps[:, b * P:(b + 1) * P], V[:, p, 2 * u + b, j * P:(j + 1) * P],
                                              ET[:, u % 2, at * P:(at + 1) * P], start=(j == 0), stop=(j == QUADS - 1))
                mm.then_inc(pv_ps, 1)

            def project_o(blk, p):
                pe.wait_ge(ot_ready, (blk + 1) * UB)
                for u in range(UB):
                    out = G_ps[:, u * P:(u + 1) * P]
                    for h in range(2):
                        mm = nc.tensor.matmul(out, OT[:, p, h, u * P:(u + 1) * P], wo_of[:, h, :], start=(h == 0),
                                              stop=(h == 1 and not cross))
                    if cross:
                        mm = nc.tensor.matmul(out, k.ones_row[0:1, 0:P], bo[:], start=False, stop=True)
                mm.then_inc(y_ps, 1)

            def prologue():
                pe.wait_ge(weights, 16 * N_WEIGHTS)
                pe.wait_ge(wo_split, 2)
                transpose_x(0)
                project_q(0)
                project_k(0, 0)
                project_v(0, 0)
                for u in range(LAG):
                    scores(0, u, 0)
                transpose_e(0, 0)

            def step(blk, p, prev, nxt):
                for u in range(UB):
                    if u + LAG < UB or nxt:
                        scores(*ahead(blk, u, p, LAG))
                    if u == 3 and prev:
                        pe.wait_ge(x_done, blk)
                    if u + 1 < UB or nxt:
                        transpose_e(*ahead(blk, u, p, 1)[:2])
                    if u == 0 and nxt:
                        transpose_x(blk + 1)
                    if u == 1 and nxt:
                        project_k(blk + 1, 1 - p)
                    weigh_values(blk, u, p)
                    if u == 0 and nxt:
                        project_q(blk + 1)
                    if u == 1 and nxt:
                        project_v(blk + 1, 1 - p)
                    if u == 2 and prev:
                        if nxt:
                            pe.wait_ge(v_ready, blk + 2)
                        project_o(blk - 1, 1 - p)

            def epilogue():
                project_o(NB - 1, (NB - 1) % 2)

            run_blocks(pe, NB, prologue, step, epilogue)

        @block.scalar
        def _(act):
            def evacuate_xT(nb):
                act.wait_ge(xnT_ps, nb + 1)
                if later(nb, 1):
                    act.wait_ge(v_ps, nb)
                nc.scalar.activation(xnT[:], G_ps[:], ACT.Copy).then_inc(xnT_ready, 1)

            def spread_q(nb, p):
                act.wait_ge(q_ps, nb + 1)
                if later(nb, 2):
                    act.wait_ge(s_ps, (nb - 1) * UB)
                src = G_ps[:].rearrange("c (b t) -> c b t", t=T)
                for h in range(HALF):
                    dst = QX[:, p, :, h * T:(h + 1) * T]
                    if cross:
                        last = nc.scalar.activation(dst, src, ACT.Identity, bias=q_offset[:, h:h + 1],
                                                    scale=q_factor[:, h:h + 1])
                    else:
                        last = nc.scalar.activation(dst, src, ACT.Copy, scale=of_head[:, h:h + 1])
                last.then_inc(qx_ready, 1)

            def evacuate_k(nb, p):
                act.wait_ge(k_ps, nb + 1)
                if later(nb, 2):
                    act.wait_ge(s_ps, (nb - 1) * UB)
                if cross:
                    nc.scalar.activation(KT[:, p, :], G_ps[:], ACT.Identity, bias=bk[:, 0:1]).then_inc(kT_ready, 1)
                else:
                    nc.scalar.activation(KT[:, p, :], G_ps[:], ACT.Copy).then_inc(kT_ready, 1)

            def evacuate_v(nb, p):
                act.wait_ge(v_ps, nb + 1)
                if later(nb, 2):
                    act.wait_ge(pv_ps, (nb - 1) * UB)
                src = G_ps[:].rearrange("p (u j r e) -> p u j r e", u=UB, j=QUADS, r=2)
                dst = V[:, p].rearrange("p (u r) (j e) -> p u r j e", r=2, j=QUADS)
                for r in range(2):
                    for j in range(2):
                        last = nc.scalar.activation(dst[64 * j:64 * j + 64, :, r, :, 2 * D0 * j:2 * D0 * (j + 1)],
                                                    src[64 * r:64 * r + 64, :, :, j, :], ACT.Copy)
                last.then_inc(v_ready, 1)

            def exponentials(blk, u):
                act.wait_ge(d_ready, blk * UB + u + 1)
                nc.scalar.activation(E[:, u % 2, :], E[:, u % 2, :], ACT.Exp,
                                     scale=1.0 if cross else float(D0) ** -0.5).then_inc(e_ready, 1)

            def evacuate_e(blk, u):
                n_ = blk * UB + u
                act.wait_ge(et_ps, n_ + 1)
                if later(blk, 1) or u >= 2:
                    act.wait_ge(pv_ps, n_ - 1)
                nc.scalar.activation(ET[:, u % 2, :], ET_ps[:], ACT.Copy).then_inc(et_ready, 1)

            def prologue():
                act.wait_ge(weights, 16 * N_WEIGHTS)
                act.wait_ge(setup, 2)
                if cross:
                    act.wait_ge(q_tables, Q_TABLES)
                evacuate_xT(0)
                spread_q(0, 0)
                evacuate_k(0, 0)
                evacuate_v(0, 0)
                for u in range(LAG):
                    exponentials(0, u)
                evacuate_e(0, 0)

            def step(blk, p, prev, nxt):
                for u in range(UB):
                    if u + 1 < UB or nxt:
                        evacuate_e(*ahead(blk, u, p, 1)[:2])
                    if u == 0 and nxt:
                        evacuate_xT(blk + 1)
                    if u == 1 and nxt:
                        evacuate_k(blk + 1, 1 - p)
                    if u + LAG < UB or nxt:
                        exponentials(*ahead(blk, u, p, LAG)[:2])
                    if u == 0 and nxt:
                        spread_q(blk + 1, 1 - p)
                    if u == 1 and nxt:
                        evacuate_v(blk + 1, 1 - p)

            run_blocks(act, NB, prologue, step, lambda: None)

        @block.vector
        def _(dve):
            def statistics(nb):
                for u in range(UB):
                    last = nc.vector.bn_stats(stats[:, u, :], k.X[:, nb * UB + u, :])
                last.then_inc(stats_done, 1)
                wait_here(dve, stats_done, nb * 2 + 1, passed)
                for u in range(UB):
                    last = nc.vector.bn_aggr(mv[:, u, :], stats[:, u, :])
                last.then_inc(stats_done, 1)
                dve.wait_ge(stats_done, nb * 2 + 2)
                nc.vector.tensor_scalar(var_eps[:], mv[:, :, 1], EPS, None, ALU.add).then_inc(var_ready, 1)

            def normalise(nb):
                dve.wait_ge(rstd_ready, nb + 1)
                if later(nb, 1):
                    dve.wait_ge(xnT_ps, nb)
                for u in range(UB):
                    last = nc.vector.tensor_scalar(xn[:, u, :], k.X[:, nb * UB + u, :], mv[:, u, 0:1], rstd[:, u:u + 1],
                                                   ALU.subtract, ALU.mult)
                last.then_inc(xn_ready, 1)

            def subtract_max(blk, u):
                n_ = blk * UB + u
                dve.wait_ge(s_ps, n_ + 1)
                src = S_ps[u % 2][:].rearrange("p r (j t) -> p (r j) t", t=T)
                nc.vector.tensor_reduce(row_max[:, u % 2, :], src, AX.X, ALU.max).then_inc(max_done, 1)
                dve.wait_ge(max_done, n_ + 1)
                if later(blk, 1) or u >= 2:
                    dve.wait_ge(et_ps, n_ - 1)
                nc.vector.tensor_tensor(E[:, u % 2, :].rearrange("p (j t) -> p j t", t=T), src,
                                        row_max[:, u % 2, :].unsqueeze(2).broadcast_to([P, ROWS, T]),
                                        ALU.subtract).then_inc(d_ready, 1)

            def sums(blk, u):
                n_ = blk * UB + u
                dve.wait_ge(e_ready, n_ + 1)
                nc.vector.tensor_reduce(row_sum[:], E[:, u % 2, :].rearrange("p (r t) -> p r t", t=T), AX.X, ALU.add)\
                    .then_inc(sum_done, 1)
                dve.wait_ge(sum_done, n_ + 1)
                if later(blk, 1) or u >= 2:
                    dve.wait_ge(en_ready, n_ - 1)
                nc.vector.reciprocal(rsum[:, u % 2, :], row_sum[:]).then_inc(rsum_ready, 1)

            def evacuate_o(blk, u, p):
                dve.wait_ge(pv_ps, blk * UB + u + 1)
                dst = OT[:, p, :, u * P:(u + 1) * P].rearrange("c h (b t) -> c b h t", b=2)
                src = PV_ps[:, 0:2 * P].rearrange("c (b h t) -> c b h t", b=2, h=2)
                nc.vector.tensor_copy(dst, src).then_inc(ot_ready, 1)

            def add_residual(blk):
                dve.wait_ge(y_ps, blk + 1)
                x = k.X[:, bass.ds(blk * UB, UB), :]
                nc.vector.tensor_tensor(x, G_ps[:].rearrange("p (u c) -> p u c", u=UB), x, ALU.add).then_inc(x_done, 1)

            def prologue():
                statistics(0)
                normalise(0)
                dve.wait_ge(weights, 16 * N_WEIGHTS)
                if cross:
                    nc.vector.reciprocal(temp[:], temp[:]).then_inc(q_tables, 1)
                    dve.wait_ge(q_tables, 1)
                    nc.vector.tensor_scalar(qscale[:], temp[:], float(D0) ** -0.5, None, ALU.mult).then_inc(q_tables, 1)
                    dve.wait_ge(q_tables, 2)
                    nc.vector.tensor_scalar(q_factor[:], of_head[:], qscale[:, 0:1], None, ALU.mult).then_inc(q_tables, 1)
                    dve.wait_ge(q_tables, 3)
                    nc.vector.tensor_scalar(q_offset[:], q_factor[:], bq[:, 0:1], None, ALU.mult).then_inc(q_tables, 1)
                for h in range(2):
                    nc.vector.tensor_scalar(wo_of[:, h, :], wo[:], parity[:, h:h + 1], None, ALU.mult).then_inc(wo_split, 1)
                for u in range(LAG):
                    subtract_max(0, u)
                    sums(0, u)

            def step(blk, p, prev, nxt):
                for u in range(UB):
                    if u == 0 and nxt:
                        statistics(blk + 1)
                        normalise(blk + 1)
                    if u == 3 and prev:
                        add_residual(blk - 1)
                    if u + LAG < UB or nxt:
                        subtract_max(*ahead(blk, u, p, LAG)[:2])
                        sums(*ahead(blk, u, p, LAG)[:2])
                    evacuate_o(blk, u, p)

            run_blocks(dve, NB, prologue, step, lambda: add_residual(NB - 1))


def mixture_phases(nc, k):
    NE = 8
    F = 512
    FC = F // P
    NT = 2 * NU + NE
    d = k.d
    with ExitStack() as ctx:
        def sb(name, shape, dt=F32):
            return ctx.enter_context(nc.sbuf_tensor(f"m0_{name}", shape, dt))

        LG = sb("LG", [P, NU, NE])
        experts = sb("experts", [1, NT], I32)
        tokens = sb("tokens", [P, NT], I32)
        gate_w = sb("gate_w", [P, NE * F])
        up_w = sb("up_w", [P, NE * F])
        down_w = sb("down_w", [P, NE * F])
        w_loaded = nc.alloc_semaphore("m0_w_loaded")
        run_phase(nc, router_phase, k, LG, gate_w, up_w, down_w, w_loaded)
        run_phase(nc, plan_phase, k, LG, experts, tokens)
        run_phase(nc, expert_phase, k, experts, tokens, gate_w, up_w, down_w, w_loaded, NT)


def router_phase(nc, k, LG, gate_w, up_w, down_w, w_loaded):
    UB = 4
    NB = NU // UB
    NE = 8
    d = k.d
    with ExitStack() as ctx:
        def sb(name, shape, dt=F32):
            return ctx.enter_context(nc.sbuf_tensor(f"r_{name}", shape, dt))

        def sem(name):
            return nc.alloc_semaphore(f"r_{name}")

        rw = sb("rw", [P, NE])
        rb = sb("rb", [1, NE])
        stats = sb("stats", [P, UB, 6])
        mv = sb("mv", [P, UB, 2])
        var_eps = sb("var_eps", [P, UB])
        minus_half = sb("minus_half", [P, UB])
        rstd = sb("rstd", [P, UB])
        xn = sb("xn", [P, 2, UB, C])
        xnT = sb("xnT", [P, 2, UB * P])
        T_ps = [ctx.enter_context(nc.psum_tensor(f"r_T{i}", [P, 512], F32)) for i in range(2)]
        L_ps = [ctx.enter_context(nc.psum_tensor(f"r_L{i}", [P, 512], F32)) for i in range(2)]

        loaded = sem("loaded")
        setup = sem("setup")
        stats_done = sem("stats_done")
        var_ready = sem("var_ready")
        rstd_ready = sem("rstd_ready")
        xn_ready = sem("xn_ready")
        kept = [sem("kept0"), sem("kept1")]
        xnT_ps = sem("xnT_ps")
        xnT_ready = sem("xnT_ready")
        l_ps = sem("l_ps")
        l_ready = sem("l_ready")
        passed = sem("passed")
        block = ctx.enter_context(nc.Block())

        def later(blk, least):
            return not isinstance(blk, int) or blk >= least

        def pairs(eng, body):
            body(0, 0)
            body(1, 1)
            with eng.Fori(1, NB // 2) as i:
                body(i * 2, 0)
                body(i * 2 + 1, 1)

        @block.sync
        def _(sp):
            sp.dma_start(rw[:], d["L0_ffn_router_w"]).then_inc(loaded, 16)
            sp.dma_start(rb[:], d["L0_ffn_router_b"]).then_inc(loaded, 16)
            for w, name in ((gate_w, "gate_w"), (up_w, "up_w"), (down_w, "down_w")):
                sp.dma_start(w[:], d[f"L0_ffn_{name}"]).then_inc(w_loaded, 16)

            def body(blk, p):
                wait_here(sp, xn_ready, blk + 1, passed)
                rows = k.xn_rows[bass.ds(blk * (UB * P), UB * P), :].rearrange("(u t) c -> t u c", t=P)
                sp.dma_start(rows, xn[:, p]).then_inc(kept[p], 16)

            pairs(sp, body)
            for q in kept:
                sp.wait_ge(q, NB // 2 * 16)

        @block.gpsimd
        def _(pool):
            nc.gpsimd.memset(minus_half[:], -0.5).then_inc(setup, 1)
            pool.wait_ge(setup, 1)

            def body(blk, p):
                pool.wait_ge(var_ready, blk + 1)
                nc.gpsimd.tensor_tensor(rstd[:], var_eps[:], minus_half[:], ALU.pow).then_inc(rstd_ready, 1)

            pairs(pool, body)

        @block.tensor
        def _(pe):
            pe.wait_ge(loaded, 32)

            def logits(blk, p):
                pe.wait_ge(xnT_ready, blk + 1)
                if later(blk, 2):
                    pe.wait_ge(l_ready, blk - 1)
                for u in range(UB):
                    out = L_ps[p][:, u * NE:(u + 1) * NE]
                    nc.tensor.matmul(out, xnT[:, p, u * P:(u + 1) * P], rw[:], start=True, stop=False)
                    mm = nc.tensor.matmul(out, k.ones_row[0:1, 0:P], rb[:], start=False, stop=True)
                mm.then_inc(l_ps, 1)

            def body(blk, p):
                pe.wait_ge(xn_ready, blk + 1)
                if later(blk, 2):
                    pe.wait_ge(xnT_ready, blk - 1)
                for u in range(UB):
                    mm = nc.tensor.transpose(T_ps[p][:, u * P:(u + 1) * P], xn[:, p, u, :], k.ident[:])
                mm.then_inc(xnT_ps, 1)
                logits(blk, p)

            pairs(pe, body)

        @block.scalar
        def _(act):
            def body(blk, p):
                act.wait_ge(xnT_ps, blk + 1)
                if later(blk, 2):
                    act.wait_ge(l_ps, blk - 1)
                nc.scalar.activation(xnT[:, p, :], T_ps[p][:], ACT.Copy).then_inc(xnT_ready, 1)
                act.wait_ge(l_ps, blk + 1)
                nc.scalar.activation(LG[:, bass.ds(blk * UB, UB), :], L_ps[p][:, 0:UB * NE].rearrange("p (u e) -> p u e", e=NE),
                                     ACT.Copy).then_inc(l_ready, 1)

            pairs(act, body)

        @block.vector
        def _(dve):
            def body(blk, p):
                for u in range(UB):
                    last = nc.vector.bn_stats(stats[:, u, :], k.X[:, blk * UB + u, :])
                last.then_inc(stats_done, 1)
                wait_here(dve, stats_done, blk * 2 + 1, passed)
                for u in range(UB):
                    last = nc.vector.bn_aggr(mv[:, u, :], stats[:, u, :])
                last.then_inc(stats_done, 1)
                dve.wait_ge(stats_done, blk * 2 + 2)
                nc.vector.tensor_scalar(var_eps[:], mv[:, :, 1], EPS, None, ALU.add).then_inc(var_ready, 1)
                dve.wait_ge(rstd_ready, blk + 1)
                if later(blk, 2):
                    dve.wait_ge(xnT_ps, blk - 1)
                    dve.wait_ge(kept[p], blk // 2 * 16)
                for u in range(UB):
                    last = nc.vector.tensor_scalar(xn[:, p, u, :], k.X[:, blk * UB + u, :], mv[:, u, 0:1], rstd[:, u:u + 1],
                                                   ALU.subtract, ALU.mult)
                last.then_inc(xn_ready, 1)

            pairs(dve, body)


def plan_phase(nc, k, LG, experts, tokens):
    gates, slots = k.gates, k.slots
    NE = 8
    N = NU * NE
    NT = experts.shape[1]
    d = k.d
    with ExitStack() as ctx:
        def sb(name, shape, dt=F32):
            return ctx.enter_context(nc.sbuf_tensor(f"p_{name}", shape, dt))

        def sem(name):
            return nc.alloc_semaphore(f"p_{name}")

        upper = sb("upper", [P, P])
        ones = sb("ones", [P, P])
        rank = sb("rank", [P, NE])
        tile_no = sb("tile_no", [P, NT])
        row_no = sb("row_no", [P, P])
        token_no = sb("token_no", [P, 1, NU])
        best = sb("best", [P, 2, NU])
        eq = sb("eq", [P, NU, NE])
        who = sb("who", [P, 2, NU])
        hot = sb("hot", [P, 2, NU, NE])
        rest = sb("rest", [P, NU, NE])
        chosen = sb("chosen", [P, N])
        delta = sb("delta", [P, NU])
        ratio = sb("ratio", [P, NU])
        total = sb("total", [P, 1 + N // NE, NE])
        run = sb("run", [P, 2, N])
        place = sb("place", [P, N])
        count = sb("count", [P, NE])
        tiles_i = sb("tiles_i", [P, NE], I32)
        base = sb("base", [P, 2, NE])
        picked = sb("picked", [P, NU, NE])
        slot_f = sb("slot_f", [P, 2, NU])
        past = sb("past", [1, NT, NE - 1])
        expert_f = sb("expert_f", [1, NT])
        tile_i = sb("tile_i", [P, 2, NU], I32)
        tile_f = sb("tile_f", [P, 2, NU])
        row_f = sb("row_f", [P, 2, NU])
        row_hot = sb("row_hot", [P, 4, P])
        tile_hot = sb("tile_hot", [P, 4, NT])
        token_ps = ctx.enter_context(nc.psum_tensor("p_token_ps", [P, 512], F32))
        before_ps = ctx.enter_context(nc.psum_tensor("p_before_ps", [P, 512], F32))
        total_ps = ctx.enter_context(nc.psum_tensor("p_total_ps", [P, 512], F32))

        loaded = sem("loaded")
        chain = sem("chain")
        chosen_ready = sem("chosen_ready")
        delta_ready = sem("delta_ready")
        ratio_ready = sem("ratio_ready")
        counted = sem("counted")
        hot_ready = sem("hot_ready")
        placed = sem("placed")
        block = ctx.enter_context(nc.Block())

        @block.sync
        def _(sp):
            for dst, name in ((upper, "c_upper"), (ones, "c_ones"), (rank, "c_rank"), (tile_no, "c_tile_no"),
                              (row_no, "c_row_no"), (token_no, "c_token_no")):
                sp.dma_start(dst[:], d[name]).then_inc(loaded, 16)

        @block.tensor
        def _(pe):
            pe.wait_ge(loaded, 96)
            pe.wait_ge(chosen_ready, 1)
            nc.tensor.matmul(before_ps[:, 0:N], upper[:], chosen[:], start=True, stop=True).then_inc(counted, 1)
            nc.tensor.matmul(total_ps[:, 0:N], ones[:], chosen[:], start=True, stop=True).then_inc(counted, 1)

            def place(n_, q, start=False, stop=False):
                pe.wait_ge(hot_ready, n_ + 1)
                nc.tensor.matmul(token_ps[:, 0:NT], row_hot[:, q], tile_hot[:, q], start=start, stop=stop,
                                 skip_group_check=True).then_inc(placed, 1)

            for q in range(4):
                place(q, q, start=q == 0)
            with pe.Fori(1, 2 * NU // 4 - 1) as i:
                for q in range(4):
                    place(i * 4 + q, q)
            for q in range(4):
                place(2 * NU - 4 + q, q, stop=q == 3)

        @block.scalar
        def _(act):
            act.wait_ge(delta_ready, 1)
            nc.scalar.activation(ratio[:], delta[:], ACT.Exp).then_inc(ratio_ready, 1)

        @block.vector
        def _(dve):
            steps = [0]

            def chained(ins):
                steps[0] += 1
                ins.then_inc(chain, 1)
                dve.wait_ge(chain, steps[0])

            tt, ts = nc.vector.tensor_tensor, nc.vector.tensor_scalar
            by_unit = lambda ap: ap.unsqueeze(2).broadcast_to([P, NU, NE])
            dve.wait_ge(loaded, 96)
            for i, logits in enumerate((LG, rest)):
                chained(nc.vector.tensor_reduce(best[:, i], logits[:], AX.X, ALU.max))
                chained(tt(eq[:], logits[:], by_unit(best[:, i]), ALU.is_equal))
                chained(tt(eq[:], eq[:], rank[:].unsqueeze(1).broadcast_to([P, NU, NE]), ALU.mult))
                chained(nc.vector.tensor_reduce(who[:, i], eq[:], AX.X, ALU.max))
                chained(tt(hot[:, i], rank[:].unsqueeze(1).broadcast_to([P, NU, NE]), by_unit(who[:, i]), ALU.is_equal))
                if i == 0:
                    chained(nc.vector.scalar_tensor_tensor(out=rest[:], in0=hot[:, 0], scalar=NEG, in1=LG[:],
                                                           op0=ALU.mult, op1=ALU.add))
            tt(delta[:], best[:, 1], best[:, 0], ALU.subtract).then_inc(delta_ready, 1)
            tt(chosen[:].rearrange("p (u e) -> p u e", e=NE), hot[:, 0], hot[:, 1], ALU.add).then_inc(chosen_ready, 1)
            dve.wait_ge(ratio_ready, 1)
            chained(ts(gates[:, 0], ratio[:], 1.0, None, ALU.add))
            chained(nc.vector.reciprocal(gates[:, 0], gates[:, 0]))
            chained(tt(gates[:, 1], ratio[:], gates[:, 0], ALU.mult))
            dve.wait_ge(counted, 2)
            chained(nc.vector.tensor_copy(run[:, 0], total_ps[:, 0:N]))
            src = 0
            reach = 1
            while reach < NU:
                w = reach * NE
                nc.vector.tensor_copy(run[:, 1 - src, 0:w], run[:, src, 0:w])
                chained(tt(run[:, 1 - src, w:N], run[:, src, w:N], run[:, src, 0:N - w], ALU.add))
                src, reach = 1 - src, reach * 2
            nc.vector.tensor_copy(count[:], run[:, src, N - NE:N])
            chained(tt(place[:], before_ps[:, 0:N], run[:, src], ALU.add))
            chained(tt(place[:], total_ps[:, 0:N], place[:], ALU.subtract))
            chained(ts(place[:], place[:], -1.0, None, ALU.mult))
            chained(ts(count[:], count[:], float(P - 1), None, ALU.add))
            chained(nc.vector.tensor_copy(tiles_i[:], count[:]))
            chained(ts(tiles_i[:], tiles_i[:], 7, None, ALU.arith_shift_right))
            chained(nc.vector.tensor_copy(base[:, 0], tiles_i[:]))
            chained(nc.vector.tensor_copy(count[:], base[:, 0]))
            b = 0
            for reach in (1, 2, 4):
                nc.vector.tensor_copy(base[:, 1 - b, 0:reach], base[:, b, 0:reach])
                chained(tt(base[:, 1 - b, reach:NE], base[:, b, reach:NE], base[:, b, 0:NE - reach], ALU.add))
                b = 1 - b
            chained(tt(base[:, b], base[:, b], count[:], ALU.subtract))
            chained(tt(past[:], tile_no[0:1].unsqueeze(2).broadcast_to([1, NT, NE - 1]),
                       base[0:1, b, 1:NE].unsqueeze(1).broadcast_to([1, NT, NE - 1]), ALU.is_ge))
            chained(nc.vector.tensor_reduce(expert_f[:], past[:], AX.X, ALU.add))
            nc.vector.tensor_copy(experts[:], expert_f[:])
            chained(ts(base[:, 1 - b], base[:, b], float(P), None, ALU.mult))
            chained(tt(place[:].rearrange("p (u e) -> p u e", e=NE), place[:].rearrange("p (u e) -> p u e", e=NE),
                       base[:, 1 - b].unsqueeze(1).broadcast_to([P, NU, NE]), ALU.add))
            for i in range(2):
                chained(tt(picked[:], hot[:, i], place[:].rearrange("p (u e) -> p u e", e=NE), ALU.mult))
                chained(nc.vector.tensor_reduce(slot_f[:, i], picked[:], AX.X, ALU.add))
            chained(nc.vector.tensor_copy(slots[:], slot_f[:]))
            chained(ts(tile_i[:], slots[:], 7, None, ALU.arith_shift_right))
            chained(nc.vector.tensor_copy(tile_f[:], tile_i[:]))
            chained(ts(row_f[:], tile_f[:], -float(P), None, ALU.mult))
            chained(tt(row_f[:], row_f[:], slot_f[:], ALU.add))

            def hot_ones(i, u, q, wait_for):
                if wait_for is not None:
                    dve.wait_ge(placed, wait_for)
                ts(row_hot[:, q], row_no[:], row_f[:, i, bass.ds(u, 1)], None, ALU.is_equal)
                ts(tile_hot[:, q], tile_no[:], tile_f[:, i, bass.ds(u, 1)], token_no[:, 0, bass.ds(u, 1)],
                   ALU.is_equal, ALU.mult).then_inc(hot_ready, 1)

            for q in range(4):
                hot_ones(0, q, q, None)
            with dve.Fori(1, NU // 4) as i:
                for q in range(4):
                    hot_ones(0, i * 4 + q, q, i * 4 + q - 3)
            with dve.Fori(0, NU // 4) as i:
                for q in range(4):
                    hot_ones(1, i * 4 + q, q, i * 4 + q + (NU - 3))
            dve.wait_ge(placed, 2 * NU)
            nc.vector.tensor_copy(tokens[:], token_ps[:, 0:NT])


def expert_phase(nc, k, experts, tokens, gate_w, up_w, down_w, w_loaded, NT):
    F = 512
    FC = F // P
    with ExitStack() as ctx:
        def sb(name, shape, dt=F32):
            return ctx.enter_context(nc.sbuf_tensor(f"e_{name}", shape, dt))

        def ps(name):
            return ctx.enter_context(nc.psum_tensor(f"e_{name}_ps", [P, 512], F32))

        def sem(name):
            return nc.alloc_semaphore(f"e_{name}")

        where = sb("where", [P, 4, 1], I32)
        x = sb("x", [P, 4, C])
        xT = sb("xT", [P, 2, P])
        silu = sb("silu", [P, 2, F])
        h = sb("h", [P, 2, F])
        hT = sb("hT", [P, 2, F])
        y = sb("y", [P, 2, C])
        xT_ps = ps("xT")
        G_ps = [ps(f"G{i}") for i in range(2)]
        U_ps = [ps(f"U{i}") for i in range(2)]
        hT_ps = [ps(f"hT{i}") for i in range(2)]
        Y_ps = ps("Y")

        where_ready = sem("where_ready")
        x_in = [sem(f"x_in{i}") for i in range(4)]
        xT_done = sem("xT_done")
        xT_ready = sem("xT_ready")
        gate_done = sem("gate_done")
        up_done = sem("up_done")
        silu_ready = sem("silu_ready")
        h_ready = sem("h_ready")
        hT_done = sem("hT_done")
        hT_ready = sem("hT_ready")
        y_done = sem("y_done")
        y_ready = sem("y_ready")
        stored = [sem("stored0"), sem("stored1")]
        passed = sem("passed")
        block = ctx.enter_context(nc.Block())
        Q = 4

        def later(t, least):
            return not isinstance(t, int) or t >= least

        def tiles(eng, body):
            for j in range(Q):
                body(j, j, NT)
            with eng.Fori(1, NT // Q - 1) as i:
                for j in range(Q):
                    body(i * Q + j, j, NT)
            for j in range(Q):
                body(NT - Q + j, j, Q - j)

        @block.sync
        def _(sp):
            def body(t, j, left):
                p = j % 2
                wait_here(sp, y_ready, t + 1, passed)
                sp.dma_start(k.slot_out[bass.ds(t * P, P), :], y[:, p, :]).then_inc(stored[p], 16)

            tiles(sp, body)
            for q in stored:
                sp.wait_ge(q, NT // 2 * 16)

        @block.scalar
        def _(act):
            def body(t, j, left):
                p = j % 2
                act.wait_ge(gate_done, t + 1)
                if later(t, 2):
                    act.wait_ge(h_ready, t - 1)
                nc.scalar.activation(silu[:, p, :], G_ps[p][:], ACT.Silu).then_inc(silu_ready, 1)
                if later(t, 1):
                    hidden_turned(t - 1, 1 - p)

            def hidden_turned(t, p):
                act.wait_ge(hT_done, t + 1)
                if later(t, 2):
                    act.wait_ge(y_done, t - 1)
                nc.scalar.activation(hT[:, p, :], hT_ps[p][:], ACT.Copy).then_inc(hT_ready, 1)

            tiles(act, body)
            hidden_turned(NT - 1, 1)

        @block.tensor
        def _(pe):
            def turn_x(t, j):
                pe.wait_ge(x_in[j], (t // Q + 1) * 16)
                if later(t, 1):
                    pe.wait_ge(xT_ready, t)
                nc.tensor.transpose(xT_ps[:, 0:P], x[:, j, :], k.ident[:]).then_inc(xT_done, 1)

            def gate_up(t, j):
                p = j % 2
                e = nc.tensor.value_load(experts[0:1, bass.ds(t, 1)], min_val=0, max_val=7)
                pe.wait_ge(xT_ready, t + 1)
                if later(t, 2):
                    pe.wait_ge(h_ready, t - 1)
                nc.tensor.matmul(G_ps[p][:], xT[:, p, :], gate_w[:, bass.ds(e * F, F)], start=True, stop=True)\
                    .then_inc(gate_done, 1)
                nc.tensor.matmul(U_ps[p][:], xT[:, p, :], up_w[:, bass.ds(e * F, F)], start=True, stop=True)\
                    .then_inc(up_done, 1)

            def turn_h(t, j):
                p = j % 2
                pe.wait_ge(h_ready, t + 1)
                if later(t, 2):
                    pe.wait_ge(hT_ready, t - 1)
                for c in range(FC):
                    mm = nc.tensor.transpose(hT_ps[p][:, c * P:(c + 1) * P], h[:, p, c * P:(c + 1) * P], k.ident[:])
                mm.then_inc(hT_done, 1)

            def down(t, j):
                p = j % 2
                e = nc.tensor.value_load(experts[0:1, bass.ds(t, 1)], min_val=0, max_val=7)
                pe.wait_ge(hT_ready, t + 1)
                if later(t, 1):
                    pe.wait_ge(y_ready, t)
                for c in range(FC):
                    mm = nc.tensor.matmul(Y_ps[:, 0:C], hT[:, p, c * P:(c + 1) * P], down_w[:, bass.ds(e * F + c * C, C)],
                                          start=(c == 0), stop=(c == FC - 1))
                mm.then_inc(y_done, 1)

            pe.wait_ge(w_loaded, 48)
            turn_x(0, 0)
            turn_x(1, 1)
            gate_up(0, 0)

            def body(t, j, left):
                if left > 2:
                    turn_x(t + 2, (j + 2) % Q)
                if left > 1:
                    gate_up(t + 1, (j + 1) % Q)
                turn_h(t, j)
                if later(t, 1):
                    down(t - 1, (j - 1) % Q)

            tiles(pe, body)
            down(NT - 1, Q - 1)

        @block.vector
        def _(dve):
            def x_turned(t, p):
                dve.wait_ge(xT_done, t + 1)
                if later(t, 2):
                    dve.wait_ge(up_done, t - 1)
                nc.vector.tensor_copy(xT[:, p, :], xT_ps[:, 0:P]).then_inc(xT_ready, 1)

            def output(t, p):
                dve.wait_ge(y_done, t + 1)
                if later(t, 2):
                    dve.wait_ge(stored[p], (t // 2) * 16)
                nc.vector.tensor_copy(y[:, p, :], Y_ps[:, 0:C]).then_inc(y_ready, 1)

            for j in range(Q):
                nc.vector.tensor_copy(where[:, j, :], tokens[:, j:j + 1]).then_inc(where_ready, 1)
            x_turned(0, 0)
            x_turned(1, 1)

            def body(t, j, left):
                p = j % 2
                if left > Q:
                    nc.vector.tensor_copy(where[:, j, :], tokens[:, bass.ds(t + Q, 1)]).then_inc(where_ready, 1)
                if left > 2:
                    x_turned(t + 2, p)
                dve.wait_ge(silu_ready, t + 1)
                dve.wait_ge(up_done, t + 1)
                if later(t, 2):
                    dve.wait_ge(hT_done, t - 1)
                nc.vector.tensor_tensor(h[:, p, :], U_ps[p][:], silu[:, p, :], ALU.mult).then_inc(h_ready, 1)
                if later(t, 1):
                    output(t - 1, 1 - p)

            tiles(dve, body)
            output(NT - 1, 1)

        @block.gpsimd
        def _(pool):
            def body(t, j, left):
                wait_here(pool, where_ready, t + 1, passed)
                nc.gpsimd.indirect_dma_start(
                    out=x[:, j, :], out_offset=None, in_=k.xn_rows,
                    in_offset=bass.IndirectOffsetOnAxis(ap=where[:, j, :], axis=0)).then_inc(x_in[j], 16)

            tiles(pool, body)


def wide_attention_phase(nc, k):
    UB = 2
    NB = NU // UB
    BB = 2 * UB
    TOK = UB * P
    D1 = 64
    G = H // 4
    SCALE = float(D1) ** -0.5
    n = "a1"
    d = k.d
    with ExitStack() as ctx:
        def sb(name, shape, dt=F32):
            return ctx.enter_context(nc.sbuf_tensor(f"{n}_{name}", shape, dt))

        def ps(name, shape):
            return ctx.enter_context(nc.psum_tensor(f"{n}_{name}_ps", shape, F32))

        def sem(name):
            return nc.alloc_semaphore(f"{n}_{name}")

        where = sb("where", [P, 2, 2, UB], I32)
        expert_rows = sb("expert_rows", [P, 2, 2, UB, C])
        wq = sb("wq", [P, G, 2, P])
        wk = sb("wk", [P, G, 2, P])
        wv = sb("wv", [P, G, 4 * D1])
        wo = sb("wo", [P, G, 2, C])
        bo = sb("bo", [1, C])
        cos = sb("cos", [P, T])
        sin = sb("sin", [P, T])
        parity = sb("parity", [P, 2])
        stats = sb("stats", [P, UB, 6])
        mv = sb("mv", [P, UB, 2])
        var_eps = sb("var_eps", [P, UB])
        minus_half = sb("minus_half", [P, UB])
        rstd = sb("rstd", [P, UB])
        xn = sb("xn", [P, UB, C])
        xnT = sb("xnT", [P, 2, TOK])
        PQ = sb("PQ", [P, 2, 2, TOK])
        PK = sb("PK", [P, 2, 2, TOK])
        RQ = sb("RQ", [P, 2, TOK])
        QD = sb("QD", [P, 2, 2, BB, P])
        KT = sb("KT", [P, 2, 2, TOK])
        V = sb("V", [P, 2, BB, 2, P])
        row_max = sb("row_max", [P, 2, BB])
        row_sum = sb("row_sum", [P, 2 * BB])
        rsum = sb("rsum", [P, 2, 2 * BB])
        E = sb("E", [P, 2, 512])
        ET = sb("ET", [P, 2, 512])
        OT = sb("OT", [P, 2, 2, TOK])
        Q_ps = ps("Q", [P, 512])
        K_ps = ps("K", [P, 512])
        V_ps = ps("V", [P, 512])
        S_ps = ps("S", [P, 2, 512])
        ET_ps = ps("ET", [P, 512])
        PV_ps = ps("PV", [P, 512])
        Y_ps = ps("Y", [P, 512])

        weights = sem("weights")
        setup = sem("setup")
        where_ready = sem("where_ready")
        got = [sem("got0"), sem("got1")]
        combined = sem("combined")
        stats_done = sem("stats_done")
        var_ready = sem("var_ready")
        rstd_ready = sem("rstd_ready")
        xn_ready = sem("xn_ready")
        xnT_ps = sem("xnT_ps")
        xnT_ready = sem("xnT_ready")
        q_ps = sem("q_ps")
        k_ps = sem("k_ps")
        v_ps = sem("v_ps")
        pq_ready = sem("pq_ready")
        pk_ready = sem("pk_ready")
        rq_ready = sem("rq_ready")
        kt_ready = sem("kt_ready")
        qd_ready = sem("qd_ready")
        v_ready = sem("v_ready")
        s_ps = sem("s_ps")
        max_done = sem("max_done")
        d_ready = sem("d_ready")
        e_ready = sem("e_ready")
        sum_done = sem("sum_done")
        rsum_ready = sem("rsum_ready")
        en_ready = sem("en_ready")
        et_ps = sem("et_ps")
        et_ready = sem("et_ready")
        pv_ps = sem("pv_ps")
        ot_ready = sem("ot_ready")
        y_ps = sem("y_ps")
        x_done = sem("x_done")
        passed = sem("passed")
        N_WEIGHTS = 8

        block = ctx.enter_context(nc.Block())

        def blocks(eng, prologue, step, epilogue):
            prologue()
            step(0, 0, prev=False, nxt=2)
            with eng.Fori(0, NB // 2 - 2) as i:
                step(i * 2 + 1, 1, prev=True, nxt=2)
                step(i * 2 + 2, 0, prev=True, nxt=2)
            for blk in range(NB - 3, NB):
                step(blk, blk % 2, prev=True, nxt=min(2, NB - 1 - blk))
            epilogue()

        def item_at(blk, g):
            return blk + g // G, g % G

        def later(blk, least):
            return not isinstance(blk, int) or blk >= least

        @block.sync
        def _(sp):
            for dst, name in [(wq, "L1_attn_wq"), (wk, "L1_attn_wk"), (wv, "L1_attn_wv"), (wo, "L1_attn_wo"),
                              (bo, "L1_attn_bo"), (cos, "c_cos"), (sin, "c_sin"), (parity, "c_parity")]:
                sp.dma_start(dst[:], d[name]).then_inc(weights, 16)

        @block.gpsimd
        def _(pool):
            def power(nb):
                pool.wait_ge(var_ready, nb + 1)
                nc.gpsimd.tensor_tensor(rstd[:], var_eps[:], minus_half[:], ALU.pow).then_inc(rstd_ready, 1)

            def rotate(dst, src):
                nc.gpsimd.tensor_tensor(dst[:, 0, :], src[:, 0, 0, :], src[:, 1, 1, :], ALU.subtract)
                return nc.gpsimd.tensor_tensor(dst[:, 1, :], src[:, 1, 0, :], src[:, 0, 1, :], ALU.add)

            def rotate_k(blk, g):
                n_ = blk * G + g
                pool.wait_ge(pk_ready, n_ + 1)
                if later(n_, 2):
                    pool.wait_ge(s_ps, n_ - 1)
                rotate(KT[:, g % 2], PK).then_inc(kt_ready, 1)

            def rotate_q(blk, g):
                n_ = blk * G + g
                pool.wait_ge(pq_ready, n_ + 1)
                if later(n_, 1):
                    pool.wait_ge(qd_ready, n_)
                rotate(RQ, PQ).then_inc(rq_ready, 1)

            def normalise_e(blk, g):
                n_ = blk * G + g
                pool.wait_ge(rsum_ready, n_ + 1)
                e = E[:, g % 2, :].rearrange("p (r t) -> p r t", t=T)
                nc.gpsimd.tensor_tensor(e, e, rsum[:, g % 2, :].unsqueeze(2).broadcast_to([P, 2 * BB, T]), ALU.mult)\
                    .then_inc(en_ready, 1)

            def gather(nb, u, p):
                if u == 0 and later(nb, 2):
                    pool.wait_ge(combined, (nb - 1) * 2)
                wait_here(pool, where_ready, nb + 1, passed)
                for i in range(2):
                    nc.gpsimd.indirect_dma_start(
                        out=expert_rows[:, p, i, u, :], out_offset=None, in_=k.slot_out,
                        in_offset=bass.IndirectOffsetOnAxis(ap=where[:, p, i, u:u + 1], axis=0)).then_inc(got[p], 16)

            def prologue():
                for nb in range(2):
                    for u in range(UB):
                        gather(nb, u, nb)
                nc.gpsimd.memset(minus_half[:], -0.5).then_inc(setup, 1)
                nc.gpsimd.memset(V[:], 0.0).then_inc(setup, 1)
                pool.wait_ge(setup, 2)
                power(0)
                for g in range(3):
                    rotate_q(0, g)
                    rotate_k(0, g)
                    if g == 1:
                        normalise_e(0, 0)

            def step(blk, p, prev, nxt):
                for g in range(G):
                    if nxt and g == 0:
                        power(blk + 1)
                    if g + 1 < G or nxt:
                        normalise_e(*item_at(blk, g + 1))
                    if g + 3 < G or nxt:
                        rotate_q(*item_at(blk, g + 3))
                        rotate_k(*item_at(blk, g + 3))
                    if nxt == 2 and g in (1, 2):
                        gather(blk + 2, g - 1, p)

            blocks(pool, prologue, step, lambda: None)

        @block.tensor
        def _(pe):
            def transpose_x(nb, p):
                pe.wait_ge(xn_ready, nb + 1)
                if later(nb, 1):
                    pe.wait_ge(pq_ready, nb * G)
                for u in range(UB):
                    mm = nc.tensor.transpose(Q_ps[:, u * P:(u + 1) * P], xn[:, u, :], k.ident[:])
                mm.then_inc(xnT_ps, 1)

            def project_qk(blk, g, p):
                n_ = blk * G + g
                pe.wait_ge(xnT_ready, blk + 1)
                if later(n_, 1):
                    pe.wait_ge(pq_ready, n_)
                for a in range(2):
                    mm = nc.tensor.matmul(Q_ps[:, a * TOK:(a + 1) * TOK], wq[:, g, a, :], xnT[:, p, :], start=True, stop=True)
                mm.then_inc(q_ps, 1)
                if later(n_, 1):
                    pe.wait_ge(pk_ready, n_)
                for a in range(2):
                    mm = nc.tensor.matmul(K_ps[:, a * TOK:(a + 1) * TOK], wk[:, g, a, :], xnT[:, p, :], start=True, stop=True)
                mm.then_inc(k_ps, 1)

            def project_v(blk, g, p):
                n_ = blk * G + g
                if later(n_, 1):
                    pe.wait_ge(v_ready, n_)
                for u in range(UB):
                    mm = nc.tensor.matmul(V_ps[:, u * 256:(u + 1) * 256], xnT[:, p, u * P:(u + 1) * P], wv[:, g, :],
                                          start=True, stop=True)
                mm.then_inc(v_ps, 1)

            def scores(blk, g):
                n_ = blk * G + g
                pe.wait_ge(qd_ready, n_ + 1)
                pe.wait_ge(kt_ready, n_ + 1)
                if later(n_, 1):
                    pe.wait_ge(d_ready, n_)
                rows = [slice(64 * pair, 64 * pair + 64) for pair in range(2)]
                bank = [S_ps[:, pair, 0:BB * T] for pair in range(2)]
                for pair in range(2):
                    nc.tensor.matmul(bank[pair], k.causal_queries[rows[pair], :], k.causal_keys[rows[pair], 0:BB * T],
                                     start=True, stop=False)
                for b in range(BB):
                    for a in range(2):
                        for pair in range(2):
                            mm = nc.tensor.matmul(bank[pair][:, b * T:(b + 1) * T], QD[rows[pair], g % 2, a, b, :],
                                                  KT[rows[pair], g % 2, a, b * T:(b + 1) * T], start=False,
                                                  stop=(b == BB - 1 and a == 1))
                mm.then_inc(s_ps, 1)

            def transpose_e(blk, g):
                n_ = blk * G + g
                pe.wait_ge(en_ready, n_ + 1)
                if later(n_, 1):
                    pe.wait_ge(et_ready, n_)
                for b in range(BB):
                    mm = nc.tensor.transpose(ET_ps[:, b * P:(b + 1) * P], E[:, g % 2, b * P:(b + 1) * P], k.ident[:])
                mm.then_inc(et_ps, 1)

            def weigh_values(blk, g):
                n_ = blk * G + g
                pe.wait_ge(et_ready, n_ + 1)
                pe.wait_ge(v_ready, n_ + 1)
                if later(n_, 1):
                    pe.wait_ge(ot_ready, n_)
                for h in range(2):
                    for b in range(BB):
                        at = h * TOK + b * T
                        mm = nc.tensor.matmul(PV_ps[:, at:at + T], V[:, g % 2, b, h, :],
                                              ET[:, g % 2, b * P + h * T:b * P + (h + 1) * T], start=True, stop=True)
                mm.then_inc(pv_ps, 1)

            def project_o(blk, g):
                n_ = blk * G + g
                pe.wait_ge(ot_ready, n_ + 1)
                if g == 0 and later(blk, 1):
                    pe.wait_ge(x_done, blk)
                for u in range(UB):
                    out = Y_ps[:, u * P:(u + 1) * P]
                    for h in range(2):
                        mm = nc.tensor.matmul(out, OT[:, g % 2, h, u * P:(u + 1) * P], wo[:, g, h, :],
                                              start=(g == 0 and u == 0 and h == 0), stop=False, skip_group_check=True)
                    if g == G - 1:
                        mm = nc.tensor.matmul(out, k.ones_row[0:1, 0:P], bo[:], start=False, stop=(u == UB - 1),
                                              skip_group_check=True)
                mm.then_inc(y_ps, 1)

            def prologue():
                pe.wait_ge(weights, 16 * N_WEIGHTS)
                transpose_x(0, 0)
                for g in range(3):
                    project_qk(0, g, 0)
                    if g >= 1:
                        scores(0, g - 1)
                        project_v(0, g - 1, 0)
                transpose_e(0, 0)

            def step(blk, p, prev, nxt):
                for g in range(G):
                    if g + 3 < G or nxt:
                        nb, gg = item_at(blk, g + 3)
                        project_qk(nb, gg, p if g + 3 < G else 1 - p)
                    if g + 2 < G or nxt:
                        scores(*item_at(blk, g + 2))
                    if g + 1 < G or nxt:
                        transpose_e(*item_at(blk, g + 1))
                    if nxt and g == 0:
                        transpose_x(blk + 1, 1 - p)
                    if g + 2 < G or nxt:
                        nb, gg = item_at(blk, g + 2)
                        project_v(nb, gg, p if g + 2 < G else 1 - p)
                    weigh_values(blk, g)
                    if g > 0:
                        project_o(blk, g - 1)
                    elif prev:
                        project_o(blk - 1, G - 1)

            blocks(pe, prologue, step, lambda: project_o(NB - 1, G - 1))

        @block.scalar
        def _(act):
            def evacuate_xT(nb, p):
                act.wait_ge(xnT_ps, nb + 1)
                if later(nb, 2):
                    act.wait_ge(v_ps, (nb - 1) * G)
                nc.scalar.activation(xnT[:, p, :], Q_ps[:, 0:TOK], ACT.Copy).then_inc(xnT_ready, 1)

            def spread_q(blk, g):
                n_ = blk * G + g
                act.wait_ge(rq_ready, n_ + 1)
                if later(n_, 2):
                    act.wait_ge(s_ps, n_ - 1)
                for h in range(2):
                    last = nc.scalar.activation(QD[:, g % 2, :, :, h * T:(h + 1) * T],
                                                RQ[:].rearrange("p a (b t) -> p a b t", t=T), ACT.Copy,
                                                scale=parity[:, h:h + 1])
                last.then_inc(qd_ready, 1)

            def evacuate_v(blk, g):
                n_ = blk * G + g
                act.wait_ge(v_ps, n_ + 1)
                if later(n_, 2):
                    act.wait_ge(pv_ps, n_ - 1)
                src = V_ps[:].rearrange("p (u q h e) -> p u q h e", u=UB, q=2, h=2)
                dst = V[:, g % 2].rearrange("p (u r) h (q e) -> p u r h q e", r=2, q=2)
                for r in range(2):
                    for q in range(2):
                        last = nc.scalar.activation(dst[64 * q:64 * q + 64, :, r, :, q, :],
                                                    src[64 * r:64 * r + 64, :, q, :, :], ACT.Copy)
                last.then_inc(v_ready, 1)

            def exponentials(blk, g):
                n_ = blk * G + g
                act.wait_ge(d_ready, n_ + 1)
                nc.scalar.activation(E[:, g % 2, :], E[:, g % 2, :], ACT.Exp, scale=SCALE).then_inc(e_ready, 1)

            def evacuate_e(blk, g):
                n_ = blk * G + g
                act.wait_ge(et_ps, n_ + 1)
                if later(n_, 2):
                    act.wait_ge(pv_ps, n_ - 1)
                nc.scalar.activation(ET[:, g % 2, :], ET_ps[:], ACT.Copy).then_inc(et_ready, 1)

            def evacuate_o(blk, g):
                n_ = blk * G + g
                act.wait_ge(pv_ps, n_ + 1)
                if later(n_, 2):
                    act.wait_ge(y_ps, n_ - 1)
                nc.scalar.activation(OT[:, g % 2].rearrange("p h t -> p (h t)"), PV_ps[:], ACT.Copy).then_inc(ot_ready, 1)

            def slots_of(nb, p):
                if later(nb, 2):
                    act.wait_ge(got[p], (nb // 2) * (16 * 2 * UB))
                nc.scalar.activation(where[:, p], k.slots[:, :, bass.ds(nb * UB, UB)], ACT.Copy).then_inc(where_ready, 1)

            def prologue():
                slots_of(0, 0)
                slots_of(1, 1)
                act.wait_ge(weights, 16 * N_WEIGHTS)
                act.wait_ge(setup, 2)
                evacuate_xT(0, 0)
                spread_q(0, 0)
                for g in range(1, 3):
                    exponentials(0, g - 1)
                    evacuate_v(0, g - 1)
                    spread_q(0, g)
                evacuate_e(0, 0)

            def step(blk, p, prev, nxt):
                for g in range(G):
                    if g + 3 < G or nxt:
                        spread_q(*item_at(blk, g + 3))
                    if g + 1 < G or nxt:
                        evacuate_e(*item_at(blk, g + 1))
                    if nxt and g == 0:
                        evacuate_xT(blk + 1, 1 - p)
                    if g + 2 < G or nxt:
                        exponentials(*item_at(blk, g + 2))
                        evacuate_v(*item_at(blk, g + 2))
                    evacuate_o(blk, g)
                    if nxt == 2 and g == 0:
                        slots_of(blk + 2, p)

            blocks(act, prologue, step, lambda: None)

        @block.vector
        def _(dve):
            def combine(nb, p):
                dve.wait_ge(got[p], (nb // 2 + 1) * (16 * 2 * UB))
                for i in range(2):
                    for u in range(UB):
                        x = k.X[:, nb * UB + u, :]
                        last = nc.vector.scalar_tensor_tensor(out=x, in0=expert_rows[:, p, i, u, :],
                                                              scalar=k.gates[:, i, bass.ds(nb * UB + u, 1)], in1=x,
                                                              op0=ALU.mult, op1=ALU.add)
                    last.then_inc(combined, 1)
                    wait_here(dve, combined, nb * 2 + i + 1, passed)

            def statistics(nb):
                for u in range(UB):
                    last = nc.vector.bn_stats(stats[:, u, :], k.X[:, nb * UB + u, :])
                last.then_inc(stats_done, 1)
                wait_here(dve, stats_done, nb * 2 + 1, passed)
                for u in range(UB):
                    last = nc.vector.bn_aggr(mv[:, u, :], stats[:, u, :])
                last.then_inc(stats_done, 1)
                dve.wait_ge(stats_done, nb * 2 + 2)
                nc.vector.tensor_scalar(var_eps[:], mv[:, :, 1], EPS, None, ALU.add).then_inc(var_ready, 1)

            def normalise(nb):
                dve.wait_ge(rstd_ready, nb + 1)
                if later(nb, 1):
                    dve.wait_ge(xnT_ps, nb)
                for u in range(UB):
                    last = nc.vector.tensor_scalar(xn[:, u, :], k.X[:, nb * UB + u, :], mv[:, u, 0:1], rstd[:, u:u + 1],
                                                   ALU.subtract, ALU.mult)
                last.then_inc(xn_ready, 1)

            def products(bank, dst):
                src = bank[:].rearrange("p (r t) -> p r t", t=T)
                for i, table in enumerate((cos, sin)):
                    last = nc.vector.tensor_tensor(dst[:, i].rearrange("p a (b t) -> p (a b) t", t=T), src,
                                                   table[:].unsqueeze(1).broadcast_to([P, 2 * BB, T]), ALU.mult)
                return last

            def products_qk(blk, g):
                n_ = blk * G + g
                dve.wait_ge(q_ps, n_ + 1)
                if later(n_, 1):
                    dve.wait_ge(rq_ready, n_)
                products(Q_ps, PQ).then_inc(pq_ready, 1)
                dve.wait_ge(k_ps, n_ + 1)
                if later(n_, 1):
                    dve.wait_ge(kt_ready, n_)
                products(K_ps, PK).then_inc(pk_ready, 1)

            def subtract_max(blk, g):
                n_ = blk * G + g
                dve.wait_ge(s_ps, n_ + 1)
                src = S_ps[:, :, 0:BB * T].rearrange("p q (b t) -> p q b t", t=T)
                nc.vector.tensor_reduce(row_max[:], src, AX.X, ALU.max).then_inc(max_done, 1)
                dve.wait_ge(max_done, n_ + 1)
                if later(n_, 2):
                    dve.wait_ge(et_ps, n_ - 1)
                dst = E[:, g % 2, :].rearrange("p (b q t) -> p q b t", b=BB, q=2)
                nc.vector.tensor_tensor(dst, src, row_max[:].unsqueeze(3).broadcast_to([P, 2, BB, T]), ALU.subtract)\
                    .then_inc(d_ready, 1)

            def sums(blk, g):
                n_ = blk * G + g
                dve.wait_ge(e_ready, n_ + 1)
                nc.vector.tensor_reduce(row_sum[:], E[:, g % 2, :].rearrange("p (r t) -> p r t", t=T), AX.X, ALU.add)\
                    .then_inc(sum_done, 1)
                dve.wait_ge(sum_done, n_ + 1)
                if later(n_, 2):
                    dve.wait_ge(en_ready, n_ - 1)
                nc.vector.reciprocal(rsum[:, g % 2, :], row_sum[:]).then_inc(rsum_ready, 1)

            def add_residual(blk):
                dve.wait_ge(y_ps, (blk + 1) * G)
                x = k.X[:, bass.ds(blk * UB, UB), :]
                nc.vector.tensor_tensor(x, Y_ps[:, 0:TOK].rearrange("p (u c) -> p u c", u=UB), x, ALU.add)\
                    .then_inc(x_done, 1)

            def prologue():
                dve.wait_ge(weights, 16 * N_WEIGHTS)
                combine(0, 0)
                statistics(0)
                normalise(0)
                products_qk(0, 0)
                for g in range(1, 3):
                    products_qk(0, g)
                    subtract_max(0, g - 1)
                    if g == 1:
                        sums(0, 0)

            def step(blk, p, prev, nxt):
                for g in range(G):
                    if nxt and g == 0:
                        combine(blk + 1, 1 - p)
                        statistics(blk + 1)
                    if g + 1 < G or nxt:
                        sums(*item_at(blk, g + 1))
                    if nxt and g == 0:
                        normalise(blk + 1)
                    if g + 3 < G or nxt:
                        products_qk(*item_at(blk, g + 3))
                    if g + 2 < G or nxt:
                        subtract_max(*item_at(blk, g + 2))
                    if prev and g == 1:
                        add_residual(blk - 1)

            blocks(dve, prologue, step, lambda: add_residual(NB - 1))


def masked_attention_phase(nc, k):
    UB = 4
    NB = NU // UB
    BB = 2 * UB
    TOK = UB * P
    n = "x1"
    d = k.d
    with ExitStack() as ctx:
        def sb(name, shape, dt=F32):
            return ctx.enter_context(nc.sbuf_tensor(f"{n}_{name}", shape, dt))

        def ps(name, shape):
            return ctx.enter_context(nc.psum_tensor(f"{n}_{name}_ps", shape, F32))

        def sem(name):
            return nc.alloc_semaphore(f"{n}_{name}")

        ctxT = sb("ctxT", [P, 2, TOK])
        ctxK = sb("ctxK", [T, 2, BB, C])
        mask = sb("mask", [2, NU * T], I32)
        pad = sb("pad", [2, NU * T], BF16)
        stats = sb("stats", [P, UB, 6])
        mv = sb("mv", [P, UB, 2])
        var_eps = sb("var_eps", [P, UB])
        minus_half = sb("minus_half", [P, UB])
        rstd = sb("rstd", [P, UB])
        xn = sb("xn", [P, UB, C])
        xnT = sb("xnT", [P, TOK])
        row_max = sb("row_max", [P, UB])
        row_sum = sb("row_sum", [P, UB])
        rsum = sb("rsum", [P, UB])
        E = sb("E", [P, UB, T])
        ET = sb("ET", [T, TOK])
        xT_ps = ps("xT", [P, 512])
        S_ps = [ps(f"S{i}", [P, 512]) for i in range(2)]
        ET_ps = ps("ET", [P, 512])
        PV_ps = ps("PV", [P, 512])

        loaded = sem("loaded")
        ctx_in = [sem("ctx_in0"), sem("ctx_in1")]
        setup = sem("setup")
        stats_done = sem("stats_done")
        var_ready = sem("var_ready")
        rstd_ready = sem("rstd_ready")
        xn_ready = sem("xn_ready")
        xnT_ps = sem("xnT_ps")
        xnT_ready = sem("xnT_ready")
        s_ps = sem("s_ps")
        softmax_done = sem("softmax_done")
        d_ready = sem("d_ready")
        e_ready = sem("e_ready")
        en_ready = sem("en_ready")
        et_ps = sem("et_ps")
        et_ready = sem("et_ready")
        pv_ps = sem("pv_ps")
        x_done = sem("x_done")
        passed = sem("passed")

        block = ctx.enter_context(nc.Block())

        def later(blk, least):
            return not isinstance(blk, int) or blk >= least

        @block.sync
        def _(sp):
            sp.dma_start(mask[:], d["mask"]).then_inc(loaded, 16)

            def load_ctx(nb, p):
                if later(nb, 2):
                    wait_here(sp, pv_ps, nb - 1, passed)
                sp.dma_start(ctxT[:, p, :], d["ctxT"][:, bass.ds(nb * TOK, TOK)]).then_inc(ctx_in[p], 16)
                sp.dma_start(ctxK[:, p, :, :], d["ctxK"][:, bass.ds(nb * BB, BB), :]).then_inc(ctx_in[p], 16)

            def step(blk, p, prev, nxt):
                if nxt:
                    load_ctx(blk + 1, 1 - p)

            run_blocks(sp, NB, lambda: load_ctx(0, 0), step, lambda: None)

        @block.gpsimd
        def _(pool):
            nc.gpsimd.memset(minus_half[:], -0.5).then_inc(setup, 1)
            pool.wait_ge(setup, 1)

            def power(nb):
                pool.wait_ge(var_ready, nb + 1)
                nc.gpsimd.tensor_tensor(rstd[:], var_eps[:], minus_half[:], ALU.pow).then_inc(rstd_ready, 1)

            def step(blk, p, prev, nxt):
                if nxt:
                    power(blk + 1)

            run_blocks(pool, NB, lambda: power(0), step, lambda: None)

        @block.tensor
        def _(pe):
            def front(nb, p):
                pe.wait_ge(xn_ready, nb + 1)
                if later(nb, 1):
                    pe.wait_ge(xnT_ready, nb)
                for u in range(UB):
                    mm = nc.tensor.transpose(xT_ps[:, u * P:(u + 1) * P], xn[:, u, :], k.ident[:])
                mm.then_inc(xnT_ps, 1)
                bank = S_ps[p]
                if later(nb, 2):
                    pe.wait_ge(d_ready, nb - 1)
                nc.tensor.matmul(bank[:, 0:UB * T], k.causal_queries[0:T, :], k.causal_keys[0:T, 0:UB * T],
                                 start=True, stop=False)
                nc.tensor.matmul(bank[:, 0:UB * T], k.of_batch[:], pad[:, bass.ds(nb * UB * T, UB * T)],
                                 start=False, stop=False)
                pe.wait_ge(ctx_in[p], (nb // 2 + 1) * 32)
                pe.wait_ge(xnT_ready, nb + 1)
                for b in range(BB):
                    half = slice(64 * (b % 2), 64 * (b % 2) + 64)
                    mm = nc.tensor.matmul(bank[half, (b // 2) * T:(b // 2 + 1) * T], xnT[:, b * T:(b + 1) * T],
                                          ctxT[:, p, b * T:(b + 1) * T], start=False, stop=(b >= BB - 2))
                mm.then_inc(s_ps, 1)

            def back(blk, p):
                if later(blk, 1):
                    pe.wait_ge(et_ready, blk)
                wait_here(pe, en_ready, blk + 1, passed)
                for u in range(UB):
                    mm = nc.tensor.transpose(ET_ps[0:T, u * P:(u + 1) * P], E[:, u, :], k.ident[:])
                mm.then_inc(et_ps, 1)
                if later(blk, 1):
                    pe.wait_ge(x_done, blk)
                wait_here(pe, et_ready, blk + 1, passed)
                for b in range(BB):
                    half = slice(64 * (b % 2), 64 * (b % 2) + 64)
                    mm = nc.tensor.matmul(PV_ps[half, (b // 2) * C:(b // 2 + 1) * C], ET[:, b * T:(b + 1) * T],
                                          ctxK[:, p, b, :], start=True, stop=True)
                mm.then_inc(pv_ps, 1)

            def prologue():
                pe.wait_ge(softmax_done, 1)
                front(0, 0)

            def step(blk, p, prev, nxt):
                if nxt:
                    front(blk + 1, 1 - p)
                back(blk, p)

            run_blocks(pe, NB, prologue, step, lambda: None)

        @block.scalar
        def _(act):
            def evacuate_xT(nb):
                act.wait_ge(xnT_ps, nb + 1)
                if later(nb, 1):
                    act.wait_ge(s_ps, nb)
                nc.scalar.activation(xnT[:], xT_ps[:], ACT.Copy).then_inc(xnT_ready, 1)

            def step(blk, p, prev, nxt):
                if nxt:
                    evacuate_xT(blk + 1)
                act.wait_ge(d_ready, blk + 1)
                nc.scalar.activation(E[:], E[:], ACT.Exp, scale=float(C) ** -0.5).then_inc(e_ready, 1)
                act.wait_ge(et_ps, blk + 1)
                if later(blk, 1):
                    act.wait_ge(pv_ps, blk)
                nc.scalar.activation(ET[:], ET_ps[0:T, :], ACT.Copy).then_inc(et_ready, 1)

            run_blocks(act, NB, lambda: evacuate_xT(0), step, lambda: None)

        @block.vector
        def _(dve):
            def front(nb):
                for u in range(UB):
                    last = nc.vector.bn_stats(stats[:, u, :], k.X[:, nb * UB + u, :])
                last.then_inc(stats_done, 1)
                wait_here(dve, stats_done, nb * 2 + 1, passed)
                for u in range(UB):
                    last = nc.vector.bn_aggr(mv[:, u, :], stats[:, u, :])
                last.then_inc(stats_done, 1)
                dve.wait_ge(stats_done, nb * 2 + 2)
                nc.vector.tensor_scalar(var_eps[:], mv[:, :, 1], EPS, None, ALU.add).then_inc(var_ready, 1)
                dve.wait_ge(rstd_ready, nb + 1)
                if later(nb, 1):
                    dve.wait_ge(xnT_ps, nb)
                for u in range(UB):
                    last = nc.vector.tensor_scalar(xn[:, u, :], k.X[:, nb * UB + u, :], mv[:, u, 0:1], rstd[:, u:u + 1],
                                                   ALU.subtract, ALU.mult)
                last.then_inc(xn_ready, 1)

            def back(blk, p):
                done = blk * 3 + 1
                dve.wait_ge(s_ps, blk + 1)
                src = S_ps[p][:, 0:UB * T].rearrange("p (u t) -> p u t", t=T)
                nc.vector.tensor_reduce(row_max[:], src, AX.X, ALU.max).then_inc(softmax_done, 1)
                dve.wait_ge(softmax_done, done + 1)
                if later(blk, 1):
                    dve.wait_ge(et_ps, blk)
                nc.vector.tensor_tensor(E[:], src, row_max[:].unsqueeze(2).broadcast_to([P, UB, T]), ALU.subtract)\
                    .then_inc(d_ready, 1)
                dve.wait_ge(e_ready, blk + 1)
                nc.vector.tensor_reduce(row_sum[:], E[:], AX.X, ALU.add).then_inc(softmax_done, 1)
                dve.wait_ge(softmax_done, done + 2)
                nc.vector.reciprocal(rsum[:], row_sum[:]).then_inc(softmax_done, 1)
                dve.wait_ge(softmax_done, done + 3)
                nc.vector.tensor_tensor(E[:], E[:], rsum[:].unsqueeze(2).broadcast_to([P, UB, T]), ALU.mult)\
                    .then_inc(en_ready, 1)
                dve.wait_ge(pv_ps, blk + 1)
                x = k.X[:, bass.ds(blk * UB, UB), :]
                nc.vector.tensor_tensor(x, PV_ps[:].rearrange("p (u c) -> p u c", u=UB), x, ALU.add).then_inc(x_done, 1)

            def prologue():
                dve.wait_ge(loaded, 16)
                nc.vector.tensor_scalar(pad[:], mask[:], 0.0, NEG, ALU.is_equal, ALU.mult).then_inc(softmax_done, 1)
                front(0)

            def step(blk, p, prev, nxt):
                if nxt:
                    front(blk + 1)
                back(blk, p)

            run_blocks(dve, NB, prologue, step, lambda: None)


MAGIC = 1.5 * 2.0 ** 23
QMAX = 127.0


def quantised_ffn_phase(nc, k):
    UB = 4
    NB = NU // UB
    TOK = UB * P
    I = k.d["L1_ffn_w_down"].shape[1]
    NC = (I + P - 1) // P
    ROWS = [min(P, I - c * P) for c in range(NC)]
    n = "q1"
    d = k.d
    with ExitStack() as ctx:
        def sb(name, shape, dt=F32):
            return ctx.enter_context(nc.sbuf_tensor(f"{n}_{name}", shape, dt))

        def ps(name, shape, dt=F32):
            return ctx.enter_context(nc.psum_tensor(f"{n}_{name}_ps", shape, dt))

        def sem(name):
            return nc.alloc_semaphore(f"{n}_{name}")

        w_rows = [sb("w_gate", [P, NC, C]), sb("w_up", [P, NC, C])]
        w_down = sb("w_down", [P, I])
        w_q = sb("w_q", [P, 2, NC, C], BF16)
        w_t = sb("w_t", [P, NC * C])
        wd_q = sb("wd_q", [P, I], BF16)
        wT = sb("wT", [P, 2, NC * P], BF16)
        wdT = sb("wdT", [P, NC, C], BF16)
        w_max = sb("w_max", [P, 2 * NC + 1])
        w_scale = sb("w_scale", [P, 2 * NC + 1])
        w_inv = sb("w_inv", [P, 2 * NC + 1])
        clip = sb("clip", [P, 2])
        sig = sb("sig", [P, 2])
        stats = sb("stats", [P, UB, 6])
        mv = sb("mv", [P, UB, 2])
        var_eps = sb("var_eps", [P, UB])
        minus_half = sb("minus_half", [P, UB])
        rstd = sb("rstd", [P, UB])
        XN = sb("XN", [P, NU, C])
        x_max = sb("x_max", [P, NB])
        h_max = sb("h_max", [P, NB * NC])
        all_max = sb("all_max", [P, 4])
        scale = sb("scale", [P, 2])
        inv = sb("inv", [P, 2])
        gu_scale = sb("gu_scale", [P, 2 * NC])
        out_scale = sb("out_scale", [P, 1])
        out_row = sb("out_row", [P, C])
        tq = sb("tq", [P, 2, NC * TOK])
        xq = sb("xq", [P, 2, TOK], BF16)
        xqT = sb("xqT", [P, 2, TOK], BF16)
        act_g = sb("act_g", [P, 2, TOK])
        HT = sb("HT", [P, NC, NB * TOK])
        hq = sb("hq", [P, 2, NC * TOK], BF16)
        y = sb("y", [P, 2, TOK])
        T_ps = ps("T", [P, 1024], BF16)
        G_ps = [ps(f"G{i}", [P, 512]) for i in range(2)]
        U_ps = [ps(f"U{i}", [P, 512]) for i in range(2)]
        D_ps = [ps(f"D{i}", [P, 512]) for i in range(2)]

        loaded = sem("loaded")
        setup = sem("setup")
        stats_done = sem("stats_done")
        var_ready = sem("var_ready")
        rstd_ready = sem("rstd_ready")
        xn_done = sem("xn_done")
        xmax_done = sem("xmax_done")
        wprep = sem("wprep")
        wq_ready = sem("wq_ready")
        wt_ps = sem("wt_ps")
        wt_ready = sem("wt_ready")
        local_max = sem("local_max")
        whole_max = sem("whole_max")
        sig_steps = sem("sig_steps")
        scale_steps = sem("scale_steps")
        gu_ready = sem("gu_ready")
        tq_done = sem("tq_done")
        xq_ready = sem("xq_ready")
        xqT_ps = sem("xqT_ps")
        xqT_ready = sem("xqT_ready")
        g_ps = sem("g_ps")
        u_ps = sem("u_ps")
        silu_ready = sem("silu_ready")
        h_done = sem("h_done")
        hmax_done = sem("hmax_done")
        row_ps = sem("row_ps")
        row_ready = sem("row_ready")
        tq2_done = sem("tq2_done")
        tq2_clipped = sem("tq2_clipped")
        hq_ready = sem("hq_ready")
        d_ps = sem("d_ps")
        y_scaled = sem("y_scaled")
        y_ready = sem("y_ready")
        stored = [sem("stored0"), sem("stored1")]
        passed = sem("passed")
        out_d = k.out.rearrange("(u r) t d -> (r t) u d", r=2)

        block = ctx.enter_context(nc.Block())

        def later(blk, least):
            return not isinstance(blk, int) or blk >= least

        def pairs(eng, body):
            body(0, 0)
            body(1, 1)
            with eng.Fori(1, NB // 2) as i:
                body(i * 2, 0)
                body(i * 2 + 1, 1)

        @block.sync
        def _(sp):
            sp.wait_ge(setup, 3)
            for w, name in zip(w_rows, ("L1_ffn_w_gate", "L1_ffn_w_up")):
                for c in range(NC):
                    sp.dma_start(w[0:ROWS[c], c, :], d[name][c * P:c * P + ROWS[c], :]).then_inc(loaded, 16)
            sp.dma_start(w_down[:], d["L1_ffn_w_down"]).then_inc(loaded, 16)
            sp.dma_start(clip[:], d["L1_ffn_clips"]).then_inc(loaded, 16)

            def store(blk, p):
                wait_here(sp, y_ready, blk + 1, passed)
                sp.dma_start(out_d[:, bass.ds(blk * UB, UB), :], y[:, p, :].rearrange("p (u c) -> p u c", c=C))\
                    .then_inc(stored[p], 16)

            pairs(sp, store)
            for q in stored:
                sp.wait_ge(q, 16 * NB // 2)

        @block.gpsimd
        def _(pool):
            for w in w_rows:
                nc.gpsimd.memset(w[:], 1.0).then_inc(setup, 1)
            nc.gpsimd.memset(h_max[:], 0.0).then_inc(setup, 1)
            nc.gpsimd.memset(minus_half[:], -0.5).then_inc(setup, 1)
            pool.wait_ge(setup, 4)
            nc.gpsimd.memset(HT[ROWS[-1]:P, NC - 1, :], 0.0).then_inc(setup, 1)
            pool.wait_ge(setup, 5)
            with pool.Fori(0, NB) as nb:
                pool.wait_ge(var_ready, nb + 1)
                nc.gpsimd.tensor_tensor(rstd[:], var_eps[:], minus_half[:], ALU.pow).then_inc(rstd_ready, 1)
            for i in range(2):
                pool.wait_ge(local_max, i + 1)
                nc.gpsimd.partition_all_reduce(all_max[:, 2 * i + 1:2 * i + 2], all_max[:, 2 * i:2 * i + 1], P,
                                               bass.bass_isa.ReduceOp.max).then_inc(whole_max, 1)

        @block.tensor
        def _(pe):
            pe.wait_ge(wq_ready, 1)
            for c in range(2 * NC):
                if c >= 4:
                    pe.wait_ge(wt_ready, 1)
                mm = nc.tensor.transpose(T_ps[:, (c % 4) * P:(c % 4 + 1) * P], w_q[:, c // NC, c % NC, :], k.identb[:])
                if c == 3:
                    mm.then_inc(wt_ps, 1)
            mm.then_inc(wt_ps, 1)
            pe.wait_ge(wt_ready, 2)
            for c in range(NC):
                mm = nc.tensor.transpose(T_ps[0:ROWS[c], c * P:(c + 1) * P], wd_q[:, c * P:c * P + ROWS[c]], k.identb[:])
            mm.then_inc(wt_ps, 1)
            pe.wait_ge(wt_ready, 3)

            def up(blk, p):
                pe.wait_ge(xq_ready, blk + 1)
                if later(blk, 1):
                    pe.wait_ge(xqT_ready, blk)
                for u in range(UB):
                    mm = nc.tensor.transpose(T_ps[:, u * P:(u + 1) * P], xq[:, p, u * P:(u + 1) * P], k.identb[:])
                mm.then_inc(xqT_ps, 1)
                pe.wait_ge(xqT_ready, blk + 1)
                for c in range(NC):
                    n_ = blk * NC + c
                    r = (p * NC + c) % 2
                    if later(n_, 2):
                        pe.wait_ge(h_done, n_ - 1)
                    nc.tensor.matmul(G_ps[r][0:ROWS[c], :], wT[:, 0, c * P:c * P + ROWS[c]], xqT[:, p, :],
                                     start=True, stop=True).then_inc(g_ps, 1)
                    nc.tensor.matmul(U_ps[r][0:ROWS[c], :], wT[:, 1, c * P:c * P + ROWS[c]], xqT[:, p, :],
                                     start=True, stop=True).then_inc(u_ps, 1)

            pairs(pe, up)
            pe.wait_ge(scale_steps, 5)
            nc.tensor.matmul(D_ps[0][:, 0:C], out_scale[:, 0:1].broadcast_to([P, P]), k.ident[:], start=True, stop=True)\
                .then_inc(row_ps, 1)
            pe.wait_ge(row_ready, 1)

            def down(blk, p):
                pe.wait_ge(hq_ready, blk + 1)
                if later(blk, 2):
                    pe.wait_ge(y_scaled, blk - 1)
                for u in range(UB):
                    for c in range(NC):
                        mm = nc.tensor.matmul(D_ps[p][:, u * C:(u + 1) * C],
                                              hq[0:ROWS[c], p, c * TOK + u * P:c * TOK + (u + 1) * P],
                                              wdT[0:ROWS[c], c, :], start=(c == 0), stop=(c == NC - 1))
                mm.then_inc(d_ps, 1)

            pairs(pe, down)

        @block.scalar
        def _(act):
            act.wait_ge(loaded, 16 * (2 * NC + 2))
            nc.scalar.activation(sig[:], clip[:], ACT.Exp, scale=-1.0).then_inc(sig_steps, 1)
            act.wait_ge(wt_ps, 1)
            nc.scalar.activation(wT[:].rearrange("p g n -> p (g n)")[:, 0:4 * P], T_ps[:, 0:4 * P], ACT.Copy).then_inc(wt_ready, 1)
            act.wait_ge(wt_ps, 2)
            nc.scalar.activation(wT[:].rearrange("p g n -> p (g n)")[:, 4 * P:6 * P], T_ps[:, 0:2 * P], ACT.Copy).then_inc(wt_ready, 1)
            act.wait_ge(wt_ps, 3)
            for c in range(NC):
                last = nc.scalar.activation(wdT[0:ROWS[c], c, :], T_ps[0:ROWS[c], c * P:(c + 1) * P], ACT.Copy)
            last.then_inc(wt_ready, 1)
            act.wait_ge(gu_ready, 1)

            def up(blk, p):
                act.wait_ge(tq_done, blk * 2 + 2)
                if later(blk, 2):
                    act.wait_ge(xqT_ps, blk - 1)
                nc.scalar.activation(xq[:, p, :], tq[:, p, 0:TOK], ACT.Copy, bias=-MAGIC).then_inc(xq_ready, 1)
                act.wait_ge(xqT_ps, blk + 1)
                if later(blk, 2):
                    act.wait_ge(u_ps, (blk - 1) * NC)
                nc.scalar.activation(xqT[:, p, :], T_ps[:, 0:TOK], ACT.Copy).then_inc(xqT_ready, 1)
                for c in range(NC):
                    n_ = blk * NC + c
                    r = (p * NC + c) % 2
                    act.wait_ge(g_ps, n_ + 1)
                    if later(n_, 2):
                        act.wait_ge(h_done, n_ - 1)
                    nc.scalar.activation(act_g[0:ROWS[c], r, :], G_ps[r][0:ROWS[c], :], ACT.Silu,
                                         scale=gu_scale[0:ROWS[c], c:c + 1]).then_inc(silu_ready, 1)

            pairs(act, up)

            def down(blk, p):
                act.wait_ge(tq2_clipped, blk + 1)
                if later(blk, 2):
                    act.wait_ge(d_ps, blk - 1)
                nc.scalar.activation(hq[:, p, :], tq[:, p, :], ACT.Copy, bias=-MAGIC).then_inc(hq_ready, 1)

            act.wait_ge(scale_steps, 5)
            pairs(act, down)

        @block.vector
        def _(dve):
            step_no = [0]

            def chained(ins):
                step_no[0] += 1
                ins.then_inc(wprep, 1)
                dve.wait_ge(wprep, step_no[0])

            dve.wait_ge(loaded, 16 * (2 * NC + 2))
            for g in range(2):
                nc.vector.tensor_reduce(w_max[:, g * NC:(g + 1) * NC], w_rows[g][:], AX.X, ALU.max, apply_absolute_value=True)
            chained(nc.vector.tensor_reduce(w_max[:, 2 * NC:2 * NC + 1], w_down[:], AX.X, ALU.max, apply_absolute_value=True))
            chained(nc.vector.tensor_scalar(w_scale[:], w_max[:], 1.0 / QMAX, None, ALU.mult))
            chained(nc.vector.reciprocal(w_inv[:], w_scale[:]))
            for g in range(2):
                t3 = w_t[:].rearrange("p (c n) -> p c n", n=C)
                chained(nc.vector.tensor_tensor(t3, w_rows[g][:], w_inv[:, g * NC:(g + 1) * NC].unsqueeze(2)
                                                .broadcast_to([P, NC, C]), ALU.mult))
                chained(nc.vector.tensor_scalar(w_t[:], w_t[:], MAGIC, MAGIC - QMAX - 1.0, ALU.add, ALU.max))
                chained(nc.vector.tensor_scalar(w_q[:, g].rearrange("p c n -> p (c n)"), w_t[:], MAGIC + QMAX, MAGIC,
                                                ALU.min, ALU.subtract))
            chained(nc.vector.tensor_scalar(w_t[:, 0:I], w_down[:], w_inv[:, 2 * NC:2 * NC + 1], MAGIC, ALU.mult, ALU.add))
            chained(nc.vector.tensor_scalar(w_t[:, 0:I], w_t[:, 0:I], MAGIC - QMAX - 1.0, MAGIC + QMAX, ALU.max, ALU.min))
            nc.vector.tensor_scalar(wd_q[:], w_t[:, 0:I], MAGIC, None, ALU.subtract).then_inc(wq_ready, 1)
            dve.wait_ge(sig_steps, 1)
            chained(nc.vector.tensor_scalar(sig[:], sig[:], 1.0, None, ALU.add))
            chained(nc.vector.reciprocal(sig[:], sig[:]))

            dve.wait_ge(setup, 5)
            with dve.Fori(0, NB) as nb:
                for u in range(UB):
                    last = nc.vector.bn_stats(stats[:, u, :], k.X[:, nb * UB + u, :])
                last.then_inc(stats_done, 1)
                wait_here(dve, stats_done, nb * 2 + 1, passed)
                for u in range(UB):
                    last = nc.vector.bn_aggr(mv[:, u, :], stats[:, u, :])
                last.then_inc(stats_done, 1)
                dve.wait_ge(stats_done, nb * 2 + 2)
                nc.vector.tensor_scalar(var_eps[:], mv[:, :, 1], EPS, None, ALU.add).then_inc(var_ready, 1)
                dve.wait_ge(rstd_ready, nb + 1)
                for u in range(UB):
                    last = nc.vector.tensor_scalar(XN[:, nb * UB + u, :], k.X[:, nb * UB + u, :], mv[:, u, 0:1],
                                                   rstd[:, u:u + 1], ALU.subtract, ALU.mult)
                last.then_inc(xn_done, 1)
                dve.wait_ge(xn_done, nb + 1)
                nc.vector.tensor_reduce(x_max[:, bass.ds(nb, 1)], XN[:, bass.ds(nb * UB, UB), :].rearrange("p u c -> p (u c)"),
                                        AX.X, ALU.max, apply_absolute_value=True).then_inc(xmax_done, 1)
            dve.wait_ge(xmax_done, NB)

            def find_scale(i, maxima):
                nc.vector.tensor_reduce(all_max[:, 2 * i:2 * i + 1], maxima[:], AX.X, ALU.max).then_inc(local_max, 1)
                dve.wait_ge(whole_max, i + 1)
                nc.vector.tensor_scalar(scale[:, i:i + 1], all_max[:, 2 * i + 1:2 * i + 2], sig[:, i:i + 1], 1.0 / QMAX,
                                        ALU.mult, ALU.mult).then_inc(scale_steps, 1)
                dve.wait_ge(scale_steps, 2 * i + 1)
                nc.vector.reciprocal(inv[:, i:i + 1], scale[:, i:i + 1]).then_inc(scale_steps, 1)
                dve.wait_ge(scale_steps, 2 * i + 2)

            find_scale(0, x_max)
            nc.vector.tensor_scalar(gu_scale[:], w_scale[:, 0:2 * NC], scale[:, 0:1], None, ALU.mult)\
                .then_inc(gu_ready, 1)
            dve.wait_ge(gu_ready, 1)

            def quantise_x(blk, p):
                if later(blk, 2):
                    dve.wait_ge(xq_ready, blk - 1)
                t = tq[:, p, 0:TOK]
                nc.vector.tensor_scalar(t, XN[:, bass.ds(blk * UB, UB), :].rearrange("p u c -> p (u c)"), inv[:, 0:1], MAGIC,
                                        ALU.mult, ALU.add).then_inc(tq_done, 1)
                dve.wait_ge(tq_done, blk * 2 + 1)
                nc.vector.tensor_scalar(t, t, MAGIC - QMAX - 1.0, MAGIC + QMAX, ALU.max, ALU.min).then_inc(tq_done, 1)

            def hidden(blk, p):
                for c in range(NC):
                    n_ = blk * NC + c
                    r = (p * NC + c) % 2
                    h = HT[0:ROWS[c], c, bass.ds(blk * TOK, TOK)]
                    dve.wait_ge(u_ps, n_ + 1)
                    dve.wait_ge(silu_ready, n_ + 1)
                    nc.vector.scalar_tensor_tensor(out=h, in0=U_ps[r][0:ROWS[c], :],
                                                   scalar=gu_scale[0:ROWS[c], NC + c:NC + c + 1],
                                                   in1=act_g[0:ROWS[c], r, :], op0=ALU.mult, op1=ALU.mult).then_inc(h_done, 1)
                    dve.wait_ge(h_done, n_ + 1)
                    nc.vector.tensor_reduce(h_max[0:ROWS[c], bass.ds(n_, 1)], h, AX.X, ALU.max, apply_absolute_value=True)\
                        .then_inc(hmax_done, 1)

            def up(blk, p):
                quantise_x(blk + 1, 1 - p)
                hidden(blk, p)

            quantise_x(0, 0)
            up(0, 0)
            up(1, 1)
            with dve.Fori(1, NB // 2 - 1) as i:
                up(i * 2, 0)
                up(i * 2 + 1, 1)
            up(NB - 2, 0)
            hidden(NB - 1, 1)
            dve.wait_ge(hmax_done, NB * NC)
            find_scale(1, h_max)
            nc.vector.tensor_scalar(out_scale[:], w_scale[:, 2 * NC:2 * NC + 1], scale[:, 1:2], None, ALU.mult)\
                .then_inc(scale_steps, 1)
            dve.wait_ge(scale_steps, 5)
            dve.wait_ge(row_ps, 1)
            nc.vector.tensor_copy(out_row[:], D_ps[0][:, 0:C]).then_inc(row_ready, 1)
            dve.wait_ge(row_ready, 1)

            def quantise_h(blk, p):
                t = tq[:, p, :]
                if later(blk, 2):
                    dve.wait_ge(hq_ready, blk - 1)
                for c in range(NC):
                    last = nc.vector.tensor_scalar(tq[:, p, c * TOK:(c + 1) * TOK], HT[:, c, bass.ds(blk * TOK, TOK)],
                                                   inv[:, 1:2], MAGIC, ALU.mult, ALU.add)
                last.then_inc(tq2_done, 1)
                dve.wait_ge(tq2_done, blk + 1)
                nc.vector.tensor_scalar(t, t, MAGIC - QMAX - 1.0, MAGIC + QMAX, ALU.max, ALU.min).then_inc(tq2_clipped, 1)

            def output(blk, p):
                dve.wait_ge(d_ps, blk + 1)
                if later(blk, 2):
                    dve.wait_ge(stored[p], (blk // 2) * 16)
                y3 = y[:, p, :].rearrange("p (u c) -> p u c", c=C)
                nc.vector.tensor_tensor(y3, D_ps[p][:].rearrange("p (u c) -> p u c", c=C),
                                        out_row[:].unsqueeze(1).broadcast_to([P, UB, C]), ALU.mult).then_inc(y_scaled, 1)
                dve.wait_ge(y_scaled, blk + 1)
                nc.vector.tensor_tensor(y3, y3, k.X[:, bass.ds(blk * UB, UB), :], ALU.add).then_inc(y_ready, 1)

            def down(blk, p):
                quantise_h(blk + 1, 1 - p)
                output(blk, p)

            quantise_h(0, 0)
            down(0, 0)
            down(1, 1)
            with dve.Fori(1, NB // 2 - 1) as i:
                down(i * 2, 0)
                down(i * 2 + 1, 1)
            down(NB - 2, 0)
            output(NB - 1, 1)


def store_phase(nc, k):
    with ExitStack() as ctx:
        stored = nc.alloc_semaphore("stored")
        block = ctx.enter_context(nc.Block())

        @block.sync
        def _(sp):
            sp.dma_start(k.out.rearrange("(u r) t d -> (r t) u d", r=2), k.X[:]).then_inc(stored, 16)
            sp.wait_ge(stored, 16)


TEST = ""


def decoder_kernel(nc, dram, out):
    k = Core()
    k.d = dram
    k.out = out
    with ExitStack() as ctx:
        def sb(name, shape, dt=F32):
            return ctx.enter_context(nc.sbuf_tensor(name, shape, dt))

        k.X = sb("X", [P, NU, C])
        k.ident = sb("ident", [P, P])
        k.ones_row = sb("ones_row", [1, 512])
        k.causal_queries = sb("causal_queries", [P, P], BF16)
        k.causal_keys = sb("causal_keys", [P, 512], BF16)
        k.identb = sb("identb", [P, P], BF16)
        k.of_batch = sb("of_batch", [2, P], BF16)
        k.gates = sb("gates", [P, 2, NU])
        k.slots = sb("slots", [P, 2, NU], I32)
        k.xn_rows = nc.dram_tensor("xn_rows", (NU * P, C), F32, kind="Internal").ap()
        k.slot_out = nc.dram_tensor("slot_out", ((2 * NU + 8) * P, C), F32, kind="Internal").ap()
        run_phase(nc, load_phase, k)
        phases = TEST or "abcdef"
        if "a" in phases: run_phase(nc, narrow_attention_phase, k, cross=False)
        if "b" in phases: run_phase(nc, narrow_attention_phase, k, cross=True)
        if "c" in phases: mixture_phases(nc, k)
        if "d" in phases: run_phase(nc, wide_attention_phase, k)
        if "e" in phases: run_phase(nc, masked_attention_phase, k)
        if "f" in phases:
            run_phase(nc, quantised_ffn_phase, k)
        else:
            run_phase(nc, store_phase, k)


def constants():
    t = np.arange(T)
    inv_freq = np.float32(1.0) / np.float32(10000.0) ** (np.arange(0, 64, 2, dtype=np.float32) / np.float32(64))
    angle = inv_freq[:, None] * t.astype(np.float32)[None, :]
    return {
        "c_ident": np.eye(P, dtype=np.float32),
        "c_upper": np.triu(np.ones((P, P), np.float32), 1),
        "c_ones": np.ones((P, P), np.float32),
        "c_rank": np.tile(8.0 - np.arange(8, dtype=np.float32), (P, 1)),
        "c_tile_no": np.tile(np.arange(2 * NU + 8, dtype=np.float32), (P, 1)),
        "c_row_no": np.tile(np.arange(P, dtype=np.float32), (P, 1)),
        "c_token_no": (np.arange(NU)[None, None, :] * P + np.arange(P)[:, None, None]).astype(np.float32),
        "c_of_batch": (np.arange(P)[None, :] // T == np.arange(2)[:, None]).astype(np.float32),
        "c_ones_row": np.ones((1, 512), np.float32),
        "c_causal_queries": np.tile(np.eye(T), (2, 2)).astype(np.float32),
        "c_causal_keys": np.tile(np.where(t[None, :] > t[:, None], NEG, 0.0), (2, 8)).astype(np.float32),
        "c_cos": np.tile(np.cos(angle), (4, 1)).astype(np.float32),
        "c_sin": np.tile(np.sin(angle), (4, 1)).astype(np.float32),
        "c_narrow_parity": (np.arange(P)[:, None] // D0 % 2 == np.arange(2)[None, :]).astype(np.float32),
        "c_of_head": (np.arange(P)[:, None] % 64 // D0 == np.arange(H // 2)[None, :]).astype(np.float32),
        "c_parity": (np.arange(P)[:, None] // 32 % 2 == np.arange(2)[None, :]).astype(np.float32),
    }


def laid_out(inputs):
    a = {name: np.asarray(v) for name, v in inputs.items()}
    f = {"x": a["x"], "ctxT": a["ctx_1024"].reshape(B * T, C).T,
         "ctxK": a["ctx_1024"].transpose(1, 0, 2), "mask": a["mask_BxS2_ik1"].reshape(NU, 2, T).transpose(1, 0, 2).reshape(2, NU * T)}
    for n in ("w_gate", "w_up", "w_down"):
        f[f"L1_ffn_{n}"] = a[f"L1_ffn_{n}"]
    f["L1_ffn_clips"] = np.broadcast_to(np.stack([a["L1_ffn_clip_x"], a["L1_ffn_clip_down"]], 1), (P, 2))
    qkv = a["L0_attn_W_qkv"]
    for i, n in enumerate("qkv"):
        f[f"L0_attn_w{n}T"] = qkv[i * C:(i + 1) * C].T
        f[f"L0_xattn_w{n}T"] = a[f"L0_xattn_W{n}"].T
    f["L0_attn_woT"] = a["L0_attn_W_proj"].T
    f["L0_xattn_woT"] = a["L0_xattn_Wo"].T
    for n in ("bq", "bk"):
        f[f"L0_xattn_{n}"] = a[f"L0_xattn_{n}"].reshape(C, 1)
    for n in ("bv", "bo"):
        f[f"L0_xattn_{n}"] = a[f"L0_xattn_{n}"].reshape(1, C)
    f["L0_xattn_temp"] = np.repeat(a["L0_xattn_temperature"].reshape(H), D0).reshape(C, 1)
    f["L0_ffn_router_w"] = a["L0_ffn_router_w"].T
    f["L0_ffn_router_b"] = a["L0_ffn_router_b"].reshape(1, 8)
    for n in ("gate_w", "up_w"):
        f[f"L0_ffn_{n}"] = a[f"L0_ffn_{n}"].transpose(2, 0, 1).reshape(C, -1)
    f["L0_ffn_down_w"] = a["L0_ffn_down_w"].reshape(8, C, 4, P).transpose(3, 0, 2, 1).reshape(P, -1)
    for n in "qk":
        f[f"L1_attn_w{n}"] = a[f"L1_attn_W{n}"].reshape(C, 4, 4, 32, 2).transpose(0, 1, 4, 2, 3).reshape(C, 4, 2, P)
    f["L1_attn_wv"] = a["L1_attn_Wv"].reshape(C, 4, 256)
    f["L1_attn_wo"] = a["L1_attn_Wo"].reshape(4, 2, 2, 64, C).transpose(1, 3, 0, 2, 4).reshape(P, 4, 2, C)
    f["L1_attn_bo"] = a["L1_attn_bo"].reshape(1, C)
    return f


def kernel(**inputs):
    import concourse.bacc as _bacc
    from concourse.bass_utils import run_bass_kernel_spmd as _run

    nc = _bacc.Bacc("TRN2", target_bir_lowering=False, num_devices=1)
    arrays, dram = {}, {}
    for name, a in {**laid_out(inputs), **constants()}.items():
        a = np.ascontiguousarray(a)
        arrays[f"in_{name}"] = a
        dram[name] = nc.dram_tensor(f"in_{name}", a.shape, mybir.dt.from_np(a.dtype), kind="ExternalInput").ap()
    out = nc.dram_tensor("out_x", (B, T, C), F32, kind="ExternalOutput").ap()
    decoder_kernel(nc, dram, out)
    r = _run(nc, [arrays], core_ids=[0])
    return r.results[0]["out_x"]
```

```python
from contextlib import ExitStack

import numpy as np

import concourse.bass as bass
from concourse import mybir

P = 128
B, T, C = 64, 64, 128
NU = B * T // P
H = 16
D0 = C // H
EPS = 1e-5
NEG = -1e30

F32 = mybir.dt.float32
BF16 = mybir.dt.bfloat16
I32 = mybir.dt.int32
ALU = mybir.AluOpType
ACT = mybir.ActivationFunctionType
AX = mybir.AxisListType


class Core:
    pass


def run_blocks(eng, n_blocks, prologue, step, epilogue):
    prologue()
    step(0, 0, prev=False, nxt=True)
    with eng.Fori(0, n_blocks // 2 - 1) as i:
        step(i * 2 + 1, 1, prev=True, nxt=True)
        step(i * 2 + 2, 0, prev=True, nxt=True)
    step(n_blocks - 1, (n_blocks - 1) % 2, prev=True, nxt=False)
    epilogue()


def run_blocks_far(eng, n_blocks, prologue, step, epilogue):
    prologue()
    step(0, 0, prev=False, nxt=2)
    with eng.Fori(0, n_blocks // 2 - 2) as i:
        step(i * 2 + 1, 1, prev=True, nxt=2)
        step(i * 2 + 2, 0, prev=True, nxt=2)
    for blk in range(n_blocks - 3, n_blocks):
        step(blk, blk % 2, prev=True, nxt=min(2, n_blocks - 1 - blk))
    epilogue()


def wait_here(eng, sem, value, passed):
    eng.wait_ge(sem, value)
    eng.sem_inc(passed, 1)


def all_statistics(nc, dve, k, stats, mv, var_eps, stats_done, var_ready):
    for reads, write in ((k.X, lambda u: nc.vector.bn_stats(stats[:, u, :], k.X[:, u, :])),
                         (stats, lambda u: nc.vector.bn_aggr(mv[:, u, :], stats[:, u, :]))):
        for u in range(NU):
            last = write(u)
        last.then_inc(stats_done, 1)
        dve.wait_ge(stats_done, 1 if reads is k.X else 2)
    nc.vector.tensor_scalar(var_eps[:], mv[:, :, 1], EPS, None, ALU.add).then_inc(var_ready, 1)


def run_phase(nc, phase, *args, **named):
    with nc.cleanup_on_exit():
        phase(nc, *args, **named)


def load_phase(nc, k):
    with ExitStack() as ctx:
        staged_in = nc.alloc_semaphore("staged_in")
        narrowed = [(dst, ctx.enter_context(nc.sbuf_tensor(f"staged_{name}", list(dst.shape), F32)), name)
                    for dst, name in ((k.causal_keys, "c_causal_keys"), (k.causal_queries, "c_causal_queries"),
                                      (k.identb, "c_ident"), (k.of_batch, "c_of_batch"))]
        block = ctx.enter_context(nc.Block())

        @block.sync
        def _(sp):
            for _, staged, name in narrowed:
                sp.dma_start(staged[:], k.d[name]).then_inc(staged_in, 16)
            sp.dma_start(k.ident[:], k.d["c_ident"]).then_inc(k.loaded, 16)
            sp.dma_start(k.ones_row[:], k.d["c_ones_row"]).then_inc(k.loaded, 16)
            sp.dma_start(k.X[:], k.d["x"].rearrange("(u r) t d -> (r t) u d", r=2)).then_inc(k.loaded, 16)

        @block.vector
        def _(dve):
            dve.wait_ge(staged_in, 16 * len(narrowed))
            for dst, staged, _ in narrowed:
                nc.vector.tensor_copy(dst[:], staged[:])


def narrow_attention_phase(nc, k, cross):
    UB = 4
    NB = NU // UB
    BB = 2 * UB
    TOK = UB * P
    HALF = H // 2
    PAIRS = HALF // 2
    QUADS = H // 4
    ROWS = 2 * H // 2
    POOL_ROWS = 8
    LAG = 2
    QW = 2 * 2 * D0
    n = "x0" if cross else "a0"
    d = k.d
    with ExitStack() as ctx:
        def sb(name, shape, dt=F32):
            return ctx.enter_context(nc.sbuf_tensor(f"{n}_{name}", shape, dt))

        def ps(name, shape):
            return ctx.enter_context(nc.psum_tensor(f"{n}_{name}_ps", shape, F32))

        def sem(name):
            return nc.alloc_semaphore(f"{n}_{name}")

        wq = sb("wq", [P, C])
        wk = sb("wk", [P, C])
        wv = sb("wv", [P, C])
        wo = sb("wo", [P, C])
        wo_of = sb("wo_of", [P, 2, C])
        parity = sb("parity", [P, 2])
        bq = sb("bq", [P, 1])
        bk = sb("bk", [P, 1])
        bv = sb("bv", [1, C])
        bo = sb("bo", [1, C])
        temp = sb("temp", [P, 1])
        qscale = sb("qscale", [P, 1])
        of_head = sb("of_head", [P, HALF])
        q_factor = sb("q_factor", [P, HALF])
        q_offset = sb("q_offset", [P, HALF])
        ctxT = sb("ctxT", [P, 2, TOK])
        stats = sb("stats", [P, UB, 6])
        mv = sb("mv", [P, UB, 2])
        var_eps = sb("var_eps", [P, UB])
        minus_half = sb("minus_half", [P, UB])
        rstd = sb("rstd", [P, UB])
        xn = sb("xn", [P, UB, C])
        xnT = sb("xnT", [P, TOK])
        QX = sb("QX", [P, 2, BB, HALF * T])
        KT = sb("KT", [P, 2, TOK])
        V = sb("V", [P, 2, BB, QUADS * (P + QW)])
        row_max = sb("row_max", [P, 2, ROWS])
        E = sb("E", [P, 2, ROWS * T])
        ET = sb("ET", [P, 2, ROWS * T])
        row_sum = sb("row_sum", [P, ROWS])
        rsum = sb("rsum", [P, 2, ROWS])
        OT = sb("OT", [P, 2, 2, TOK])
        S_ps = [ps(f"S{i}", [P, 2, 512]) for i in range(2)]
        ET_ps = ps("ET", [P, 2 * 512])
        PV_ps = ps("PV", [P, 512])
        G_ps = ps("G", [P, 512])

        weights = sem("weights")
        ctx_in = [sem("ctx_in0"), sem("ctx_in1")]
        setup = sem("setup")
        wo_split = sem("wo_split")
        stats_done = sem("stats_done")
        max_done = sem("max_done")
        sum_done = sem("sum_done")
        q_tables = sem("q_tables")
        var_ready = sem("var_ready")
        rstd_ready = sem("rstd_ready")
        xn_ready = sem("xn_ready")
        xnT_ps = sem("xnT_ps")
        xnT_ready = sem("xnT_ready")
        q_ps = sem("q_ps")
        k_ps = sem("k_ps")
        v_ps = sem("v_ps")
        qx_ready = sem("qx_ready")
        kT_ready = sem("kT_ready")
        v_ready = sem("v_ready")
        s_ps = sem("s_ps")
        d_ready = sem("d_ready")
        e_ready = sem("e_ready")
        rsum_ready = sem("rsum_ready")
        en_ready = sem("en_ready")
        en_dve = sem("en_dve")
        et_ps = sem("et_ps")
        et_ready = sem("et_ready")
        pv_ps = sem("pv_ps")
        ot_ready = sem("ot_ready")
        y_ps = sem("y_ps")
        x_done = sem("x_done")
        passed = sem("passed")
        N_WEIGHTS = 11 if cross else 6
        Q_TABLES = 4 if cross else 0

        block = ctx.enter_context(nc.Block())

        def later(number, least):
            return not isinstance(number, int) or number >= least

        def ahead(blk, u, p, by):
            return (blk, u + by, p) if u + by < UB else (blk + 1, u + by - UB, 1 - p)

        @block.sync
        def _(sp):
            w = "L0_xattn_" if cross else "L0_attn_"
            names = [(wq, w + "wqT"), (wk, w + "wkT"), (wv, w + "wvT"), (wo, w + "woT"), (of_head, "c_of_head"),
                     (parity, "c_narrow_parity")]
            if cross:
                names += [(t, w + name) for t, name in ((bq, "bq"), (bk, "bk"), (bv, "bv"), (bo, "bo"), (temp, "temp"))]
            for dst, name in names:
                sp.dma_start(dst[:], d[name]).then_inc(weights, 16)

            def load_ctx(nb, p):
                if cross:
                    sp.dma_start(ctxT[:, p, :], d["ctxT"][:, bass.ds(nb * TOK, TOK)]).then_inc(ctx_in[p], 16)

            def step(blk, p, prev, nxt):
                if nxt and cross:
                    if prev:
                        wait_here(sp, v_ps, blk, passed)
                    load_ctx(blk + 1, 1 - p)

            run_blocks_far(sp, NB, lambda: load_ctx(0, 0), step, lambda: None)

        @block.gpsimd
        def _(pool):
            def power(nb):
                pool.wait_ge(var_ready, nb + 1)
                nc.gpsimd.tensor_tensor(rstd[:], var_eps[:], minus_half[:], ALU.pow).then_inc(rstd_ready, 1)

            def normalise_e(blk, u):
                pool.wait_ge(rsum_ready, blk * UB + u + 1)
                e = E[:, u % 2, 0:POOL_ROWS * T].rearrange("p (r t) -> p r t", t=T)
                r = rsum[:, u % 2, 0:POOL_ROWS].unsqueeze(2).broadcast_to([P, POOL_ROWS, T])
                nc.gpsimd.tensor_tensor(e, e, r, ALU.mult).then_inc(en_ready, 1)

            def prologue():
                nc.gpsimd.memset(minus_half[:], -0.5).then_inc(setup, 1)
                pool.wait_ge(setup, 1)
                power(0)
                pool.wait_ge(rstd_ready, 1)
                nc.gpsimd.memset(V[:], 0.0).then_inc(setup, 1)
                pool.wait_ge(setup, 2)
                power(1)
                normalise_e(0, 0)
                normalise_e(0, 1)

            def step(blk, p, prev, nxt):
                for u in range(UB):
                    if u + LAG < UB or nxt:
                        normalise_e(*ahead(blk, u, p, LAG)[:2])
                    if u == 2 and nxt == 2:
                        power(blk + 2)

            run_blocks_far(pool, NB, prologue, step, lambda: None)

        @block.tensor
        def _(pe):
            def transpose_x(nb):
                pe.wait_ge(xn_ready, nb + 1)
                if later(nb, 1):
                    pe.wait_ge(v_ready, nb)
                for u in range(UB):
                    mm = nc.tensor.transpose(G_ps[:, u * P:(u + 1) * P], xn[:, u, :], k.ident[:])
                mm.then_inc(xnT_ps, 1)

            def project_q(nb):
                pe.wait_ge(xnT_ready, nb + 1)
                nc.tensor.matmul(G_ps[:], wq[:], xnT[:], start=True, stop=True).then_inc(q_ps, 1)

            def project_k(nb, p):
                if cross:
                    pe.wait_ge(ctx_in[p], (nb // 2 + 1) * 16)
                pe.wait_ge(qx_ready, nb + 1)
                src = ctxT[:, p, :] if cross else xnT[:]
                nc.tensor.matmul(G_ps[:], wk[:], src, start=True, stop=True).then_inc(k_ps, 1)

            def project_v(nb, p):
                pe.wait_ge(kT_ready, nb + 1)
                for u in range(UB):
                    src = ctxT[:, p, u * P:(u + 1) * P] if cross else xnT[:, u * P:(u + 1) * P]
                    out = G_ps[:, u * P:(u + 1) * P]
                    mm = nc.tensor.matmul(out, src, wv[:], start=True, stop=not cross)
                    if cross:
                        mm = nc.tensor.matmul(out, k.ones_row[0:1, 0:P], bv[:], start=False, stop=True)
                mm.then_inc(v_ps, 1)

            def scores(blk, u, p, b):
                n_ = blk * UB + u
                if u == 0 and b == 0:
                    pe.wait_ge(qx_ready, blk + 1)
                    pe.wait_ge(kT_ready, blk + 1)
                if b == 0 and (later(blk, 1) or u >= 2):
                    pe.wait_ge(d_ready, n_ - 1)
                rows = [slice(64 * r, 64 * r + 64) for r in range(2)]
                bank = [S_ps[u % 2][:, r, :] for r in range(2)]
                if not cross and b == 0:
                    for r in range(2):
                        nc.tensor.matmul(bank[r], k.causal_queries[rows[r], :], k.causal_keys[rows[r], :],
                                         start=True, stop=False)
                for j in range(PAIRS):
                    for r in range(2):
                        at = (b * PAIRS + j) * T
                        token = (2 * u + b) * T
                        mm = nc.tensor.matmul(bank[r][:, at:at + T],
                                              QX[rows[r], p, 2 * u + b, 2 * j * T:2 * (j + 1) * T],
                                              KT[rows[r], p, token:token + T], start=cross,
                                              stop=cross or (b == 1 and j == PAIRS - 1))
                if b == 1:
                    mm.then_inc(s_ps, 1)

            def transpose_e(blk, u):
                n_ = blk * UB + u
                pe.wait_ge(en_ready, n_ + 1)
                pe.wait_ge(en_dve, n_ + 1)
                if later(n_, 1):
                    pe.wait_ge(et_ready, n_)
                for b in range(2):
                    for j in range(QUADS):
                        at = (b * QUADS + j) * P
                        src = (j // 2 * 2 + b) * 256 + j % 2 * P
                        mm = nc.tensor.transpose(ET_ps[:, at:at + P], E[:, u % 2, src:src + P], k.ident[:])
                mm.then_inc(et_ps, 1)

            def weigh_values(blk, u, p, b):
                n_ = blk * UB + u
                if b == 0:
                    if u == 0:
                        pe.wait_ge(v_ready, blk + 1)
                    pe.wait_ge(et_ready, n_ + 1)
                    if later(n_, 1):
                        pe.wait_ge(ot_ready, n_)
                for j in range(QUADS):
                    at = b * QUADS + j
                    mm = nc.tensor.matmul(PV_ps[:, b * P:(b + 1) * P], V[:, p, 2 * u + b, j * P:(j + 1) * P],
                                          ET[:, u % 2, at * P:(at + 1) * P], start=(j == 0), stop=(j == QUADS - 1))
                if b == 1:
                    mm.then_inc(pv_ps, 1)

            def project_o(blk, p):
                pe.wait_ge(ot_ready, (blk + 1) * UB)
                for u in range(UB):
                    out = G_ps[:, u * P:(u + 1) * P]
                    for h in range(2):
                        mm = nc.tensor.matmul(out, OT[:, p, h, u * P:(u + 1) * P], wo_of[:, h, :], start=(h == 0),
                                              stop=(h == 1 and not cross))
                    if cross:
                        mm = nc.tensor.matmul(out, k.ones_row[0:1, 0:P], bo[:], start=False, stop=True)
                mm.then_inc(y_ps, 1)

            def prologue():
                pe.wait_ge(k.loaded, 3 * 16)
                transpose_x(0)
                pe.wait_ge(weights, 16 * N_WEIGHTS)
                project_q(0)
                project_k(0, 0)
                project_v(0, 0)
                for u in range(LAG):
                    for b in range(2):
                        scores(0, u, 0, b)
                transpose_e(0, 0)
                pe.wait_ge(wo_split, 2)

            def step(blk, p, prev, nxt):
                for u in range(UB):
                    if u + LAG < UB or nxt:
                        scores(*ahead(blk, u, p, LAG), 0)
                    weigh_values(blk, u, p, 0)
                    if u + LAG < UB or nxt:
                        scores(*ahead(blk, u, p, LAG), 1)
                    if u == 3 and prev:
                        pe.wait_ge(x_done, blk)
                    if u + 1 < UB or nxt:
                        transpose_e(*ahead(blk, u, p, 1)[:2])
                    if u == 0 and nxt:
                        transpose_x(blk + 1)
                    if u == 1 and nxt:
                        project_k(blk + 1, 1 - p)
                    weigh_values(blk, u, p, 1)
                    if u == 0 and nxt:
                        project_q(blk + 1)
                    if u == 1 and nxt:
                        project_v(blk + 1, 1 - p)
                    if u == 2 and prev:
                        if nxt:
                            pe.wait_ge(v_ready, blk + 2)
                        project_o(blk - 1, 1 - p)

            def epilogue():
                project_o(NB - 1, (NB - 1) % 2)

            run_blocks_far(pe, NB, prologue, step, epilogue)

        @block.scalar
        def _(act):
            def evacuate_xT(nb):
                act.wait_ge(xnT_ps, nb + 1)
                if later(nb, 1):
                    act.wait_ge(v_ps, nb)
                nc.scalar.activation(xnT[:], G_ps[:], ACT.Copy).then_inc(xnT_ready, 1)

            def spread_q(nb, p):
                act.wait_ge(q_ps, nb + 1)
                if later(nb, 2):
                    act.wait_ge(s_ps, (nb - 1) * UB)
                src = G_ps[:].rearrange("c (b t) -> c b t", t=T)
                for h in range(HALF):
                    dst = QX[:, p, :, h * T:(h + 1) * T]
                    if cross:
                        last = nc.scalar.activation(dst, src, ACT.Identity, bias=q_offset[:, h:h + 1],
                                                    scale=q_factor[:, h:h + 1])
                    else:
                        last = nc.scalar.activation(dst, src, ACT.Copy, scale=of_head[:, h:h + 1])
                last.then_inc(qx_ready, 1)

            def evacuate_k(nb, p):
                act.wait_ge(k_ps, nb + 1)
                if later(nb, 2):
                    act.wait_ge(s_ps, (nb - 1) * UB)
                if cross:
                    nc.scalar.activation(KT[:, p, :], G_ps[:], ACT.Identity, bias=bk[:, 0:1]).then_inc(kT_ready, 1)
                else:
                    nc.scalar.activation(KT[:, p, :], G_ps[:], ACT.Copy).then_inc(kT_ready, 1)

            def evacuate_v(nb, p):
                act.wait_ge(v_ps, nb + 1)
                if later(nb, 2):
                    act.wait_ge(pv_ps, (nb - 1) * UB)
                src = G_ps[:].rearrange("p (u j r e) -> p u j r e", u=UB, j=QUADS, r=2)
                dst = V[:, p].rearrange("p (u r) (j e) -> p u r j e", r=2, j=QUADS)
                for r in range(2):
                    for j in range(2):
                        last = nc.scalar.activation(dst[64 * j:64 * j + 64, :, r, :, 2 * D0 * j:2 * D0 * (j + 1)],
                                                    src[64 * r:64 * r + 64, :, :, j, :], ACT.Copy)
                last.then_inc(v_ready, 1)

            def exponentials(blk, u):
                act.wait_ge(d_ready, blk * UB + u + 1)
                nc.scalar.activation(E[:, u % 2, :], E[:, u % 2, :], ACT.Exp,
                                     scale=1.0 if cross else float(D0) ** -0.5).then_inc(e_ready, 1)

            def evacuate_e(blk, u):
                n_ = blk * UB + u
                act.wait_ge(et_ps, n_ + 1)
                if later(blk, 1) or u >= 2:
                    act.wait_ge(pv_ps, n_ - 1)
                nc.scalar.activation(ET[:, u % 2, :], ET_ps[:], ACT.Copy).then_inc(et_ready, 1)

            def prologue():
                evacuate_xT(0)
                act.wait_ge(weights, 16 * N_WEIGHTS)
                if cross:
                    act.wait_ge(q_tables, Q_TABLES)
                spread_q(0, 0)
                evacuate_k(0, 0)
                act.wait_ge(setup, 2)
                evacuate_v(0, 0)
                for u in range(LAG):
                    exponentials(0, u)
                evacuate_e(0, 0)

            def step(blk, p, prev, nxt):
                for u in range(UB):
                    if u + 1 < UB or nxt:
                        evacuate_e(*ahead(blk, u, p, 1)[:2])
                    if u == 0 and nxt:
                        evacuate_xT(blk + 1)
                    if u == 1 and nxt:
                        evacuate_k(blk + 1, 1 - p)
                    if u + LAG < UB or nxt:
                        exponentials(*ahead(blk, u, p, LAG)[:2])
                    if u == 0 and nxt:
                        spread_q(blk + 1, 1 - p)
                    if u == 1 and nxt:
                        evacuate_v(blk + 1, 1 - p)

            run_blocks_far(act, NB, prologue, step, lambda: None)

        @block.vector
        def _(dve):
            def statistics(nb):
                for u in range(UB):
                    last = nc.vector.bn_stats(stats[:, u, :], k.X[:, nb * UB + u, :])
                last.then_inc(stats_done, 1)
                wait_here(dve, stats_done, nb * 2 + 1, passed)
                for u in range(UB):
                    last = nc.vector.bn_aggr(mv[:, u, :], stats[:, u, :])
                last.then_inc(stats_done, 1)
                dve.wait_ge(stats_done, nb * 2 + 2)
                nc.vector.tensor_scalar(var_eps[:], mv[:, :, 1], EPS, None, ALU.add).then_inc(var_ready, 1)

            def normalise(nb):
                dve.wait_ge(rstd_ready, nb + 1)
                if later(nb, 1):
                    dve.wait_ge(xnT_ps, nb)
                for u in range(UB):
                    last = nc.vector.tensor_scalar(xn[:, u, :], k.X[:, nb * UB + u, :], mv[:, u, 0:1], rstd[:, u:u + 1],
                                                   ALU.subtract, ALU.mult)
                last.then_inc(xn_ready, 1)

            def subtract_max(blk, u):
                n_ = blk * UB + u
                dve.wait_ge(s_ps, n_ + 1)
                src = S_ps[u % 2][:].rearrange("p r (j t) -> p (r j) t", t=T)
                nc.vector.tensor_reduce(row_max[:, u % 2, :], src, AX.X, ALU.max).then_inc(max_done, 1)
                dve.wait_ge(max_done, n_ + 1)
                if later(blk, 1) or u >= 2:
                    dve.wait_ge(et_ps, n_ - 1)
                nc.vector.tensor_tensor(E[:, u % 2, :].rearrange("p (j t) -> p j t", t=T), src,
                                        row_max[:, u % 2, :].unsqueeze(2).broadcast_to([P, ROWS, T]),
                                        ALU.subtract).then_inc(d_ready, 1)

            def sums(blk, u):
                n_ = blk * UB + u
                dve.wait_ge(e_ready, n_ + 1)
                nc.vector.tensor_reduce(row_sum[:], E[:, u % 2, :].rearrange("p (r t) -> p r t", t=T), AX.X, ALU.add)\
                    .then_inc(sum_done, 1)
                dve.wait_ge(sum_done, n_ + 1)
                if later(blk, 1) or u >= 2:
                    dve.wait_ge(en_ready, n_ - 1)
                nc.vector.reciprocal(rsum[:, u % 2, :], row_sum[:]).then_inc(rsum_ready, 1)
                dve.wait_ge(rsum_ready, n_ + 1)
                e = E[:, u % 2, POOL_ROWS * T:].rearrange("p (r t) -> p r t", t=T)
                r = rsum[:, u % 2, POOL_ROWS:].unsqueeze(2).broadcast_to([P, ROWS - POOL_ROWS, T])
                nc.vector.tensor_tensor(e, e, r, ALU.mult).then_inc(en_dve, 1)

            def evacuate_o(blk, u, p):
                dve.wait_ge(pv_ps, blk * UB + u + 1)
                dst = OT[:, p, :, u * P:(u + 1) * P].rearrange("c h (b t) -> c b h t", b=2)
                src = PV_ps[:, 0:2 * P].rearrange("c (b h t) -> c b h t", b=2, h=2)
                nc.vector.tensor_copy(dst, src).then_inc(ot_ready, 1)

            def add_residual(blk):
                dve.wait_ge(y_ps, blk + 1)
                x = k.X[:, bass.ds(blk * UB, UB), :]
                nc.vector.tensor_tensor(x, G_ps[:].rearrange("p (u c) -> p u c", u=UB), x, ALU.add).then_inc(x_done, 1)

            def prologue():
                dve.wait_ge(k.loaded, 3 * 16)
                statistics(0)
                normalise(0)
                dve.wait_ge(weights, 16 * N_WEIGHTS)
                if cross:
                    nc.vector.reciprocal(temp[:], temp[:]).then_inc(q_tables, 1)
                    dve.wait_ge(q_tables, 1)
                    nc.vector.tensor_scalar(qscale[:], temp[:], float(D0) ** -0.5, None, ALU.mult).then_inc(q_tables, 1)
                    dve.wait_ge(q_tables, 2)
                    nc.vector.tensor_scalar(q_factor[:], of_head[:], qscale[:, 0:1], None, ALU.mult).then_inc(q_tables, 1)
                    dve.wait_ge(q_tables, 3)
                    nc.vector.tensor_scalar(q_offset[:], q_factor[:], bq[:, 0:1], None, ALU.mult).then_inc(q_tables, 1)
                for h in range(2):
                    nc.vector.tensor_scalar(wo_of[:, h, :], wo[:], parity[:, h:h + 1], None, ALU.mult).then_inc(wo_split, 1)
                statistics(1)
                subtract_max(0, 0)
                sums(0, 0)
                subtract_max(0, 1)
                sums(0, 1)

            def step(blk, p, prev, nxt):
                for u in range(UB):
                    if u == 0 and nxt:
                        normalise(blk + 1)
                    if u == 3 and prev:
                        add_residual(blk - 1)
                    if u + LAG < UB or nxt:
                        subtract_max(*ahead(blk, u, p, LAG)[:2])
                    evacuate_o(blk, u, p)
                    if u + LAG < UB or nxt:
                        sums(*ahead(blk, u, p, LAG)[:2])
                    if u == 2 and nxt == 2:
                        statistics(blk + 2)

            run_blocks_far(dve, NB, prologue, step, lambda: add_residual(NB - 1))


def mixture_phases(nc, k):
    NE = 8
    F = 512
    FC = F // P
    NT = 2 * NU + NE
    d = k.d
    with ExitStack() as ctx:
        def sb(name, shape, dt=F32):
            return ctx.enter_context(nc.sbuf_tensor(f"m0_{name}", shape, dt))

        LG = sb("LG", [P, NU, NE])
        experts = sb("experts", [1, NT], I32)
        tokens = sb("tokens", [P, NT], I32)
        gate_w = sb("gate_w", [P, NE * F])
        up_w = sb("up_w", [P, NE * F])
        down_w = sb("down_w", [P, NE * F])
        w_loaded = nc.alloc_semaphore("m0_w_loaded")
        run_phase(nc, router_phase, k, LG, gate_w, up_w, down_w, w_loaded)
        run_phase(nc, plan_phase, k, LG, experts, tokens)
        run_phase(nc, expert_phase, k, experts, tokens, gate_w, up_w, down_w, w_loaded, NT)


def router_phase(nc, k, LG, gate_w, up_w, down_w, w_loaded):
    UB = 4
    NB = NU // UB
    NE = 8
    d = k.d
    with ExitStack() as ctx:
        def sb(name, shape, dt=F32):
            return ctx.enter_context(nc.sbuf_tensor(f"r_{name}", shape, dt))

        def sem(name):
            return nc.alloc_semaphore(f"r_{name}")

        rw = sb("rw", [P, NE])
        rb = sb("rb", [1, UB * NE])
        stats = sb("stats", [P, NU, 6])
        mv = sb("mv", [P, NU, 2])
        var_eps = sb("var_eps", [P, NU])
        minus_half = sb("minus_half", [P, NU])
        rstd = sb("rstd", [P, NU])
        xn = sb("xn", [P, 2, UB, C])
        xnT = sb("xnT", [P, 2, UB * P])
        T_ps = [ctx.enter_context(nc.psum_tensor(f"r_T{i}", [P, 512], F32)) for i in range(2)]
        L_ps = [ctx.enter_context(nc.psum_tensor(f"r_L{i}", [P, 512], F32)) for i in range(2)]

        loaded = sem("loaded")
        setup = sem("setup")
        stats_done = sem("stats_done")
        var_ready = sem("var_ready")
        rstd_ready = sem("rstd_ready")
        xn_ready = sem("xn_ready")
        kept = [sem("kept0"), sem("kept1")]
        xnT_ps = sem("xnT_ps")
        xnT_ready = sem("xnT_ready")
        l_ps = sem("l_ps")
        l_ready = sem("l_ready")
        passed = sem("passed")
        block = ctx.enter_context(nc.Block())

        def later(blk, least):
            return not isinstance(blk, int) or blk >= least

        def pairs(eng, body):
            body(0, 0)
            body(1, 1)
            with eng.Fori(1, NB // 2) as i:
                body(i * 2, 0)
                body(i * 2 + 1, 1)

        @block.sync
        def _(sp):
            sp.dma_start(rw[:], d["L0_ffn_router_w"]).then_inc(loaded, 16)
            sp.dma_start(rb[:], d["L0_ffn_router_b"]).then_inc(loaded, 16)
            for w, name in ((gate_w, "gate_w"), (up_w, "up_w"), (down_w, "down_w")):
                sp.dma_start(w[:], d[f"L0_ffn_{name}"]).then_inc(w_loaded, 16)

            def body(blk, p):
                wait_here(sp, xn_ready, blk + 1, passed)
                rows = k.xn_rows[bass.ds(blk * (UB * P), UB * P), :].rearrange("(u t) c -> t u c", t=P)
                sp.dma_start(rows, xn[:, p]).then_inc(kept[p], 16)

            pairs(sp, body)
            for q in kept:
                sp.wait_ge(q, NB // 2 * 16)

        @block.gpsimd
        def _(pool):
            nc.gpsimd.memset(minus_half[:], -0.5).then_inc(setup, 1)
            pool.wait_ge(setup, 1)
            pool.wait_ge(var_ready, 1)
            for blk in range(NB):
                b = slice(blk * UB, (blk + 1) * UB)
                nc.gpsimd.tensor_tensor(rstd[:, b], var_eps[:, b], minus_half[:, b], ALU.pow).then_inc(rstd_ready, 1)

        @block.tensor
        def _(pe):
            pe.wait_ge(loaded, 32)

            def logits(blk, p):
                pe.wait_ge(xnT_ready, blk + 1)
                if later(blk, 2):
                    pe.wait_ge(l_ready, blk - 1)
                nc.tensor.matmul(L_ps[p][:, 0:UB * NE], k.ones_row[0:1, 0:P], rb[:], start=True, stop=False)
                for u in range(UB):
                    mm = nc.tensor.matmul(L_ps[p][:, u * NE:(u + 1) * NE], xnT[:, p, u * P:(u + 1) * P], rw[:],
                                          start=False, stop=(u == UB - 1))
                mm.then_inc(l_ps, 1)

            def transpose_x(blk, p):
                pe.wait_ge(xn_ready, blk + 1)
                if later(blk, 2):
                    pe.wait_ge(xnT_ready, blk - 1)
                for u in range(UB):
                    mm = nc.tensor.transpose(T_ps[p][:, u * P:(u + 1) * P], xn[:, p, u, :], k.ident[:])
                mm.then_inc(xnT_ps, 1)

            transpose_x(0, 0)
            transpose_x(1, 1)
            logits(0, 0)
            with pe.Fori(1, NB // 2) as i:
                transpose_x(i * 2, 0)
                logits(i * 2 - 1, 1)
                transpose_x(i * 2 + 1, 1)
                logits(i * 2, 0)
            logits(NB - 1, 1)

        @block.scalar
        def _(act):
            def evacuate_xT(blk, p):
                act.wait_ge(xnT_ps, blk + 1)
                if later(blk, 2):
                    act.wait_ge(l_ps, blk - 1)
                nc.scalar.activation(xnT[:, p, :], T_ps[p][:], ACT.Copy).then_inc(xnT_ready, 1)

            def keep_logits(blk, p):
                act.wait_ge(l_ps, blk + 1)
                nc.scalar.activation(LG[:, bass.ds(blk * UB, UB), :], L_ps[p][:, 0:UB * NE].rearrange("p (u e) -> p u e", e=NE),
                                     ACT.Copy).then_inc(l_ready, 1)

            evacuate_xT(0, 0)
            evacuate_xT(1, 1)
            keep_logits(0, 0)
            with act.Fori(1, NB // 2) as i:
                evacuate_xT(i * 2, 0)
                keep_logits(i * 2 - 1, 1)
                evacuate_xT(i * 2 + 1, 1)
                keep_logits(i * 2, 0)
            keep_logits(NB - 1, 1)

        @block.vector
        def _(dve):
            all_statistics(nc, dve, k, stats, mv, var_eps, stats_done, var_ready)

            def body(blk, p):
                dve.wait_ge(rstd_ready, blk + 1)
                if later(blk, 2):
                    dve.wait_ge(xnT_ps, blk - 1)
                    dve.wait_ge(kept[p], blk // 2 * 16)
                for u in range(UB):
                    last = nc.vector.tensor_scalar(xn[:, p, u, :], k.X[:, blk * UB + u, :], mv[:, bass.ds(blk * UB + u, 1), 0:1].rearrange("p o c -> p (o c)"),
                                                   rstd[:, bass.ds(blk * UB + u, 1)],
                                                   ALU.subtract, ALU.mult)
                last.then_inc(xn_ready, 1)

            pairs(dve, body)


def plan_phase(nc, k, LG, experts, tokens):
    gates, slots = k.gates, k.slots
    NE = 8
    N = NU * NE
    NT = experts.shape[1]
    d = k.d
    with ExitStack() as ctx:
        def sb(name, shape, dt=F32):
            return ctx.enter_context(nc.sbuf_tensor(f"p_{name}", shape, dt))

        def sem(name):
            return nc.alloc_semaphore(f"p_{name}")

        upper = sb("upper", [P, P])
        ones = sb("ones", [P, P])
        rank = sb("rank", [P, NE])
        tile_no = sb("tile_no", [P, NT])
        row_no = sb("row_no", [P, P])
        token_no = sb("token_no", [P, 1, NU])
        best = sb("best", [P, 2, NU])
        eq = sb("eq", [P, NU, NE])
        who = sb("who", [P, 2, NU])
        hot = sb("hot", [P, 2, NU, NE])
        rest = sb("rest", [P, NU, NE])
        chosen = sb("chosen", [P, N])
        delta = sb("delta", [P, NU])
        ratio = sb("ratio", [P, NU])
        total = sb("total", [P, 1 + N // NE, NE])
        run = sb("run", [P, 2, N])
        place = sb("place", [P, N])
        count = sb("count", [P, NE])
        tiles_i = sb("tiles_i", [P, NE], I32)
        base = sb("base", [P, 2, NE])
        picked = sb("picked", [P, NU, NE])
        slot_f = sb("slot_f", [P, 2, NU])
        past = sb("past", [1, NT, NE - 1])
        expert_f = sb("expert_f", [1, NT])
        tile_i = sb("tile_i", [P, 2, NU], I32)
        tile_f = sb("tile_f", [P, 2, NU])
        row_f = sb("row_f", [P, 2, NU])
        row_hot = sb("row_hot", [P, 4, P])
        tile_hot = sb("tile_hot", [P, 4, NT])
        token_ps = ctx.enter_context(nc.psum_tensor("p_token_ps", [P, 512], F32))
        before_ps = ctx.enter_context(nc.psum_tensor("p_before_ps", [P, 512], F32))
        total_ps = ctx.enter_context(nc.psum_tensor("p_total_ps", [P, 512], F32))

        loaded = sem("loaded")
        chain = sem("chain")
        chosen_ready = sem("chosen_ready")
        delta_ready = sem("delta_ready")
        ratio_ready = sem("ratio_ready")
        counted = sem("counted")
        hot_ready = sem("hot_ready")
        placed = sem("placed")
        block = ctx.enter_context(nc.Block())

        @block.sync
        def _(sp):
            for dst, name in ((upper, "c_upper"), (ones, "c_ones"), (rank, "c_rank"), (tile_no, "c_tile_no"),
                              (row_no, "c_row_no"), (token_no, "c_token_no")):
                sp.dma_start(dst[:], d[name]).then_inc(loaded, 16)

        @block.tensor
        def _(pe):
            pe.wait_ge(loaded, 96)
            pe.wait_ge(chosen_ready, 1)
            nc.tensor.matmul(before_ps[:, 0:N], upper[:], chosen[:], start=True, stop=True).then_inc(counted, 1)
            nc.tensor.matmul(total_ps[:, 0:N], ones[:], chosen[:], start=True, stop=True).then_inc(counted, 1)

            def place(n_, q, start=False, stop=False):
                pe.wait_ge(hot_ready, n_ + 1)
                nc.tensor.matmul(token_ps[:, 0:NT], row_hot[:, q], tile_hot[:, q], start=start, stop=stop,
                                 skip_group_check=True).then_inc(placed, 1)

            for q in range(4):
                place(q, q, start=q == 0)
            with pe.Fori(1, 2 * NU // 4 - 1) as i:
                for q in range(4):
                    place(i * 4 + q, q)
            for q in range(4):
                place(2 * NU - 4 + q, q, stop=q == 3)

        @block.scalar
        def _(act):
            act.wait_ge(delta_ready, 1)
            nc.scalar.activation(ratio[:], delta[:], ACT.Exp).then_inc(ratio_ready, 1)

        @block.vector
        def _(dve):
            steps = [0]

            def chained(ins):
                steps[0] += 1
                ins.then_inc(chain, 1)
                dve.wait_ge(chain, steps[0])

            tt, ts = nc.vector.tensor_tensor, nc.vector.tensor_scalar
            by_unit = lambda ap: ap.unsqueeze(2).broadcast_to([P, NU, NE])
            dve.wait_ge(loaded, 96)
            for i, logits in enumerate((LG, rest)):
                chained(nc.vector.tensor_reduce(best[:, i], logits[:], AX.X, ALU.max))
                chained(tt(eq[:], logits[:], by_unit(best[:, i]), ALU.is_equal))
                chained(tt(eq[:], eq[:], rank[:].unsqueeze(1).broadcast_to([P, NU, NE]), ALU.mult))
                chained(nc.vector.tensor_reduce(who[:, i], eq[:], AX.X, ALU.max))
                chained(tt(hot[:, i], rank[:].unsqueeze(1).broadcast_to([P, NU, NE]), by_unit(who[:, i]), ALU.is_equal))
                if i == 0:
                    chained(nc.vector.scalar_tensor_tensor(out=rest[:], in0=hot[:, 0], scalar=NEG, in1=LG[:],
                                                           op0=ALU.mult, op1=ALU.add))
            tt(delta[:], best[:, 1], best[:, 0], ALU.subtract).then_inc(delta_ready, 1)
            tt(chosen[:].rearrange("p (u e) -> p u e", e=NE), hot[:, 0], hot[:, 1], ALU.add).then_inc(chosen_ready, 1)
            dve.wait_ge(ratio_ready, 1)
            chained(ts(gates[:, 0], ratio[:], 1.0, None, ALU.add))
            chained(nc.vector.reciprocal(gates[:, 0], gates[:, 0]))
            chained(tt(gates[:, 1], ratio[:], gates[:, 0], ALU.mult))
            dve.wait_ge(counted, 2)
            chained(nc.vector.tensor_copy(run[:, 0], total_ps[:, 0:N]))
            src = 0
            reach = 1
            while reach < NU:
                w = reach * NE
                nc.vector.tensor_copy(run[:, 1 - src, 0:w], run[:, src, 0:w])
                chained(tt(run[:, 1 - src, w:N], run[:, src, w:N], run[:, src, 0:N - w], ALU.add))
                src, reach = 1 - src, reach * 2
            nc.vector.tensor_copy(count[:], run[:, src, N - NE:N])
            chained(tt(place[:], before_ps[:, 0:N], run[:, src], ALU.add))
            chained(tt(place[:], total_ps[:, 0:N], place[:], ALU.subtract))
            chained(ts(place[:], place[:], -1.0, None, ALU.mult))
            chained(ts(count[:], count[:], float(P - 1), None, ALU.add))
            chained(nc.vector.tensor_copy(tiles_i[:], count[:]))
            chained(ts(tiles_i[:], tiles_i[:], 7, None, ALU.arith_shift_right))
            chained(nc.vector.tensor_copy(base[:, 0], tiles_i[:]))
            chained(nc.vector.tensor_copy(count[:], base[:, 0]))
            b = 0
            for reach in (1, 2, 4):
                nc.vector.tensor_copy(base[:, 1 - b, 0:reach], base[:, b, 0:reach])
                chained(tt(base[:, 1 - b, reach:NE], base[:, b, reach:NE], base[:, b, 0:NE - reach], ALU.add))
                b = 1 - b
            chained(tt(base[:, b], base[:, b], count[:], ALU.subtract))
            chained(tt(past[:], tile_no[0:1].unsqueeze(2).broadcast_to([1, NT, NE - 1]),
                       base[0:1, b, 1:NE].unsqueeze(1).broadcast_to([1, NT, NE - 1]), ALU.is_ge))
            chained(nc.vector.tensor_reduce(expert_f[:], past[:], AX.X, ALU.add))
            nc.vector.tensor_copy(experts[:], expert_f[:])
            chained(ts(base[:, 1 - b], base[:, b], float(P), None, ALU.mult))
            chained(tt(place[:].rearrange("p (u e) -> p u e", e=NE), place[:].rearrange("p (u e) -> p u e", e=NE),
                       base[:, 1 - b].unsqueeze(1).broadcast_to([P, NU, NE]), ALU.add))
            for i in range(2):
                chained(tt(picked[:], hot[:, i], place[:].rearrange("p (u e) -> p u e", e=NE), ALU.mult))
                chained(nc.vector.tensor_reduce(slot_f[:, i], picked[:], AX.X, ALU.add))
            chained(nc.vector.tensor_copy(slots[:], slot_f[:]))
            chained(ts(tile_i[:], slots[:], 7, None, ALU.arith_shift_right))
            chained(nc.vector.tensor_copy(tile_f[:], tile_i[:]))
            chained(ts(row_f[:], tile_f[:], -float(P), None, ALU.mult))
            chained(tt(row_f[:], row_f[:], slot_f[:], ALU.add))

            def hot_ones(i, u, q, wait_for):
                if wait_for is not None:
                    dve.wait_ge(placed, wait_for)
                ts(row_hot[:, q], row_no[:], row_f[:, i, bass.ds(u, 1)], None, ALU.is_equal)
                ts(tile_hot[:, q], tile_no[:], tile_f[:, i, bass.ds(u, 1)], token_no[:, 0, bass.ds(u, 1)],
                   ALU.is_equal, ALU.mult).then_inc(hot_ready, 1)

            for q in range(4):
                hot_ones(0, q, q, None)
            with dve.Fori(1, NU // 4) as i:
                for q in range(4):
                    hot_ones(0, i * 4 + q, q, i * 4 + q - 3)
            with dve.Fori(0, NU // 4) as i:
                for q in range(4):
                    hot_ones(1, i * 4 + q, q, i * 4 + q + (NU - 3))
            dve.wait_ge(placed, 2 * NU)
            nc.vector.tensor_copy(tokens[:], token_ps[:, 0:NT])


def expert_phase(nc, k, experts, tokens, gate_w, up_w, down_w, w_loaded, NT):
    F = 512
    FC = F // P
    Q = 8
    with ExitStack() as ctx:
        def sb(name, shape, dt=F32):
            return ctx.enter_context(nc.sbuf_tensor(f"e_{name}", shape, dt))

        def ps(name):
            return ctx.enter_context(nc.psum_tensor(f"e_{name}_ps", [P, 512], F32))

        def sem(name):
            return nc.alloc_semaphore(f"e_{name}")

        where = sb("where", [P, Q, 1], I32)
        x = sb("x", [P, Q, C])
        xT = sb("xT", [P, 2, P])
        silu = sb("silu", [P, 2, F])
        h = sb("h", [P, 2, F])
        hT = sb("hT", [P, 2, F])
        y = sb("y", [P, 2, C])
        xT_ps = ps("xT")
        G_ps = [ps(f"G{i}") for i in range(2)]
        U_ps = [ps(f"U{i}") for i in range(2)]
        hT_ps = [ps(f"hT{i}") for i in range(2)]
        Y_ps = ps("Y")

        where_ready = sem("where_ready")
        x_in = [sem(f"x_in{i}") for i in range(Q)]
        xT_done = sem("xT_done")
        xT_ready = sem("xT_ready")
        gate_done = sem("gate_done")
        up_done = sem("up_done")
        silu_ready = sem("silu_ready")
        h_ready = sem("h_ready")
        hT_done = sem("hT_done")
        hT_ready = sem("hT_ready")
        y_done = sem("y_done")
        y_ready = sem("y_ready")
        stored = [sem("stored0"), sem("stored1")]
        passed = sem("passed")
        block = ctx.enter_context(nc.Block())

        def later(t, least):
            return not isinstance(t, int) or t >= least

        def tiles(eng, body):
            for j in range(Q):
                body(j, j, NT)
            with eng.Fori(1, NT // Q - 1) as i:
                for j in range(Q):
                    body(i * Q + j, j, NT)
            for j in range(Q):
                body(NT - Q + j, j, Q - j)

        @block.sync
        def _(sp):
            def body(t, j, left):
                p = j % 2
                wait_here(sp, y_ready, t + 1, passed)
                sp.dma_start(k.slot_out[bass.ds(t * P, P), :], y[:, p, :]).then_inc(stored[p], 16)

            tiles(sp, body)
            for q in stored:
                sp.wait_ge(q, NT // 2 * 16)

        @block.scalar
        def _(act):
            def body(t, j, left):
                p = j % 2
                act.wait_ge(gate_done, t + 1)
                if later(t, 2):
                    act.wait_ge(h_ready, t - 1)
                nc.scalar.activation(silu[:, p, :], G_ps[p][:], ACT.Silu).then_inc(silu_ready, 1)
                if later(t, 1):
                    hidden_turned(t - 1, 1 - p)

            def hidden_turned(t, p):
                act.wait_ge(hT_done, t + 1)
                if later(t, 2):
                    act.wait_ge(y_done, t - 1)
                nc.scalar.activation(hT[:, p, :], hT_ps[p][:], ACT.Copy).then_inc(hT_ready, 1)

            tiles(act, body)
            hidden_turned(NT - 1, 1)

        @block.tensor
        def _(pe):
            def turn_x(t, j):
                pe.wait_ge(x_in[j], (t // Q + 1) * 16)
                if later(t, 1):
                    pe.wait_ge(xT_ready, t)
                nc.tensor.transpose(xT_ps[:, 0:P], x[:, j, :], k.ident[:]).then_inc(xT_done, 1)

            def expert_of(t):
                return nc.tensor.value_load(experts[0:1, bass.ds(t, 1)], min_val=0, max_val=7)

            def gate_up(t, j, e):
                p = j % 2
                pe.wait_ge(xT_ready, t + 1)
                if later(t, 2):
                    pe.wait_ge(h_ready, t - 1)
                nc.tensor.matmul(G_ps[p][:], xT[:, p, :], gate_w[:, bass.ds(e * F, F)], start=True, stop=True)\
                    .then_inc(gate_done, 1)
                nc.tensor.matmul(U_ps[p][:], xT[:, p, :], up_w[:, bass.ds(e * F, F)], start=True, stop=True)\
                    .then_inc(up_done, 1)

            def turn_h(t, j):
                p = j % 2
                pe.wait_ge(h_ready, t + 1)
                if later(t, 2):
                    pe.wait_ge(hT_ready, t - 1)
                for c in range(FC):
                    mm = nc.tensor.transpose(hT_ps[p][:, c * P:(c + 1) * P], h[:, p, c * P:(c + 1) * P], k.ident[:])
                mm.then_inc(hT_done, 1)

            def down(t, j, e):
                p = j % 2
                pe.wait_ge(hT_ready, t + 1)
                if later(t, 1):
                    pe.wait_ge(y_ready, t)
                for c in range(FC):
                    mm = nc.tensor.matmul(Y_ps[:, 0:C], hT[:, p, c * P:(c + 1) * P], down_w[:, bass.ds(e * F + c * C, C)],
                                          start=(c == 0), stop=(c == FC - 1))
                mm.then_inc(y_done, 1)

            pe.wait_ge(w_loaded, 48)
            turn_x(0, 0)
            turn_x(1, 1)
            gate_up(0, 0, expert_of(0))
            e_next = [None]

            def body(t, j, left):
                if left > 2:
                    turn_x(t + 2, (j + 2) % Q)
                if left > 1:
                    gate_up(t + 1, (j + 1) % Q, e_next[0] if j > 0 else expert_of(t + 1))
                if later(t, 1):
                    e_down = expert_of(t - 1)
                if j < Q - 1 and left > 2:
                    e_next[0] = expert_of(t + 2)
                turn_h(t, j)
                if later(t, 1):
                    down(t - 1, (j - 1) % Q, e_down)

            tiles(pe, body)
            down(NT - 1, Q - 1, expert_of(NT - 1))

        @block.vector
        def _(dve):
            def x_turned(t, p):
                dve.wait_ge(xT_done, t + 1)
                if later(t, 2):
                    dve.wait_ge(up_done, t - 1)
                nc.vector.tensor_copy(xT[:, p, :], xT_ps[:, 0:P]).then_inc(xT_ready, 1)

            def output(t, p):
                dve.wait_ge(y_done, t + 1)
                if later(t, 2):
                    dve.wait_ge(stored[p], (t // 2) * 16)
                nc.vector.tensor_copy(y[:, p, :], Y_ps[:, 0:C]).then_inc(y_ready, 1)

            for j in range(Q):
                nc.vector.tensor_copy(where[:, j, :], tokens[:, j:j + 1]).then_inc(where_ready, 1)
            x_turned(0, 0)
            x_turned(1, 1)

            def body(t, j, left):
                p = j % 2
                if left > Q:
                    nc.vector.tensor_copy(where[:, j, :], tokens[:, bass.ds(t + Q, 1)]).then_inc(where_ready, 1)
                if left > 2:
                    x_turned(t + 2, p)
                dve.wait_ge(silu_ready, t + 1)
                dve.wait_ge(up_done, t + 1)
                if later(t, 2):
                    dve.wait_ge(hT_done, t - 1)
                nc.vector.tensor_tensor(h[:, p, :], U_ps[p][:], silu[:, p, :], ALU.mult).then_inc(h_ready, 1)
                if later(t, 1):
                    output(t - 1, 1 - p)

            tiles(dve, body)
            output(NT - 1, 1)

        @block.gpsimd
        def _(pool):
            def body(t, j, left):
                wait_here(pool, where_ready, t + 1, passed)
                nc.gpsimd.indirect_dma_start(
                    out=x[:, j, :], out_offset=None, in_=k.xn_rows,
                    in_offset=bass.IndirectOffsetOnAxis(ap=where[:, j, :], axis=0)).then_inc(x_in[j], 16)

            tiles(pool, body)


def wide_attention_phase(nc, k):
    UB = 2
    NB = NU // UB
    BB = 2 * UB
    TOK = UB * P
    D1 = 64
    G = H // 4
    SCALE = float(D1) ** -0.5
    n = "a1"
    d = k.d
    with ExitStack() as ctx:
        def sb(name, shape, dt=F32):
            return ctx.enter_context(nc.sbuf_tensor(f"{n}_{name}", shape, dt))

        def ps(name, shape):
            return ctx.enter_context(nc.psum_tensor(f"{n}_{name}_ps", shape, F32))

        def sem(name):
            return nc.alloc_semaphore(f"{n}_{name}")

        where = sb("where", [P, 2, 2, UB], I32)
        expert_rows = sb("expert_rows", [P, 2, 2, UB, C])
        wq = sb("wq", [P, G, 2, P])
        wk = sb("wk", [P, G, 2, P])
        wv = sb("wv", [P, G, 4 * D1])
        wo = sb("wo", [P, G, 2, C])
        bo = sb("bo", [1, C])
        cos = sb("cos", [P, T])
        sin = sb("sin", [P, T])
        parity = sb("parity", [P, 2])
        stats = sb("stats", [P, UB, 6])
        mv = sb("mv", [P, UB, 2])
        var_eps = sb("var_eps", [P, UB])
        minus_half = sb("minus_half", [P, UB])
        rstd = sb("rstd", [P, UB])
        xn = sb("xn", [P, UB, C])
        xnT = sb("xnT", [P, 2, TOK])
        PQ = sb("PQ", [P, 2, 2, TOK])
        PK = sb("PK", [P, 2, 2, TOK])
        RQ = sb("RQ", [P, 2, TOK])
        RK = sb("RK", [P, 2, TOK])
        QD = sb("QD", [P, 2, 2, BB, P])
        KT = sb("KT", [P, 2, 2, TOK])
        V = sb("V", [P, 2, BB, 2, P])
        row_max = sb("row_max", [P, 2, BB])
        row_sum = sb("row_sum", [P, 2 * BB])
        rsum = sb("rsum", [P, 2, 2 * BB])
        E = sb("E", [P, 2, 512])
        ET = sb("ET", [P, 2, 512])
        OT = sb("OT", [P, 2, 2, TOK])
        Q_ps = ps("Q", [P, 512])
        K_ps = ps("K", [P, 512])
        V_ps = ps("V", [P, 512])
        S_ps = ps("S", [P, 512])
        ET_ps = ps("ET", [P, 512])
        PV_ps = ps("PV", [P, 2, 512])
        Y_ps = ps("Y", [P, 512])

        weights = sem("weights")
        setup = sem("setup")
        where_ready = sem("where_ready")
        got = [sem("got0"), sem("got1")]
        combined = sem("combined")
        stats_done = sem("stats_done")
        var_ready = sem("var_ready")
        rstd_ready = sem("rstd_ready")
        xn_ready = sem("xn_ready")
        xnT_ps = sem("xnT_ps")
        xnT_ready = sem("xnT_ready")
        q_ps = sem("q_ps")
        k_ps = sem("k_ps")
        v_ps = sem("v_ps")
        pq_ready = sem("pq_ready")
        pk_ready = sem("pk_ready")
        rq_ready = sem("rq_ready")
        rk_ready = sem("rk_ready")
        kt_ready = sem("kt_ready")
        qd_ready = sem("qd_ready")
        v_ready = sem("v_ready")
        s_ps = sem("s_ps")
        max_done = sem("max_done")
        d_ready = sem("d_ready")
        e_ready = sem("e_ready")
        sum_done = sem("sum_done")
        rsum_ready = sem("rsum_ready")
        en_ready = sem("en_ready")
        et_ps = sem("et_ps")
        et_ready = sem("et_ready")
        pv_ps = sem("pv_ps")
        ot_ready = sem("ot_ready")
        y_ps = sem("y_ps")
        x_done = sem("x_done")
        passed = sem("passed")
        N_WEIGHTS = 8

        block = ctx.enter_context(nc.Block())

        def item_at(blk, g):
            return blk + g // G, g % G

        def later(blk, least):
            return not isinstance(blk, int) or blk >= least

        @block.sync
        def _(sp):
            for dst, name in [(wq, "L1_attn_wq"), (wk, "L1_attn_wk"), (wv, "L1_attn_wv"), (wo, "L1_attn_wo"),
                              (bo, "L1_attn_bo"), (cos, "c_cos"), (sin, "c_sin"), (parity, "c_parity")]:
                sp.dma_start(dst[:], d[name]).then_inc(weights, 16)

        @block.gpsimd
        def _(pool):
            def power(nb):
                pool.wait_ge(var_ready, nb + 1)
                nc.gpsimd.tensor_tensor(rstd[:], var_eps[:], minus_half[:], ALU.pow).then_inc(rstd_ready, 1)

            def rotate(dst, src):
                nc.gpsimd.tensor_tensor(dst[:, 0, :], src[:, 0, 0, :], src[:, 1, 1, :], ALU.subtract)
                return nc.gpsimd.tensor_tensor(dst[:, 1, :], src[:, 1, 0, :], src[:, 0, 1, :], ALU.add)

            def rotate_k(blk, g):
                n_ = blk * G + g
                pool.wait_ge(pk_ready, n_ + 1)
                if later(n_, 1):
                    pool.wait_ge(kt_ready, n_)
                rotate(RK, PK).then_inc(rk_ready, 1)

            def rotate_q(blk, g):
                n_ = blk * G + g
                pool.wait_ge(pq_ready, n_ + 1)
                if later(n_, 1):
                    pool.wait_ge(qd_ready, n_)
                rotate(RQ, PQ).then_inc(rq_ready, 1)

            def normalise_e(blk, g):
                n_ = blk * G + g
                pool.wait_ge(rsum_ready, n_ + 1)
                e = E[:, g % 2, :].rearrange("p (r t) -> p r t", t=T)
                nc.gpsimd.tensor_tensor(e, e, rsum[:, g % 2, :].unsqueeze(2).broadcast_to([P, 2 * BB, T]), ALU.mult)\
                    .then_inc(en_ready, 1)

            def gather(nb, u, p):
                if u == 0 and later(nb, 2):
                    pool.wait_ge(combined, (nb - 1) * 2)
                wait_here(pool, where_ready, nb + 1, passed)
                for i in range(2):
                    nc.gpsimd.indirect_dma_start(
                        out=expert_rows[:, p, i, u, :], out_offset=None, in_=k.slot_out,
                        in_offset=bass.IndirectOffsetOnAxis(ap=where[:, p, i, u:u + 1], axis=0)).then_inc(got[p], 16)

            def prologue():
                nc.gpsimd.memset(minus_half[:], -0.5).then_inc(setup, 1)
                for u in range(UB):
                    gather(0, u, 0)
                nc.gpsimd.memset(V[:], 0.0).then_inc(setup, 1)
                pool.wait_ge(setup, 2)
                power(0)
                for u in range(UB):
                    gather(1, u, 1)
                for g in range(3):
                    rotate_q(0, g)
                    rotate_k(0, g)
                    if g == 1:
                        normalise_e(0, 0)

            def step(blk, p, prev, nxt):
                for g in range(G):
                    if nxt and g == 0:
                        power(blk + 1)
                    if g + 1 < G or nxt:
                        normalise_e(*item_at(blk, g + 1))
                    if g + 3 < G or nxt:
                        rotate_q(*item_at(blk, g + 3))
                        rotate_k(*item_at(blk, g + 3))
                    if nxt == 2 and g in (1, 2):
                        gather(blk + 2, g - 1, p)

            run_blocks_far(pool, NB, prologue, step, lambda: None)

        @block.tensor
        def _(pe):
            def transpose_x(nb, p):
                pe.wait_ge(xn_ready, nb + 1)
                if later(nb, 1):
                    pe.wait_ge(pq_ready, nb * G)
                for u in range(UB):
                    mm = nc.tensor.transpose(Q_ps[:, u * P:(u + 1) * P], xn[:, u, :], k.ident[:])
                mm.then_inc(xnT_ps, 1)

            def project_qk(blk, g, p):
                n_ = blk * G + g
                pe.wait_ge(xnT_ready, blk + 1)
                if later(n_, 1):
                    pe.wait_ge(pq_ready, n_)
                for a in range(2):
                    mm = nc.tensor.matmul(Q_ps[:, a * TOK:(a + 1) * TOK], wq[:, g, a, :], xnT[:, p, :], start=True, stop=True)
                mm.then_inc(q_ps, 1)
                if later(n_, 1):
                    pe.wait_ge(pk_ready, n_)
                for a in range(2):
                    mm = nc.tensor.matmul(K_ps[:, a * TOK:(a + 1) * TOK], wk[:, g, a, :], xnT[:, p, :], start=True, stop=True)
                mm.then_inc(k_ps, 1)

            def project_v(blk, g, p):
                n_ = blk * G + g
                if later(n_, 1):
                    pe.wait_ge(v_ready, n_)
                for u in range(UB):
                    mm = nc.tensor.matmul(V_ps[:, u * 256:(u + 1) * 256], xnT[:, p, u * P:(u + 1) * P], wv[:, g, :],
                                          start=True, stop=True)
                mm.then_inc(v_ps, 1)

            def scores(blk, g):
                n_ = blk * G + g
                pe.wait_ge(qd_ready, n_ + 1)
                pe.wait_ge(kt_ready, n_ + 1)
                if later(n_, 1):
                    pe.wait_ge(d_ready, n_)
                nc.tensor.matmul(S_ps[:], k.causal_queries[0:T, :], k.causal_keys[0:T, :], start=True, stop=False)
                for j in range(2):
                    for b in range(BB):
                        at = (j * BB + b) * T
                        mm = nc.tensor.matmul(S_ps[:, at:at + T], QD[:, g % 2, j, b, :], KT[:, g % 2, j, b * T:(b + 1) * T],
                                              start=False, stop=(j == 1 and b == BB - 1))
                mm.then_inc(s_ps, 1)

            def transpose_e(blk, g):
                n_ = blk * G + g
                pe.wait_ge(en_ready, n_ + 1)
                if later(n_, 1):
                    pe.wait_ge(et_ready, n_)
                for b in range(BB):
                    mm = nc.tensor.transpose(ET_ps[:, b * P:(b + 1) * P], E[:, g % 2, b * P:(b + 1) * P], k.ident[:])
                mm.then_inc(et_ps, 1)

            def weigh_values(blk, g):
                n_ = blk * G + g
                pe.wait_ge(et_ready, n_ + 1)
                pe.wait_ge(v_ready, n_ + 1)
                if later(n_, 1):
                    pe.wait_ge(ot_ready, n_)
                for h in range(2):
                    for b in range(BB):
                        mm = nc.tensor.matmul(PV_ps[:, h, b * P:(b + 1) * P], V[:, g % 2, b, h, :],
                                              ET[:, g % 2, b * P:(b + 1) * P], start=True, stop=True)
                mm.then_inc(pv_ps, 1)

            def project_o(blk, g):
                n_ = blk * G + g
                pe.wait_ge(ot_ready, n_ + 1)
                if g == 0 and later(blk, 1):
                    pe.wait_ge(x_done, blk)
                for u in range(UB):
                    out = Y_ps[:, u * P:(u + 1) * P]
                    for h in range(2):
                        mm = nc.tensor.matmul(out, OT[:, g % 2, h, u * P:(u + 1) * P], wo[:, g, h, :],
                                              start=(g == 0 and u == 0 and h == 0), stop=False, skip_group_check=True)
                    if g == G - 1:
                        mm = nc.tensor.matmul(out, k.ones_row[0:1, 0:P], bo[:], start=False, stop=(u == UB - 1),
                                              skip_group_check=True)
                mm.then_inc(y_ps, 1)

            def prologue():
                pe.wait_ge(weights, 16 * N_WEIGHTS)
                transpose_x(0, 0)
                for g in range(3):
                    project_qk(0, g, 0)
                    if g >= 1:
                        scores(0, g - 1)
                        project_v(0, g - 1, 0)
                transpose_e(0, 0)

            def step(blk, p, prev, nxt):
                for g in range(G):
                    if g + 3 < G or nxt:
                        nb, gg = item_at(blk, g + 3)
                        project_qk(nb, gg, p if g + 3 < G else 1 - p)
                    if g + 2 < G or nxt:
                        scores(*item_at(blk, g + 2))
                    if g + 1 < G or nxt:
                        transpose_e(*item_at(blk, g + 1))
                    if nxt and g == 0:
                        transpose_x(blk + 1, 1 - p)
                    if g + 2 < G or nxt:
                        nb, gg = item_at(blk, g + 2)
                        project_v(nb, gg, p if g + 2 < G else 1 - p)
                    weigh_values(blk, g)
                    if g > 0:
                        project_o(blk, g - 1)
                    elif prev:
                        project_o(blk - 1, G - 1)

            run_blocks_far(pe, NB, prologue, step, lambda: project_o(NB - 1, G - 1))

        @block.scalar
        def _(act):
            def evacuate_xT(nb, p):
                act.wait_ge(xnT_ps, nb + 1)
                if later(nb, 2):
                    act.wait_ge(v_ps, (nb - 1) * G)
                nc.scalar.activation(xnT[:, p, :], Q_ps[:, 0:TOK], ACT.Copy).then_inc(xnT_ready, 1)

            def spread_q(blk, g):
                n_ = blk * G + g
                act.wait_ge(rq_ready, n_ + 1)
                if later(n_, 2):
                    act.wait_ge(s_ps, n_ - 1)
                for j in range(2):
                    rows = slice(64 * j, 64 * j + 64)
                    for a in range(2):
                        for h in range(2):
                            last = nc.scalar.activation(QD[64 * a:64 * a + 64, g % 2, j, :, h * T:(h + 1) * T],
                                                        RQ[rows, a, :].rearrange("p (b t) -> p b t", t=T), ACT.Copy,
                                                        scale=parity[rows, h:h + 1])
                last.then_inc(qd_ready, 1)

            def evacuate_v(blk, g):
                n_ = blk * G + g
                act.wait_ge(v_ps, n_ + 1)
                if later(n_, 2):
                    act.wait_ge(pv_ps, n_ - 1)
                src = V_ps[:].rearrange("p (u q h e) -> p u q h e", u=UB, q=2, h=2)
                dst = V[:, g % 2].rearrange("p (u r) h (q e) -> p u r h q e", r=2, q=2)
                for r in range(2):
                    for q in range(2):
                        last = nc.scalar.activation(dst[64 * q:64 * q + 64, :, r, :, q, :],
                                                    src[64 * r:64 * r + 64, :, q, :, :], ACT.Copy)
                last.then_inc(v_ready, 1)

            def exponentials(blk, g):
                n_ = blk * G + g
                act.wait_ge(d_ready, n_ + 1)
                nc.scalar.activation(E[:, g % 2, :], E[:, g % 2, :], ACT.Exp, scale=SCALE).then_inc(e_ready, 1)

            def evacuate_e(blk, g):
                n_ = blk * G + g
                act.wait_ge(et_ps, n_ + 1)
                if later(n_, 2):
                    act.wait_ge(pv_ps, n_ - 1)
                nc.scalar.activation(ET[:, g % 2, :], ET_ps[:], ACT.Copy).then_inc(et_ready, 1)

            def evacuate_o(blk, g):
                n_ = blk * G + g
                act.wait_ge(pv_ps, n_ + 1)
                if later(n_, 2):
                    act.wait_ge(y_ps, n_ - 1)
                for h in range(2):
                    last = nc.scalar.activation(OT[:, g % 2, h, :].rearrange("p (b t) -> p b t", t=T),
                                                PV_ps[:, h, :].rearrange("p (b x t) -> p b x t", b=BB, x=2)[:, :, h, :],
                                                ACT.Copy)
                last.then_inc(ot_ready, 1)

            def slots_of(nb, p):
                if later(nb, 2):
                    act.wait_ge(got[p], (nb // 2) * (16 * 2 * UB))
                nc.scalar.activation(where[:, p], k.slots[:, :, bass.ds(nb * UB, UB)], ACT.Copy).then_inc(where_ready, 1)

            def prologue():
                slots_of(0, 0)
                slots_of(1, 1)
                act.wait_ge(weights, 16 * N_WEIGHTS)
                act.wait_ge(setup, 2)
                evacuate_xT(0, 0)
                spread_q(0, 0)
                for g in range(1, 3):
                    exponentials(0, g - 1)
                    evacuate_v(0, g - 1)
                    spread_q(0, g)
                evacuate_e(0, 0)

            def step(blk, p, prev, nxt):
                for g in range(G):
                    if g + 1 < G or nxt:
                        evacuate_e(*item_at(blk, g + 1))
                    if nxt and g == 0:
                        evacuate_xT(blk + 1, 1 - p)
                    if g + 2 < G or nxt:
                        exponentials(*item_at(blk, g + 2))
                    if g + 3 < G or nxt:
                        spread_q(*item_at(blk, g + 3))
                    if g + 2 < G or nxt:
                        evacuate_v(*item_at(blk, g + 2))
                    evacuate_o(blk, g)
                    if nxt == 2 and g == 0:
                        slots_of(blk + 2, p)

            run_blocks_far(act, NB, prologue, step, lambda: None)

        @block.vector
        def _(dve):
            def combine(nb, p):
                dve.wait_ge(got[p], (nb // 2 + 1) * (16 * 2 * UB))
                for i in range(2):
                    for u in range(UB):
                        x = k.X[:, nb * UB + u, :]
                        last = nc.vector.scalar_tensor_tensor(out=x, in0=expert_rows[:, p, i, u, :],
                                                              scalar=k.gates[:, i, bass.ds(nb * UB + u, 1)], in1=x,
                                                              op0=ALU.mult, op1=ALU.add)
                    last.then_inc(combined, 1)
                    wait_here(dve, combined, nb * 2 + i + 1, passed)

            def statistics(nb):
                for u in range(UB):
                    last = nc.vector.bn_stats(stats[:, u, :], k.X[:, nb * UB + u, :])
                last.then_inc(stats_done, 1)
                wait_here(dve, stats_done, nb * 2 + 1, passed)
                for u in range(UB):
                    last = nc.vector.bn_aggr(mv[:, u, :], stats[:, u, :])
                last.then_inc(stats_done, 1)
                dve.wait_ge(stats_done, nb * 2 + 2)
                nc.vector.tensor_scalar(var_eps[:], mv[:, :, 1], EPS, None, ALU.add).then_inc(var_ready, 1)

            def normalise(nb):
                dve.wait_ge(rstd_ready, nb + 1)
                if later(nb, 1):
                    dve.wait_ge(xnT_ps, nb)
                for u in range(UB):
                    last = nc.vector.tensor_scalar(xn[:, u, :], k.X[:, nb * UB + u, :], mv[:, u, 0:1], rstd[:, u:u + 1],
                                                   ALU.subtract, ALU.mult)
                last.then_inc(xn_ready, 1)

            def products(bank, dst):
                src = bank[:].rearrange("p (r t) -> p r t", t=T)
                for i, table in enumerate((cos, sin)):
                    last = nc.vector.tensor_tensor(dst[:, i].rearrange("p a (b t) -> p (a b) t", t=T), src,
                                                   table[:].unsqueeze(1).broadcast_to([P, 2 * BB, T]), ALU.mult)
                return last

            def products_qk(blk, g):
                n_ = blk * G + g
                dve.wait_ge(q_ps, n_ + 1)
                if later(n_, 1):
                    dve.wait_ge(rq_ready, n_)
                products(Q_ps, PQ).then_inc(pq_ready, 1)
                dve.wait_ge(k_ps, n_ + 1)
                if later(n_, 1):
                    dve.wait_ge(rk_ready, n_)
                products(K_ps, PK).then_inc(pk_ready, 1)

            def keys_by_pair(blk, g):
                n_ = blk * G + g
                dve.wait_ge(rk_ready, n_ + 1)
                if later(n_, 2):
                    dve.wait_ge(s_ps, n_ - 1)
                for j in range(2):
                    for a in range(2):
                        last = nc.vector.tensor_copy(KT[64 * a:64 * a + 64, g % 2, j, :], RK[64 * j:64 * j + 64, a, :])
                last.then_inc(kt_ready, 1)

            def subtract_max(blk, g):
                n_ = blk * G + g
                dve.wait_ge(s_ps, n_ + 1)
                src = S_ps[:].rearrange("p (q b t) -> p q b t", q=2, t=T)
                nc.vector.tensor_reduce(row_max[:], src, AX.X, ALU.max).then_inc(max_done, 1)
                dve.wait_ge(max_done, n_ + 1)
                if later(n_, 2):
                    dve.wait_ge(et_ps, n_ - 1)
                dst = E[:, g % 2, :].rearrange("p (b q t) -> p q b t", b=BB, q=2)
                nc.vector.tensor_tensor(dst, src, row_max[:].unsqueeze(3).broadcast_to([P, 2, BB, T]), ALU.subtract)\
                    .then_inc(d_ready, 1)

            def sums(blk, g):
                n_ = blk * G + g
                dve.wait_ge(e_ready, n_ + 1)
                nc.vector.tensor_reduce(row_sum[:], E[:, g % 2, :].rearrange("p (r t) -> p r t", t=T), AX.X, ALU.add)\
                    .then_inc(sum_done, 1)
                dve.wait_ge(sum_done, n_ + 1)
                if later(n_, 2):
                    dve.wait_ge(en_ready, n_ - 1)
                nc.vector.reciprocal(rsum[:, g % 2, :], row_sum[:]).then_inc(rsum_ready, 1)

            def add_residual(blk):
                dve.wait_ge(y_ps, (blk + 1) * G)
                x = k.X[:, bass.ds(blk * UB, UB), :]
                nc.vector.tensor_tensor(x, Y_ps[:, 0:TOK].rearrange("p (u c) -> p u c", u=UB), x, ALU.add)\
                    .then_inc(x_done, 1)

            def prologue():
                dve.wait_ge(weights, 16 * N_WEIGHTS)
                combine(0, 0)
                statistics(0)
                normalise(0)
                products_qk(0, 0)
                keys_by_pair(0, 0)
                for g in range(1, 3):
                    products_qk(0, g)
                    keys_by_pair(0, g)
                    subtract_max(0, g - 1)
                    if g == 1:
                        sums(0, 0)

            def step(blk, p, prev, nxt):
                for g in range(G):
                    if nxt and g == 0:
                        combine(blk + 1, 1 - p)
                        statistics(blk + 1)
                    if g + 1 < G or nxt:
                        sums(*item_at(blk, g + 1))
                    if nxt and g == 0:
                        normalise(blk + 1)
                    if g + 3 < G or nxt:
                        products_qk(*item_at(blk, g + 3))
                    if g + 2 < G or nxt:
                        subtract_max(*item_at(blk, g + 2))
                    if g + 3 < G or nxt:
                        keys_by_pair(*item_at(blk, g + 3))
                    if prev and g == 1:
                        add_residual(blk - 1)

            run_blocks_far(dve, NB, prologue, step, lambda: add_residual(NB - 1))


def masked_attention_phase(nc, k):
    UB = 4
    NB = NU // UB
    BB = 2 * UB
    TOK = UB * P
    n = "x1"
    d = k.d
    with ExitStack() as ctx:
        def sb(name, shape, dt=F32):
            return ctx.enter_context(nc.sbuf_tensor(f"{n}_{name}", shape, dt))

        def ps(name, shape):
            return ctx.enter_context(nc.psum_tensor(f"{n}_{name}_ps", shape, F32))

        def sem(name):
            return nc.alloc_semaphore(f"{n}_{name}")

        ctxT = sb("ctxT", [P, 2, TOK])
        ctxK = sb("ctxK", [T, 2, BB, C])
        mask = sb("mask", [2, NU * T], I32)
        pad = sb("pad", [2, NU * T], BF16)
        stats = sb("stats", [P, NU, 6])
        mv = sb("mv", [P, NU, 2])
        var_eps = sb("var_eps", [P, NU])
        minus_half = sb("minus_half", [P, NU])
        rstd = sb("rstd", [P, NU])
        xn = sb("xn", [P, 2, UB, C])
        xnT = sb("xnT", [P, 2, TOK])
        row_max = sb("row_max", [P, 2, UB])
        row_sum = sb("row_sum", [P, UB])
        rsum = sb("rsum", [P, 2, UB])
        E = sb("E", [P, 2, UB, T])
        ET = sb("ET", [T, TOK])
        xT_ps = ps("xT", [P, 512])
        S_ps = [ps(f"S{i}", [P, 512]) for i in range(2)]
        ET_ps = ps("ET", [P, 512])
        PV_ps = ps("PV", [P, 512])

        loaded = sem("loaded")
        ctx_in = [sem("ctx_in0"), sem("ctx_in1")]
        setup = sem("setup")
        stats_done = sem("stats_done")
        var_ready = sem("var_ready")
        rstd_ready = sem("rstd_ready")
        xn_ready = sem("xn_ready")
        xnT_ps = sem("xnT_ps")
        xnT_ready = sem("xnT_ready")
        s_ps = sem("s_ps")
        pad_ready = sem("pad_ready")
        max_done = sem("max_done")
        sum_done = sem("sum_done")
        d_ready = sem("d_ready")
        e_ready = sem("e_ready")
        en_ready = sem("en_ready")
        et_ps = sem("et_ps")
        et_ready = sem("et_ready")
        pv_ps = sem("pv_ps")
        x_done = sem("x_done")
        passed = sem("passed")

        block = ctx.enter_context(nc.Block())

        def later(blk, least):
            return not isinstance(blk, int) or blk >= least

        @block.sync
        def _(sp):
            sp.dma_start(mask[:], d["mask"]).then_inc(loaded, 16)

            def load_ctx(nb, p):
                if later(nb, 2):
                    wait_here(sp, pv_ps, nb - 1, passed)
                sp.dma_start(ctxT[:, p, :], d["ctxT"][:, bass.ds(nb * TOK, TOK)]).then_inc(ctx_in[p], 16)
                sp.dma_start(ctxK[:, p, :, :], d["ctxK"][:, bass.ds(nb * BB, BB), :]).then_inc(ctx_in[p], 16)

            def step(blk, p, prev, nxt):
                if nxt:
                    load_ctx(blk + 1, 1 - p)

            run_blocks(sp, NB, lambda: load_ctx(0, 0), step, lambda: None)

        @block.gpsimd
        def _(pool):
            nc.gpsimd.memset(minus_half[:], -0.5).then_inc(setup, 1)
            pool.wait_ge(setup, 1)
            pool.wait_ge(var_ready, 1)
            for blk in range(NB):
                b = slice(blk * UB, (blk + 1) * UB)
                nc.gpsimd.tensor_tensor(rstd[:, b], var_eps[:, b], minus_half[:, b], ALU.pow).then_inc(rstd_ready, 1)

        @block.tensor
        def _(pe):
            def transpose_x(nb, p):
                pe.wait_ge(xn_ready, nb + 1)
                if later(nb, 1):
                    pe.wait_ge(xnT_ready, nb)
                for u in range(UB):
                    mm = nc.tensor.transpose(xT_ps[:, u * P:(u + 1) * P], xn[:, p, u, :], k.ident[:])
                mm.then_inc(xnT_ps, 1)

            def scores(nb, p):
                bank = S_ps[p]
                if later(nb, 2):
                    pe.wait_ge(d_ready, nb - 1)
                nc.tensor.matmul(bank[:, 0:UB * T], k.causal_queries[0:T, :], k.causal_keys[0:T, 0:UB * T],
                                 start=True, stop=False)
                nc.tensor.matmul(bank[:, 0:UB * T], k.of_batch[:], pad[:, bass.ds(nb * UB * T, UB * T)],
                                 start=False, stop=False)
                pe.wait_ge(ctx_in[p], (nb // 2 + 1) * 32)
                pe.wait_ge(xnT_ready, nb + 1)
                for b in range(BB):
                    half = slice(64 * (b % 2), 64 * (b % 2) + 64)
                    mm = nc.tensor.matmul(bank[half, (b // 2) * T:(b // 2 + 1) * T], xnT[:, p, b * T:(b + 1) * T],
                                          ctxT[:, p, b * T:(b + 1) * T], start=False, stop=(b >= BB - 2))
                mm.then_inc(s_ps, 1)

            def transpose_e(blk, p):
                if later(blk, 1):
                    pe.wait_ge(et_ready, blk)
                wait_here(pe, en_ready, blk + 1, passed)
                for u in range(UB):
                    mm = nc.tensor.transpose(ET_ps[0:T, u * P:(u + 1) * P], E[:, p, u, :], k.ident[:])
                mm.then_inc(et_ps, 1)

            def weigh_values(blk, p):
                if later(blk, 1):
                    pe.wait_ge(x_done, blk)
                wait_here(pe, et_ready, blk + 1, passed)
                for b in range(BB):
                    half = slice(64 * (b % 2), 64 * (b % 2) + 64)
                    mm = nc.tensor.matmul(PV_ps[half, (b // 2) * C:(b // 2 + 1) * C], ET[:, b * T:(b + 1) * T],
                                          ctxK[:, p, b, :], start=True, stop=True)
                mm.then_inc(pv_ps, 1)

            def prologue():
                transpose_x(0, 0)
                transpose_x(1, 1)
                pe.wait_ge(pad_ready, 1)
                scores(0, 0)

            def step(blk, p, prev, nxt):
                if nxt:
                    scores(blk + 1, 1 - p)
                transpose_e(blk, p)
                weigh_values(blk, p)
                if nxt == 2:
                    transpose_x(blk + 2, p)

            run_blocks_far(pe, NB, prologue, step, lambda: None)

        @block.scalar
        def _(act):
            def evacuate_xT(nb, p):
                act.wait_ge(xnT_ps, nb + 1)
                if later(nb, 2):
                    act.wait_ge(s_ps, nb - 1)
                nc.scalar.activation(xnT[:, p, :], xT_ps[:], ACT.Copy).then_inc(xnT_ready, 1)

            def exponentials(nb, p):
                act.wait_ge(d_ready, nb + 1)
                nc.scalar.activation(E[:, p], E[:, p], ACT.Exp, scale=float(C) ** -0.5).then_inc(e_ready, 1)

            def prologue():
                evacuate_xT(0, 0)
                evacuate_xT(1, 1)
                exponentials(0, 0)

            def step(blk, p, prev, nxt):
                act.wait_ge(et_ps, blk + 1)
                if later(blk, 1):
                    act.wait_ge(pv_ps, blk)
                nc.scalar.activation(ET[:], ET_ps[0:T, :], ACT.Copy).then_inc(et_ready, 1)
                if nxt:
                    exponentials(blk + 1, 1 - p)
                if nxt == 2:
                    evacuate_xT(blk + 2, p)

            run_blocks_far(act, NB, prologue, step, lambda: None)

        @block.vector
        def _(dve):
            def normalise(nb, p):
                dve.wait_ge(rstd_ready, nb + 1)
                if later(nb, 2):
                    dve.wait_ge(xnT_ps, nb - 1)
                for u in range(UB):
                    at = nb * UB + u
                    last = nc.vector.tensor_scalar(xn[:, p, u, :], k.X[:, at, :],
                                                   mv[:, bass.ds(at, 1), 0:1].rearrange("p o c -> p (o c)"),
                                                   rstd[:, bass.ds(at, 1)], ALU.subtract, ALU.mult)
                last.then_inc(xn_ready, 1)

            def subtract_max(nb, p):
                dve.wait_ge(s_ps, nb + 1)
                src = S_ps[p][:, 0:UB * T].rearrange("p (u t) -> p u t", t=T)
                nc.vector.tensor_reduce(row_max[:, p, :], src, AX.X, ALU.max).then_inc(max_done, 1)
                dve.wait_ge(max_done, nb + 1)
                if later(nb, 2):
                    dve.wait_ge(et_ps, nb - 1)
                nc.vector.tensor_tensor(E[:, p], src, row_max[:, p, :].unsqueeze(2).broadcast_to([P, UB, T]), ALU.subtract)\
                    .then_inc(d_ready, 1)

            def normalise_e(blk, p):
                dve.wait_ge(e_ready, blk + 1)
                nc.vector.tensor_reduce(row_sum[:], E[:, p], AX.X, ALU.add).then_inc(sum_done, 1)
                dve.wait_ge(sum_done, blk * 2 + 1)
                nc.vector.reciprocal(rsum[:, p, :], row_sum[:]).then_inc(sum_done, 1)
                dve.wait_ge(sum_done, blk * 2 + 2)
                nc.vector.tensor_tensor(E[:, p], E[:, p], rsum[:, p, :].unsqueeze(2).broadcast_to([P, UB, T]), ALU.mult)\
                    .then_inc(en_ready, 1)

            def add_residual(blk):
                dve.wait_ge(pv_ps, blk + 1)
                x = k.X[:, bass.ds(blk * UB, UB), :]
                nc.vector.tensor_tensor(x, PV_ps[:].rearrange("p (u c) -> p u c", u=UB), x, ALU.add).then_inc(x_done, 1)

            def prologue():
                all_statistics(nc, dve, k, stats, mv, var_eps, stats_done, var_ready)
                dve.wait_ge(loaded, 16)
                nc.vector.tensor_scalar(pad[:], mask[:], 0.0, NEG, ALU.is_equal, ALU.mult).then_inc(pad_ready, 1)
                normalise(0, 0)
                normalise(1, 1)
                subtract_max(0, 0)

            def step(blk, p, prev, nxt):
                normalise_e(blk, p)
                if nxt:
                    subtract_max(blk + 1, 1 - p)
                if nxt == 2:
                    normalise(blk + 2, p)
                add_residual(blk)

            run_blocks_far(dve, NB, prologue, step, lambda: None)


MAGIC = 1.5 * 2.0 ** 23
QMAX = 127.0


def quantised_ffn_phase(nc, k):
    UB = 4
    NB = NU // UB
    TOK = UB * P
    I = k.d["L1_ffn_w_down"].shape[1]
    NC = (I + P - 1) // P
    ROWS = [min(P, I - c * P) for c in range(NC)]
    n = "q1"
    d = k.d
    with ExitStack() as ctx:
        def sb(name, shape, dt=F32):
            return ctx.enter_context(nc.sbuf_tensor(f"{n}_{name}", shape, dt))

        def ps(name, shape, dt=F32):
            return ctx.enter_context(nc.psum_tensor(f"{n}_{name}_ps", shape, dt))

        def sem(name):
            return nc.alloc_semaphore(f"{n}_{name}")

        w_rows = [sb("w_gate", [P, NC, C]), sb("w_up", [P, NC, C])]
        w_down = sb("w_down", [P, I])
        w_q = sb("w_q", [P, 2, NC, C], BF16)
        w_t = sb("w_t", [P, NC * C])
        wd_q = sb("wd_q", [P, I], BF16)
        wT = sb("wT", [P, 2, NC * P], BF16)
        wdT = sb("wdT", [P, NC, C], BF16)
        w_max = sb("w_max", [P, 2 * NC + 1])
        w_scale = sb("w_scale", [P, 2 * NC + 1])
        w_inv = sb("w_inv", [P, 2 * NC + 1])
        clip = sb("clip", [P, 2])
        sig = sb("sig", [P, 2])
        stats = sb("stats", [P, NU, 6])
        mv = sb("mv", [P, NU, 2])
        var_eps = sb("var_eps", [P, NU])
        minus_half = sb("minus_half", [P, NU])
        rstd = sb("rstd", [P, NU])
        XN = sb("XN", [P, NU, C])
        x_max = sb("x_max", [P, NB])
        h_max = sb("h_max", [P, NB * NC])
        all_max = sb("all_max", [P, 4])
        scale = sb("scale", [P, 2])
        inv = sb("inv", [P, 2])
        gu_scale = sb("gu_scale", [P, 2 * NC])
        out_scale = sb("out_scale", [P, 1])
        out_row = sb("out_row", [P, C])
        tq = sb("tq", [P, 2, NC * TOK])
        xq = sb("xq", [P, 2, TOK], BF16)
        xqT = sb("xqT", [P, 2, TOK], BF16)
        act_g = sb("act_g", [P, 2, TOK])
        HT = sb("HT", [P, NC, NB * TOK])
        hq = sb("hq", [P, 2, NC * TOK], BF16)
        y = sb("y", [P, 2, TOK])
        T_ps = ps("T", [P, 1024], BF16)
        G_ps = [ps(f"G{i}", [P, 512]) for i in range(2)]
        U_ps = [ps(f"U{i}", [P, 512]) for i in range(2)]
        D_ps = [ps(f"D{i}", [P, 512]) for i in range(2)]

        loaded = sem("loaded")
        setup = sem("setup")
        stats_done = sem("stats_done")
        var_ready = sem("var_ready")
        rstd_ready = sem("rstd_ready")
        xn_done = sem("xn_done")
        xmax_done = sem("xmax_done")
        wprep = sem("wprep")
        wq_ready = sem("wq_ready")
        wt_ps = sem("wt_ps")
        wt_ready = sem("wt_ready")
        local_max = sem("local_max")
        whole_max = sem("whole_max")
        sig_steps = sem("sig_steps")
        scale_steps = sem("scale_steps")
        gu_ready = sem("gu_ready")
        tq_done = sem("tq_done")
        xq_ready = sem("xq_ready")
        xqT_ps = sem("xqT_ps")
        xqT_ready = sem("xqT_ready")
        g_ps = sem("g_ps")
        u_ps = sem("u_ps")
        silu_ready = sem("silu_ready")
        h_done = sem("h_done")
        hmax_done = sem("hmax_done")
        row_ps = sem("row_ps")
        row_ready = sem("row_ready")
        tq2_done = sem("tq2_done")
        tq2_clipped = sem("tq2_clipped")
        hq_ready = sem("hq_ready")
        d_ps = sem("d_ps")
        y_scaled = sem("y_scaled")
        y_ready = sem("y_ready")
        stored = [sem("stored0"), sem("stored1")]
        passed = sem("passed")
        out_d = k.out.rearrange("(u r) t d -> (r t) u d", r=2)

        block = ctx.enter_context(nc.Block())

        def later(blk, least):
            return not isinstance(blk, int) or blk >= least

        def pairs(eng, body):
            body(0, 0)
            body(1, 1)
            with eng.Fori(1, NB // 2) as i:
                body(i * 2, 0)
                body(i * 2 + 1, 1)

        @block.sync
        def _(sp):
            sp.wait_ge(setup, 3)
            for w, name in zip(w_rows, ("L1_ffn_w_gate", "L1_ffn_w_up")):
                for c in range(NC):
                    sp.dma_start(w[0:ROWS[c], c, :], d[name][c * P:c * P + ROWS[c], :]).then_inc(loaded, 16)
            sp.dma_start(w_down[:], d["L1_ffn_w_down"]).then_inc(loaded, 16)
            sp.dma_start(clip[:], d["L1_ffn_clips"]).then_inc(loaded, 16)

            def store(blk, p):
                wait_here(sp, y_ready, blk + 1, passed)
                sp.dma_start(out_d[:, bass.ds(blk * UB, UB), :], y[:, p, :].rearrange("p (u c) -> p u c", c=C))\
                    .then_inc(stored[p], 16)

            pairs(sp, store)
            for q in stored:
                sp.wait_ge(q, 16 * NB // 2)

        @block.gpsimd
        def _(pool):
            for w in w_rows:
                nc.gpsimd.memset(w[:], 1.0).then_inc(setup, 1)
            nc.gpsimd.memset(h_max[:], 0.0).then_inc(setup, 1)
            nc.gpsimd.memset(minus_half[:], -0.5).then_inc(setup, 1)
            pool.wait_ge(setup, 4)
            nc.gpsimd.memset(HT[ROWS[-1]:P, NC - 1, :], 0.0).then_inc(setup, 1)
            pool.wait_ge(setup, 5)
            pool.wait_ge(var_ready, 1)
            for blk in range(NB):
                b = slice(blk * UB, (blk + 1) * UB)
                nc.gpsimd.tensor_tensor(rstd[:, b], var_eps[:, b], minus_half[:, b], ALU.pow).then_inc(rstd_ready, 1)
            for i in range(2):
                pool.wait_ge(local_max, i + 1)
                nc.gpsimd.partition_all_reduce(all_max[:, 2 * i + 1:2 * i + 2], all_max[:, 2 * i:2 * i + 1], P,
                                               bass.bass_isa.ReduceOp.max).then_inc(whole_max, 1)

        @block.tensor
        def _(pe):
            pe.wait_ge(wq_ready, 1)
            for c in range(2 * NC):
                if c >= 4:
                    pe.wait_ge(wt_ready, 1)
                mm = nc.tensor.transpose(T_ps[:, (c % 4) * P:(c % 4 + 1) * P], w_q[:, c // NC, c % NC, :], k.identb[:])
                if c == 3:
                    mm.then_inc(wt_ps, 1)
            mm.then_inc(wt_ps, 1)
            pe.wait_ge(wt_ready, 2)
            for c in range(NC):
                mm = nc.tensor.transpose(T_ps[0:ROWS[c], c * P:(c + 1) * P], wd_q[:, c * P:c * P + ROWS[c]], k.identb[:])
            mm.then_inc(wt_ps, 1)
            pe.wait_ge(wt_ready, 3)

            def up(blk, p):
                pe.wait_ge(xq_ready, blk + 1)
                if later(blk, 1):
                    pe.wait_ge(xqT_ready, blk)
                for u in range(UB):
                    mm = nc.tensor.transpose(T_ps[:, u * P:(u + 1) * P], xq[:, p, u * P:(u + 1) * P], k.identb[:])
                mm.then_inc(xqT_ps, 1)
                pe.wait_ge(xqT_ready, blk + 1)
                for c in range(NC):
                    n_ = blk * NC + c
                    r = (p * NC + c) % 2
                    if later(n_, 2):
                        pe.wait_ge(h_done, n_ - 1)
                    nc.tensor.matmul(G_ps[r][0:ROWS[c], :], wT[:, 0, c * P:c * P + ROWS[c]], xqT[:, p, :],
                                     start=True, stop=True).then_inc(g_ps, 1)
                    nc.tensor.matmul(U_ps[r][0:ROWS[c], :], wT[:, 1, c * P:c * P + ROWS[c]], xqT[:, p, :],
                                     start=True, stop=True).then_inc(u_ps, 1)

            pairs(pe, up)
            pe.wait_ge(scale_steps, 5)
            nc.tensor.matmul(D_ps[0][:, 0:C], out_scale[:, 0:1].broadcast_to([P, P]), k.ident[:], start=True, stop=True)\
                .then_inc(row_ps, 1)
            pe.wait_ge(row_ready, 1)

            def down(blk, p):
                pe.wait_ge(hq_ready, blk + 1)
                if later(blk, 2):
                    pe.wait_ge(y_scaled, blk - 1)
                for u in range(UB):
                    for c in range(NC):
                        mm = nc.tensor.matmul(D_ps[p][:, u * C:(u + 1) * C],
                                              hq[0:ROWS[c], p, c * TOK + u * P:c * TOK + (u + 1) * P],
                                              wdT[0:ROWS[c], c, :], start=(c == 0), stop=(c == NC - 1))
                mm.then_inc(d_ps, 1)

            pairs(pe, down)

        @block.scalar
        def _(act):
            act.wait_ge(loaded, 16 * (2 * NC + 2))
            nc.scalar.activation(sig[:], clip[:], ACT.Exp, scale=-1.0).then_inc(sig_steps, 1)
            act.wait_ge(wt_ps, 1)
            nc.scalar.activation(wT[:].rearrange("p g n -> p (g n)")[:, 0:4 * P], T_ps[:, 0:4 * P], ACT.Copy).then_inc(wt_ready, 1)
            act.wait_ge(wt_ps, 2)
            nc.scalar.activation(wT[:].rearrange("p g n -> p (g n)")[:, 4 * P:6 * P], T_ps[:, 0:2 * P], ACT.Copy).then_inc(wt_ready, 1)
            act.wait_ge(wt_ps, 3)
            for c in range(NC):
                last = nc.scalar.activation(wdT[0:ROWS[c], c, :], T_ps[0:ROWS[c], c * P:(c + 1) * P], ACT.Copy)
            last.then_inc(wt_ready, 1)
            act.wait_ge(gu_ready, 1)

            def up(blk, p):
                act.wait_ge(tq_done, blk * 2 + 2)
                if later(blk, 2):
                    act.wait_ge(xqT_ps, blk - 1)
                nc.scalar.activation(xq[:, p, :], tq[:, p, 0:TOK], ACT.Copy, bias=-MAGIC).then_inc(xq_ready, 1)
                act.wait_ge(xqT_ps, blk + 1)
                if later(blk, 2):
                    act.wait_ge(u_ps, (blk - 1) * NC)
                nc.scalar.activation(xqT[:, p, :], T_ps[:, 0:TOK], ACT.Copy).then_inc(xqT_ready, 1)
                for c in range(NC):
                    n_ = blk * NC + c
                    r = (p * NC + c) % 2
                    act.wait_ge(g_ps, n_ + 1)
                    if later(n_, 2):
                        act.wait_ge(h_done, n_ - 1)
                    nc.scalar.activation(act_g[0:ROWS[c], r, :], G_ps[r][0:ROWS[c], :], ACT.Silu,
                                         scale=gu_scale[0:ROWS[c], c:c + 1]).then_inc(silu_ready, 1)

            pairs(act, up)

            def down(blk, p):
                act.wait_ge(tq2_clipped, blk + 1)
                if later(blk, 2):
                    act.wait_ge(d_ps, blk - 1)
                nc.scalar.activation(hq[:, p, :], tq[:, p, :], ACT.Copy, bias=-MAGIC).then_inc(hq_ready, 1)

            act.wait_ge(scale_steps, 5)
            pairs(act, down)

        @block.vector
        def _(dve):
            step_no = [0]

            def chained(ins):
                step_no[0] += 1
                ins.then_inc(wprep, 1)
                dve.wait_ge(wprep, step_no[0])

            all_statistics(nc, dve, k, stats, mv, var_eps, stats_done, var_ready)
            dve.wait_ge(loaded, 16 * (2 * NC + 2))
            for g in range(2):
                nc.vector.tensor_reduce(w_max[:, g * NC:(g + 1) * NC], w_rows[g][:], AX.X, ALU.max, apply_absolute_value=True)
            chained(nc.vector.tensor_reduce(w_max[:, 2 * NC:2 * NC + 1], w_down[:], AX.X, ALU.max, apply_absolute_value=True))
            chained(nc.vector.tensor_scalar(w_scale[:], w_max[:], 1.0 / QMAX, None, ALU.mult))
            chained(nc.vector.reciprocal(w_inv[:], w_scale[:]))
            for g in range(2):
                t3 = w_t[:].rearrange("p (c n) -> p c n", n=C)
                chained(nc.vector.tensor_tensor(t3, w_rows[g][:], w_inv[:, g * NC:(g + 1) * NC].unsqueeze(2)
                                                .broadcast_to([P, NC, C]), ALU.mult))
                chained(nc.vector.tensor_scalar(w_t[:], w_t[:], MAGIC, MAGIC - QMAX - 1.0, ALU.add, ALU.max))
                chained(nc.vector.tensor_scalar(w_q[:, g].rearrange("p c n -> p (c n)"), w_t[:], MAGIC + QMAX, MAGIC,
                                                ALU.min, ALU.subtract))
            chained(nc.vector.tensor_scalar(w_t[:, 0:I], w_down[:], w_inv[:, 2 * NC:2 * NC + 1], MAGIC, ALU.mult, ALU.add))
            chained(nc.vector.tensor_scalar(w_t[:, 0:I], w_t[:, 0:I], MAGIC - QMAX - 1.0, MAGIC + QMAX, ALU.max, ALU.min))
            nc.vector.tensor_scalar(wd_q[:], w_t[:, 0:I], MAGIC, None, ALU.subtract).then_inc(wq_ready, 1)
            dve.wait_ge(sig_steps, 1)
            chained(nc.vector.tensor_scalar(sig[:], sig[:], 1.0, None, ALU.add))
            chained(nc.vector.reciprocal(sig[:], sig[:]))

            dve.wait_ge(setup, 5)
            with dve.Fori(0, NB) as nb:
                dve.wait_ge(rstd_ready, nb + 1)
                for u in range(UB):
                    last = nc.vector.tensor_scalar(XN[:, nb * UB + u, :], k.X[:, nb * UB + u, :], mv[:, bass.ds(nb * UB + u, 1), 0:1].rearrange("p o c -> p (o c)"),
                                                   rstd[:, bass.ds(nb * UB + u, 1)], ALU.subtract, ALU.mult)
                last.then_inc(xn_done, 1)
                dve.wait_ge(xn_done, nb + 1)
                nc.vector.tensor_reduce(x_max[:, bass.ds(nb, 1)], XN[:, bass.ds(nb * UB, UB), :].rearrange("p u c -> p (u c)"),
                                        AX.X, ALU.max, apply_absolute_value=True).then_inc(xmax_done, 1)
            dve.wait_ge(xmax_done, NB)

            def find_scale(i, maxima):
                nc.vector.tensor_reduce(all_max[:, 2 * i:2 * i + 1], maxima[:], AX.X, ALU.max).then_inc(local_max, 1)
                dve.wait_ge(whole_max, i + 1)
                nc.vector.tensor_scalar(scale[:, i:i + 1], all_max[:, 2 * i + 1:2 * i + 2], sig[:, i:i + 1], 1.0 / QMAX,
                                        ALU.mult, ALU.mult).then_inc(scale_steps, 1)
                dve.wait_ge(scale_steps, 2 * i + 1)
                nc.vector.reciprocal(inv[:, i:i + 1], scale[:, i:i + 1]).then_inc(scale_steps, 1)
                dve.wait_ge(scale_steps, 2 * i + 2)

            find_scale(0, x_max)
            nc.vector.tensor_scalar(gu_scale[:], w_scale[:, 0:2 * NC], scale[:, 0:1], None, ALU.mult)\
                .then_inc(gu_ready, 1)
            dve.wait_ge(gu_ready, 1)

            def quantise_x(blk, p):
                if later(blk, 2):
                    dve.wait_ge(xq_ready, blk - 1)
                t = tq[:, p, 0:TOK]
                nc.vector.tensor_scalar(t, XN[:, bass.ds(blk * UB, UB), :].rearrange("p u c -> p (u c)"), inv[:, 0:1], MAGIC,
                                        ALU.mult, ALU.add).then_inc(tq_done, 1)
                dve.wait_ge(tq_done, blk * 2 + 1)
                nc.vector.tensor_scalar(t, t, MAGIC - QMAX - 1.0, MAGIC + QMAX, ALU.max, ALU.min).then_inc(tq_done, 1)

            def hidden(blk, p):
                def chunk(c):
                    return HT[0:ROWS[c], c, bass.ds(blk * TOK, TOK)]

                def magnitude(c):
                    n_ = blk * NC + c
                    dve.wait_ge(h_done, n_ + 1)
                    nc.vector.tensor_reduce(h_max[0:ROWS[c], bass.ds(n_, 1)], chunk(c), AX.X, ALU.max,
                                            apply_absolute_value=True).then_inc(hmax_done, 1)

                for c in range(NC):
                    n_ = blk * NC + c
                    r = (p * NC + c) % 2
                    dve.wait_ge(u_ps, n_ + 1)
                    dve.wait_ge(silu_ready, n_ + 1)
                    nc.vector.scalar_tensor_tensor(out=chunk(c), in0=U_ps[r][0:ROWS[c], :],
                                                   scalar=gu_scale[0:ROWS[c], NC + c:NC + c + 1],
                                                   in1=act_g[0:ROWS[c], r, :], op0=ALU.mult, op1=ALU.mult).then_inc(h_done, 1)
                    if c > 0:
                        magnitude(c - 1)
                magnitude(NC - 1)

            def up(blk, p):
                quantise_x(blk + 1, 1 - p)
                hidden(blk, p)

            quantise_x(0, 0)
            up(0, 0)
            up(1, 1)
            with dve.Fori(1, NB // 2 - 1) as i:
                up(i * 2, 0)
                up(i * 2 + 1, 1)
            up(NB - 2, 0)
            hidden(NB - 1, 1)
            dve.wait_ge(hmax_done, NB * NC)
            find_scale(1, h_max)
            nc.vector.tensor_scalar(out_scale[:], w_scale[:, 2 * NC:2 * NC + 1], scale[:, 1:2], None, ALU.mult)\
                .then_inc(scale_steps, 1)
            dve.wait_ge(scale_steps, 5)
            dve.wait_ge(row_ps, 1)
            nc.vector.tensor_copy(out_row[:], D_ps[0][:, 0:C]).then_inc(row_ready, 1)
            dve.wait_ge(row_ready, 1)

            def quantise_h(blk, p):
                t = tq[:, p, :]
                if later(blk, 2):
                    dve.wait_ge(hq_ready, blk - 1)
                for c in range(NC):
                    last = nc.vector.tensor_scalar(tq[:, p, c * TOK:(c + 1) * TOK], HT[:, c, bass.ds(blk * TOK, TOK)],
                                                   inv[:, 1:2], MAGIC, ALU.mult, ALU.add)
                last.then_inc(tq2_done, 1)
                dve.wait_ge(tq2_done, blk + 1)
                nc.vector.tensor_scalar(t, t, MAGIC - QMAX - 1.0, MAGIC + QMAX, ALU.max, ALU.min).then_inc(tq2_clipped, 1)

            def output(blk, p):
                dve.wait_ge(d_ps, blk + 1)
                if later(blk, 2):
                    dve.wait_ge(stored[p], (blk // 2) * 16)
                y3 = y[:, p, :].rearrange("p (u c) -> p u c", c=C)
                nc.vector.tensor_tensor(y3, D_ps[p][:].rearrange("p (u c) -> p u c", c=C),
                                        out_row[:].unsqueeze(1).broadcast_to([P, UB, C]), ALU.mult).then_inc(y_scaled, 1)
                dve.wait_ge(y_scaled, blk + 1)
                nc.vector.tensor_tensor(y3, y3, k.X[:, bass.ds(blk * UB, UB), :], ALU.add).then_inc(y_ready, 1)

            def down(blk, p):
                quantise_h(blk + 1, 1 - p)
                output(blk, p)

            quantise_h(0, 0)
            down(0, 0)
            down(1, 1)
            with dve.Fori(1, NB // 2 - 1) as i:
                down(i * 2, 0)
                down(i * 2 + 1, 1)
            down(NB - 2, 0)
            output(NB - 1, 1)


def decoder_kernel(nc, dram, out):
    k = Core()
    k.d = dram
    k.out = out
    with ExitStack() as ctx:
        def sb(name, shape, dt=F32):
            return ctx.enter_context(nc.sbuf_tensor(name, shape, dt))

        k.X = sb("X", [P, NU, C])
        k.ident = sb("ident", [P, P])
        k.ones_row = sb("ones_row", [1, 512])
        k.causal_queries = sb("causal_queries", [P, P], BF16)
        k.causal_keys = sb("causal_keys", [P, 512], BF16)
        k.identb = sb("identb", [P, P], BF16)
        k.of_batch = sb("of_batch", [2, P], BF16)
        k.gates = sb("gates", [P, 2, NU])
        k.slots = sb("slots", [P, 2, NU], I32)
        k.xn_rows = nc.dram_tensor("xn_rows", (NU * P, C), F32, kind="Internal").ap()
        k.slot_out = nc.dram_tensor("slot_out", ((2 * NU + 8) * P, C), F32, kind="Internal").ap()
        k.loaded = nc.alloc_semaphore("shared_loaded")
        run_phase(nc, load_phase, k)
        run_phase(nc, narrow_attention_phase, k, cross=False)
        run_phase(nc, narrow_attention_phase, k, cross=True)
        mixture_phases(nc, k)
        run_phase(nc, wide_attention_phase, k)
        run_phase(nc, masked_attention_phase, k)
        run_phase(nc, quantised_ffn_phase, k)


def constants():
    t = np.arange(T)
    inv_freq = np.float32(1.0) / np.float32(10000.0) ** (np.arange(0, 64, 2, dtype=np.float32) / np.float32(64))
    angle = inv_freq[:, None] * t.astype(np.float32)[None, :]
    return {
        "c_ident": np.eye(P, dtype=np.float32),
        "c_upper": np.triu(np.ones((P, P), np.float32), 1),
        "c_ones": np.ones((P, P), np.float32),
        "c_rank": np.tile(8.0 - np.arange(8, dtype=np.float32), (P, 1)),
        "c_tile_no": np.tile(np.arange(2 * NU + 8, dtype=np.float32), (P, 1)),
        "c_row_no": np.tile(np.arange(P, dtype=np.float32), (P, 1)),
        "c_token_no": (np.arange(NU)[None, None, :] * P + np.arange(P)[:, None, None]).astype(np.float32),
        "c_of_batch": (np.arange(P)[None, :] // T == np.arange(2)[:, None]).astype(np.float32),
        "c_ones_row": np.ones((1, 512), np.float32),
        "c_causal_queries": np.tile(np.eye(T), (2, 2)).astype(np.float32),
        "c_causal_keys": np.tile(np.where(t[None, :] > t[:, None], NEG, 0.0), (2, 8)).astype(np.float32),
        "c_cos": np.tile(np.cos(angle), (4, 1)).astype(np.float32),
        "c_sin": np.tile(np.sin(angle), (4, 1)).astype(np.float32),
        "c_narrow_parity": (np.arange(P)[:, None] // D0 % 2 == np.arange(2)[None, :]).astype(np.float32),
        "c_of_head": (np.arange(P)[:, None] % 64 // D0 == np.arange(H // 2)[None, :]).astype(np.float32),
        "c_parity": (np.arange(P)[:, None] // 32 % 2 == np.arange(2)[None, :]).astype(np.float32),
    }


def laid_out(inputs):
    a = {name: np.asarray(v) for name, v in inputs.items()}
    f = {"x": a["x"], "ctxT": a["ctx_1024"].reshape(B * T, C).T,
         "ctxK": a["ctx_1024"].transpose(1, 0, 2), "mask": a["mask_BxS2_ik1"].reshape(NU, 2, T).transpose(1, 0, 2).reshape(2, NU * T)}
    for n in ("w_gate", "w_up", "w_down"):
        f[f"L1_ffn_{n}"] = a[f"L1_ffn_{n}"]
    f["L1_ffn_clips"] = np.broadcast_to(np.stack([a["L1_ffn_clip_x"], a["L1_ffn_clip_down"]], 1), (P, 2))
    qkv = a["L0_attn_W_qkv"]
    for i, n in enumerate("qkv"):
        f[f"L0_attn_w{n}T"] = qkv[i * C:(i + 1) * C].T
        f[f"L0_xattn_w{n}T"] = a[f"L0_xattn_W{n}"].T
    f["L0_attn_woT"] = a["L0_attn_W_proj"].T
    f["L0_xattn_woT"] = a["L0_xattn_Wo"].T
    for n in ("bq", "bk"):
        f[f"L0_xattn_{n}"] = a[f"L0_xattn_{n}"].reshape(C, 1)
    for n in ("bv", "bo"):
        f[f"L0_xattn_{n}"] = a[f"L0_xattn_{n}"].reshape(1, C)
    f["L0_xattn_temp"] = np.repeat(a["L0_xattn_temperature"].reshape(H), D0).reshape(C, 1)
    f["L0_ffn_router_w"] = a["L0_ffn_router_w"].T
    f["L0_ffn_router_b"] = np.tile(a["L0_ffn_router_b"].reshape(1, 8), (1, 4))
    for n in ("gate_w", "up_w"):
        f[f"L0_ffn_{n}"] = a[f"L0_ffn_{n}"].transpose(2, 0, 1).reshape(C, -1)
    f["L0_ffn_down_w"] = a["L0_ffn_down_w"].reshape(8, C, 4, P).transpose(3, 0, 2, 1).reshape(P, -1)
    for n in "qk":
        f[f"L1_attn_w{n}"] = a[f"L1_attn_W{n}"].reshape(C, 4, 4, 32, 2).transpose(0, 1, 4, 2, 3).reshape(C, 4, 2, P)
    f["L1_attn_wv"] = a["L1_attn_Wv"].reshape(C, 4, 256)
    f["L1_attn_wo"] = a["L1_attn_Wo"].reshape(4, 2, 2, 64, C).transpose(1, 3, 0, 2, 4).reshape(P, 4, 2, C)
    f["L1_attn_bo"] = a["L1_attn_bo"].reshape(1, C)
    return f


def kernel(**inputs):
    import concourse.bacc as _bacc
    from concourse.bass_utils import run_bass_kernel_spmd as _run

    nc = _bacc.Bacc("TRN2", target_bir_lowering=False, num_devices=1)
    arrays, dram = {}, {}
    for name, a in {**laid_out(inputs), **constants()}.items():
        a = np.ascontiguousarray(a)
        arrays[f"in_{name}"] = a
        dram[name] = nc.dram_tensor(f"in_{name}", a.shape, mybir.dt.from_np(a.dtype), kind="ExternalInput").ap()
    out = nc.dram_tensor("out_x", (B, T, C), F32, kind="ExternalOutput").ap()
    decoder_kernel(nc, dram, out)
    r = _run(nc, [arrays], core_ids=[0])
    return r.results[0]["out_x"]
```
